# Optimizing a Trainium2 kernel written in Bass

```python
import numpy as np
import jax
import jax.numpy as jnp

def _softmax(x, axis=-1):
    return jax.nn.softmax(x, axis=axis)

def _gelu(x):
    return jax.nn.gelu(x, approximate=True)

def _silu(x):
    return jax.nn.silu(x)

def _sigmoid(x):
    return jax.nn.sigmoid(x)

def _layernorm(x, axis=-1, eps=1e-05):
    m = jnp.mean(x, axis=axis, keepdims=True)
    v = jnp.var(x, axis=axis, keepdims=True)
    return (x - m) / jnp.sqrt(v + eps)

def _scatter_add(tgt, idx, src, axis=0):
    return tgt.at[idx].add(src)

def _segment_sum(src, seg, n):
    return jax.ops.segment_sum(src, seg, n)
kernel_name = 'mk_vit_tower_d2_tok_img1024_r4_cd6d66'

def setup_inputs(seed: int=0):
    np.random.seed(seed)
    _w = jnp.asarray

    def _rec_inputs():
        import jax
        import jax.numpy as jnp
        _rk = jax.random.key(seed)
        x = -0.00016672 + 0.999947 * jax.random.normal(jax.random.fold_in(_rk, 1), (64, 3, 224, 224), jnp.float32)
        return x
    x = _rec_inputs()

    def _L0_tok_setup():
        import jax, jax.numpy as jnp
        import numpy as np
        PATCH = 16
        D_MODEL = 256

        def patchify(imgs, p):
            n, c, H, W = imgs.shape
            h, w = (H // p, W // p)
            x = imgs.reshape(n, c, h, p, w, p)
            x = jnp.einsum('nchpwq->nhwpqc', x)
            return x.reshape(n, h * w, p * p * c)
        key = jax.random.key(seed)
        k1, k2, k3 = jax.random.split(key, 3)
        val = jax.random.normal(k1, (64, 3, 96, 96), dtype=jnp.float32)
        in_dim = PATCH * PATCH * 3
        bound = 1.0 / np.sqrt(in_dim)
        W = jax.random.uniform(k2, (D_MODEL, in_dim), dtype=jnp.float32, minval=-bound, maxval=bound)
        b = jax.random.uniform(k3, (D_MODEL,), dtype=jnp.float32, minval=-bound, maxval=bound)
        return {'val': val, 'W': W, 'b': b}
    _L0_tok_all = _L0_tok_setup()
    _L0_tok_in = {k: v for k, v in _L0_tok_all.items() if k in ('W', 'b')}
    del _L0_tok_all

    def _L0_attn_setup():
        import jax, jax.numpy as jnp
        import numpy as np
        import math
        D_MODEL = 256
        N_HEAD = 16
        D_HEAD = D_MODEL // N_HEAD
        D_KMAP = 128
        D_INNER = 1024

        def _layer_norm(x, g, b, eps=1e-05):
            mu = jnp.mean(x, axis=-1, keepdims=True)
            var = jnp.mean(jnp.square(x - mu), axis=-1, keepdims=True)
            return (x - mu) * jax.lax.rsqrt(var + eps) * g + b

        def _fourier_kernel(x, proj_mat):
            p = jnp.einsum('blhd,dm->blhm', x, proj_mat) / math.sqrt(D_HEAD)
            return jnp.concatenate([jnp.cos(p), jnp.sin(p)], axis=-1) / math.sqrt(D_KMAP)
        key = jax.random.key(seed)
        ks = jax.random.split(key, 12)
        s = 0.02
        return {'x': jax.random.normal(ks[0], (4, 1024, D_MODEL), dtype=jnp.float32), 'proj_mat': jax.random.normal(ks[1], (D_HEAD, D_KMAP), dtype=jnp.float32), 'wq': jax.random.normal(ks[2], (D_MODEL, D_MODEL), dtype=jnp.float32) * s, 'bq': jnp.zeros((D_MODEL,), jnp.float32), 'wk': jax.random.normal(ks[3], (D_MODEL, D_MODEL), dtype=jnp.float32) * s, 'bk': jnp.zeros((D_MODEL,), jnp.float32), 'wv': jax.random.normal(ks[4], (D_MODEL, D_MODEL), dtype=jnp.float32) * s, 'bv': jnp.zeros((D_MODEL,), jnp.float32), 'wo': jax.random.normal(ks[5], (D_MODEL, D_MODEL), dtype=jnp.float32) * s, 'bo': jnp.zeros((D_MODEL,), jnp.float32), 'ln1_g': jnp.ones((D_MODEL,), jnp.float32), 'ln1_b': jnp.zeros((D_MODEL,), jnp.float32), 'w1': jax.random.normal(ks[6], (D_MODEL, D_INNER), dtype=jnp.float32) * s, 'b1': jnp.zeros((D_INNER,), jnp.float32), 'w2': jax.random.normal(ks[7], (D_INNER, D_MODEL), dtype=jnp.float32) * s, 'b2': jnp.zeros((D_MODEL,), jnp.float32), 'ln2_g': jnp.ones((D_MODEL,), jnp.float32), 'ln2_b': jnp.zeros((D_MODEL,), jnp.float32)}
    _L0_attn_all = _L0_attn_setup()
    _L0_attn_in = {k: v for k, v in _L0_attn_all.items() if k in ('proj_mat', 'wq', 'bq', 'wk', 'bk', 'wv', 'bv', 'wo', 'bo', 'ln1_g', 'ln1_b', 'w1', 'b1', 'w2', 'b2', 'ln2_g', 'ln2_b')}
    del _L0_attn_all

    def _L0_ffn_setup():
        import jax, jax.numpy as jnp
        import numpy as np
        EPS = 1e-05

        def rmsnorm(x):
            var = jnp.mean(jnp.square(x), axis=-1, keepdims=True)
            return x * jax.lax.rsqrt(var + 1e-06)

        def activation_quant(x):
            scale = 127.0 / jnp.clip(jnp.max(jnp.abs(x), axis=-1, keepdims=True), EPS, None)
            return jnp.clip(jnp.round(x * scale), -128, 127) / scale

        def weight_quant(w):
            scale = 1.0 / jnp.clip(jnp.mean(jnp.abs(w)), EPS, None)
            return jnp.clip(jnp.round(w * scale), -1, 1) / scale

        def bitlinear(x, w, b):
            xn = rmsnorm(x)
            xq = xn + jax.lax.stop_gradient(activation_quant(xn) - xn)
            wq = w + jax.lax.stop_gradient(weight_quant(w) - w)
            return jnp.einsum('bsi,oi->bso', xq, wq) + b
        key = jax.random.key(seed)
        k1, k2, k3 = jax.random.split(key, 3)
        B, S, D, H = (4, 512, 256, 1024)
        x = jax.random.normal(k1, (B, S, D), dtype=jnp.float32)
        w1 = jax.random.normal(k2, (H, D), dtype=jnp.float32) * D ** (-0.5)
        b1 = jnp.zeros((H,), dtype=jnp.float32)
        w2 = jax.random.normal(k3, (D, H), dtype=jnp.float32) * H ** (-0.5)
        b2 = jnp.zeros((D,), dtype=jnp.float32)
        return {'x': x, 'w1': w1, 'b1': b1, 'w2': w2, 'b2': b2}
    _L0_ffn_all = _L0_ffn_setup()
    _L0_ffn_in = {k: v for k, v in _L0_ffn_all.items() if k in ('w1', 'b1', 'w2', 'b2')}
    del _L0_ffn_all

    def _L1_attn_setup():
        import jax, jax.numpy as jnp
        import numpy as np
        EMBED = 256
        key = jax.random.key(seed)
        ks = jax.random.split(key, 7)
        B, S, E = (4, 512, EMBED)
        scale = 1.0 / np.sqrt(E)
        x = jax.random.normal(ks[0], (B, S, E), dtype=jnp.float32)
        Wq = jax.random.uniform(ks[1], (E, E), jnp.float32, -scale, scale)
        bq = jax.random.uniform(ks[2], (E,), jnp.float32, -scale, scale)
        Wk = jax.random.uniform(ks[3], (E, E), jnp.float32, -scale, scale)
        bk = jax.random.uniform(ks[4], (E,), jnp.float32, -scale, scale)
        Wv = jax.random.uniform(ks[5], (E, E), jnp.float32, -scale, scale)
        bv = jax.random.uniform(ks[6], (E,), jnp.float32, -scale, scale)
        return {'x': x, 'Wq': Wq, 'bq': bq, 'Wk': Wk, 'bk': bk, 'Wv': Wv, 'bv': bv}
    _L1_attn_all = _L1_attn_setup()
    _L1_attn_in = {k: v for k, v in _L1_attn_all.items() if k in ('Wq', 'bq', 'Wk', 'bk', 'Wv', 'bv')}
    del _L1_attn_all

    def _L1_ffn_setup():
        import jax, jax.numpy as jnp
        import numpy as np
        EMBED = 256
        NUM_EXPERTS = 8
        TOP_K = 2
        key = jax.random.key(seed)
        ks = jax.random.split(key, 6)
        scale = EMBED ** (-0.5)
        return {'x': jax.random.normal(ks[0], (4, 1024, EMBED), jnp.float32), 'router_w': jax.random.normal(ks[1], (EMBED, NUM_EXPERTS), jnp.float32) * scale, 'router_b': jnp.zeros((NUM_EXPERTS,), jnp.float32), 'we_gate': jax.random.normal(ks[2], (NUM_EXPERTS, EMBED, EMBED), jnp.float32) * scale, 'we_up': jax.random.normal(ks[3], (NUM_EXPERTS, EMBED, EMBED), jnp.float32) * scale, 'we_down': jax.random.normal(ks[4], (NUM_EXPERTS, EMBED, EMBED), jnp.float32) * scale}
    _L1_ffn_all = _L1_ffn_setup()
    _L1_ffn_in = {k: v for k, v in _L1_ffn_all.items() if k in ('router_w', 'router_b', 'we_gate', 'we_up', 'we_down')}
    del _L1_ffn_all
    return {'x': x, 'L0_tok_W': _L0_tok_in['W'], 'L0_tok_b': _L0_tok_in['b'], 'L0_attn_proj_mat': _L0_attn_in['proj_mat'], 'L0_attn_wq': _L0_attn_in['wq'], 'L0_attn_bq': _L0_attn_in['bq'], 'L0_attn_wk': _L0_attn_in['wk'], 'L0_attn_bk': _L0_attn_in['bk'], 'L0_attn_wv': _L0_attn_in['wv'], 'L0_attn_bv': _L0_attn_in['bv'], 'L0_attn_wo': _L0_attn_in['wo'], 'L0_attn_bo': _L0_attn_in['bo'], 'L0_attn_ln1_g': _L0_attn_in['ln1_g'], 'L0_attn_ln1_b': _L0_attn_in['ln1_b'], 'L0_attn_w1': _L0_attn_in['w1'], 'L0_attn_b1': _L0_attn_in['b1'], 'L0_attn_w2': _L0_attn_in['w2'], 'L0_attn_b2': _L0_attn_in['b2'], 'L0_attn_ln2_g': _L0_attn_in['ln2_g'], 'L0_attn_ln2_b': _L0_attn_in['ln2_b'], 'L0_ffn_w1': _L0_ffn_in['w1'], 'L0_ffn_b1': _L0_ffn_in['b1'], 'L0_ffn_w2': _L0_ffn_in['w2'], 'L0_ffn_b2': _L0_ffn_in['b2'], 'L1_attn_Wq': _L1_attn_in['Wq'], 'L1_attn_bq': _L1_attn_in['bq'], 'L1_attn_Wk': _L1_attn_in['Wk'], 'L1_attn_bk': _L1_attn_in['bk'], 'L1_attn_Wv': _L1_attn_in['Wv'], 'L1_attn_bv': _L1_attn_in['bv'], 'L1_ffn_router_w': _L1_ffn_in['router_w'], 'L1_ffn_router_b': _L1_ffn_in['router_b'], 'L1_ffn_we_gate': _L1_ffn_in['we_gate'], 'L1_ffn_we_up': _L1_ffn_in['we_up'], 'L1_ffn_we_down': _L1_ffn_in['we_down']}

def reference(x, L0_tok_W, L0_tok_b, L0_attn_proj_mat, L0_attn_wq, L0_attn_bq, L0_attn_wk, L0_attn_bk, L0_attn_wv, L0_attn_bv, L0_attn_wo, L0_attn_bo, L0_attn_ln1_g, L0_attn_ln1_b, L0_attn_w1, L0_attn_b1, L0_attn_w2, L0_attn_b2, L0_attn_ln2_g, L0_attn_ln2_b, L0_ffn_w1, L0_ffn_b1, L0_ffn_w2, L0_ffn_b2, L1_attn_Wq, L1_attn_bq, L1_attn_Wk, L1_attn_bk, L1_attn_Wv, L1_attn_bv, L1_ffn_router_w, L1_ffn_router_b, L1_ffn_we_gate, L1_ffn_we_up, L1_ffn_we_down):
    import jax
    import jax.numpy as jnp

    def _L0_tok_ref(val, W, b):
        import jax, jax.numpy as jnp
        import numpy as np
        PATCH = 16
        D_MODEL = 256

        def patchify(imgs, p):
            n, c, H, W = imgs.shape
            h, w = (H // p, W // p)
            x = imgs.reshape(n, c, h, p, w, p)
            x = jnp.einsum('nchpwq->nhwpqc', x)
            return x.reshape(n, h * w, p * p * c)
        patches = patchify(val, PATCH)
        return jnp.einsum('nld,md->nlm', patches, W) + b

    def _L0_attn_ref(x, proj_mat, wq, bq, wk, bk, wv, bv, wo, bo, ln1_g, ln1_b, w1, b1, w2, b2, ln2_g, ln2_b):
        import jax, jax.numpy as jnp
        import numpy as np
        import math
        D_MODEL = 256
        N_HEAD = 16
        D_HEAD = D_MODEL // N_HEAD
        D_KMAP = 128
        D_INNER = 1024

        def _layer_norm(x, g, b, eps=1e-05):
            mu = jnp.mean(x, axis=-1, keepdims=True)
            var = jnp.mean(jnp.square(x - mu), axis=-1, keepdims=True)
            return (x - mu) * jax.lax.rsqrt(var + eps) * g + b

        def _fourier_kernel(x, proj_mat):
            p = jnp.einsum('blhd,dm->blhm', x, proj_mat) / math.sqrt(D_HEAD)
            return jnp.concatenate([jnp.cos(p), jnp.sin(p)], axis=-1) / math.sqrt(D_KMAP)
        B, L, _ = x.shape
        x2 = _layer_norm(x, ln1_g, ln1_b)
        q = (x2 @ wq + bq).reshape(B, L, N_HEAD, D_HEAD)
        k = (x2 @ wk + bk).reshape(B, L, N_HEAD, D_HEAD)
        v = (x2 @ wv + bv).reshape(B, L, N_HEAD, D_HEAD)
        qp = _fourier_kernel(q, proj_mat)
        kp = _fourier_kernel(k, proj_mat)
        kv = jnp.einsum('blhm,blhd->bhmd', kp, v)
        attn = jnp.einsum('blhm,bhmd->blhd', qp, kv)
        attn = attn.reshape(B, L, D_MODEL) @ wo + bo
        x = x + attn
        x2 = _layer_norm(x, ln2_g, ln2_b)
        h = jax.nn.relu(x2 @ w1 + b1)
        x = x + (h @ w2 + b2)
        return x

    def _L0_ffn_ref(x, w1, b1, w2, b2):
        import jax, jax.numpy as jnp
        import numpy as np
        EPS = 1e-05

        def rmsnorm(x):
            var = jnp.mean(jnp.square(x), axis=-1, keepdims=True)
            return x * jax.lax.rsqrt(var + 1e-06)

        def activation_quant(x):
            scale = 127.0 / jnp.clip(jnp.max(jnp.abs(x), axis=-1, keepdims=True), EPS, None)
            return jnp.clip(jnp.round(x * scale), -128, 127) / scale

        def weight_quant(w):
            scale = 1.0 / jnp.clip(jnp.mean(jnp.abs(w)), EPS, None)
            return jnp.clip(jnp.round(w * scale), -1, 1) / scale

        def bitlinear(x, w, b):
            xn = rmsnorm(x)
            xq = xn + jax.lax.stop_gradient(activation_quant(xn) - xn)
            wq = w + jax.lax.stop_gradient(weight_quant(w) - w)
            return jnp.einsum('bsi,oi->bso', xq, wq) + b
        h = bitlinear(x, w1, b1)
        h = jax.nn.gelu(h, approximate=False)
        return bitlinear(h, w2, b2)

    def _L1_attn_ref(x, Wq, bq, Wk, bk, Wv, bv):
        import jax, jax.numpy as jnp
        import numpy as np
        EMBED = 256
        E = x.shape[-1]
        Q = jnp.einsum('bse,fe->bsf', x, Wq) + bq
        K = jnp.einsum('bse,fe->bsf', x, Wk) + bk
        V = jnp.einsum('bse,fe->bsf', x, Wv) + bv
        scores = jnp.einsum('bqe,bke->bqk', Q, K) / jnp.sqrt(jnp.float32(E))
        S = x.shape[1]
        causal = jnp.tril(jnp.ones((S, S), dtype=bool))
        scores = jnp.where(causal, scores, -jnp.inf)
        attn = jax.nn.softmax(scores, axis=-1)
        return jnp.einsum('bqk,bke->bqe', attn, V)

    def _L1_ffn_ref(x, router_w, router_b, we_gate, we_up, we_down):
        import jax, jax.numpy as jnp
        import numpy as np
        EMBED = 256
        NUM_EXPERTS = 8
        TOP_K = 2
        x_shape = x.shape
        x_flat = x.reshape(-1, x_shape[-1])
        num_tokens = x_flat.shape[0]
        router_logits = x_flat @ router_w + router_b
        topk_weights, topk_indices = jax.lax.top_k(router_logits, k=TOP_K)
        topk_weights = jax.nn.softmax(topk_weights, axis=-1)
        token_idx_mesh = jnp.repeat(jnp.arange(num_tokens), TOP_K)
        expert_idx_mesh = topk_indices.reshape(-1)
        sort_permutation = jnp.argsort(expert_idx_mesh)
        sorted_expert_idx = expert_idx_mesh[sort_permutation]
        sorted_token_idx = token_idx_mesh[sort_permutation]
        group_sizes = jnp.bincount(sorted_expert_idx, length=NUM_EXPERTS)
        sorted_tokens = x_flat[sorted_token_idx]
        ff_gate = jax.lax.ragged_dot(sorted_tokens, we_gate, group_sizes)
        ff_up = jax.lax.ragged_dot(sorted_tokens, we_up, group_sizes)
        activated = jax.nn.silu(ff_gate) * ff_up
        ff_out = jax.lax.ragged_dot(activated, we_down, group_sizes)
        sorted_weights = topk_weights.reshape(-1)[sort_permutation]
        ff_out = ff_out * sorted_weights[:, None]
        output_flat = jnp.zeros_like(x_flat).at[sorted_token_idx].add(ff_out)
        return output_flat.reshape(x_shape)
    h = _L0_tok_ref(x, L0_tok_W, L0_tok_b)
    h = h + _L0_attn_ref(_layernorm(h, axis=-1), L0_attn_proj_mat, L0_attn_wq, L0_attn_bq, L0_attn_wk, L0_attn_bk, L0_attn_wv, L0_attn_bv, L0_attn_wo, L0_attn_bo, L0_attn_ln1_g, L0_attn_ln1_b, L0_attn_w1, L0_attn_b1, L0_attn_w2, L0_attn_b2, L0_attn_ln2_g, L0_attn_ln2_b)
    h = h + _L0_ffn_ref(_layernorm(h, axis=-1), L0_ffn_w1, L0_ffn_b1, L0_ffn_w2, L0_ffn_b2)
    h = h + _L1_attn_ref(_layernorm(h, axis=-1), L1_attn_Wq, L1_attn_bq, L1_attn_Wk, L1_attn_bk, L1_attn_Wv, L1_attn_bv)
    h = h + _L1_ffn_ref(_layernorm(h, axis=-1), L1_ffn_router_w, L1_ffn_router_b, L1_ffn_we_gate, L1_ffn_we_up, L1_ffn_we_down)
    return h

_drawn_inputs = setup_inputs


def setup_inputs(seed=0):
    import zlib

    import numpy as np

    out = dict(_drawn_inputs(seed))
    spreads = {'L0_attn_bq': (0.0, 0.777),
     'L0_attn_bk': (0.0, 0.753),
     'L0_attn_bv': (0.0, 0.1),
     'L0_attn_bo': (0.0, 0.52),
     'L0_attn_ln1_g': (1.0, 0.2),
     'L0_attn_ln1_b': (0.0, 0.1),
     'L0_attn_b1': (0.0, 0.8),
     'L0_attn_b2': (0.0, 0.451),
     'L0_attn_ln2_g': (1.0, 0.6),
     'L0_attn_ln2_b': (0.0, 0.8),
     'L0_ffn_b1': (0.0, 0.48),
     'L0_ffn_b2': (0.0, 0.522),
     'L1_ffn_router_b': (0.0, 0.602)}
    factors = {'L0_attn_proj_mat': 7.193,
     'L0_attn_wk': 4.746,
     'L0_attn_w1': 2.676,
     'L1_attn_Wq': 8.0,
     'L1_attn_bq': 8.0,
     'L1_attn_Wk': 8.0,
     'L1_attn_bk': 8.0,
     'L1_attn_bv': 8.0}
    for name, (base, spread) in spreads.items():
        noise = np.random.default_rng([zlib.crc32(name.encode()), seed]).standard_normal(out[name].shape)
        drawn = base * np.exp(spread * noise) if base else spread * noise
        out[name] = jnp.asarray(drawn.astype(out[name].dtype))
    for name, factor in factors.items():
        out[name] = (out[name] * factor).astype(out[name].dtype)
    return out
```

```python
from contextlib import ExitStack

import numpy as np

import concourse.bass as bass
from concourse import mybir

ALU = mybir.AluOpType
ACT = mybir.ActivationFunctionType
AX = mybir.AxisListType
F32 = mybir.dt.float32
BF16 = mybir.dt.bfloat16
U32 = mybir.dt.uint32

P = 128
LANES = 2
EPS = 1e-5
RMS_EPS = 1e-6
QUANT_EPS = 1e-5
ROUND = 1.5 * 2.0 ** 23
TURN = float(np.nextafter(np.float32(2 * np.pi), np.float32(0)))
NEG = -1e30


class Signal:

    def __init__(self, ctx, nc, name, per, credit=False):
        self.sems = [ctx.enter_context(nc.semaphore(f"{name}_{lane}")) for lane in range(LANES)]
        self.per = per
        self.credit = per if credit else 0

    def __getitem__(self, lane):
        return self.sems[lane]

    def at(self, i, k=None):
        return i * self.per + (self.per if k is None else k) + self.credit

    def before(self, i, k=None):
        return i * self.per + (self.per if k is None else k)


def vit_tower(nc, x, tok_W, tok_b, proj_mat, wq, bq, wk, bk, wv, bv, wo, bo, ln1_g, ln1_b, w1, b1, w2, b2,
              ln2_g, ln2_b, ffn_w1, ffn_b1, ffn_w2, ffn_b2, Wq, cbq, Wk, cbk, Wv, cbv,
              router_w, router_b, we_gate, we_up, we_down, out):
    IMAGES, CH, SIDE, _ = x.shape
    D = tok_W.shape[0]
    PATCH = 16
    GRID = SIDE // PATCH
    T = GRID * GRID
    C = T // 2
    KT = D // P
    DH, M = proj_mat.shape
    HEADS = D // DH
    PAIRS = HEADS // 2
    HID = w1.shape[1]
    HT = HID // P
    E = router_w.shape[1]
    HALF = PATCH // 2
    PR = CH * PATCH
    XP = 2 * PR
    UNITS = 2 * PAIRS
    SCORE_SCALE = 1.0 / float(np.sqrt(D))

    with ExitStack() as ctx:
        def sb(name, shape, dt=F32):
            return ctx.enter_context(nc.sbuf_tensor(name, shape, dt))

        def sem(name):
            return ctx.enter_context(nc.semaphore(name))

        def signal(name, per, credit=False):
            return Signal(ctx, nc, name, per, credit)

        tok_w = sb("tok_w", [XP, HALF, D])
        wq_s, wk_s, wv_s, wo_s = (sb(n, [P, KT, D]) for n in ("wq_s", "wk_s", "wv_s", "wo_s"))
        w1_s = sb("w1_s", [P, KT, HID])
        w2_s = sb("w2_s", [P, HT, D])
        f1_s = sb("f1_s", [P, KT, HID], BF16)
        f2_s = sb("f2_s", [P, HT, D], BF16)
        cq_s, ck_s, cv_s = (sb(n, [P, KT, D]) for n in ("cq_s", "ck_s", "cv_s"))
        gate_s, up_s, down_s = (sb(n, [P, E, KT, D]) for n in ("gate_s", "up_s", "down_s"))
        router_s = sb("router_s", [P, KT, E])
        proj_s = sb("proj_s", [P, 2, M])
        cols = sb("cols", [P, 9, KT])
        b1_col = sb("b1_col", [P, HT])
        tok_b_s, bv_s, bo_s, b2_s, fb2_s, cbv_s = (
            sb(n, [C, D]) for n in ("tok_b_s", "bv_s", "bo_s", "b2_s", "fb2_s", "cbv_s"))
        fb1_s = sb("fb1_s", [C, HID])
        rb_s = sb("rb_s", [C, 2, E])
        mask = sb("mask", [C, 3 * C])
        ident = sb("ident", [P, P])
        ident_b = sb("ident_b", [P, P], BF16)
        ones = sb("ones", [P, P])
        expert_no = sb("expert_no", [C, E])
        half_pi = sb("half_pi", [P, 1])
        pair_of = {n: sb(name, [C, 2]) for n, name in
                   ((-0.5, "minus_half"), (EPS, "eps_pair"), (RMS_EPS, "rms_eps_pair"), (1.0 / HID, "hid_share"))}
        wsum = sb("wsum", [P, 2])
        wscale = sb("wscale", [P, 2])
        wrecip = sb("wrecip", [P, 2])

        patches = [sb(f"patches{l}", [P, GRID * SIDE]) for l in range(LANES)]
        h = [sb(f"h{l}", [C, 2, D]) for l in range(LANES)]
        a = [sb(f"a{l}", [C, 2, D]) for l in range(LANES)]
        zn = [sb(f"zn{l}", [C, 2, D]) for l in range(LANES)]
        v = [sb(f"v{l}", [C, 2, D]) for l in range(LANES)]
        xT = [sb(f"xT{l}", [P, KT, T]) for l in range(LANES)]
        qT = [sb(f"qT{l}", [P, KT, T]) for l in range(LANES)]
        kT = [sb(f"kT{l}", [P, KT, T]) for l in range(LANES)]
        kv = [sb(f"kv{l}", [P, PAIRS, 2, 2, 2 * DH]) for l in range(LANES)]
        arena = [sb(f"arena{l}", [P, 4096]) for l in range(LANES)]
        stats = [sb(f"stats{l}", [C, 2, 6]) for l in range(LANES)]
        mv = [sb(f"mv{l}", [C, 2, 2]) for l in range(LANES)]
        sm = [sb(f"sm{l}", [C, 16, 2]) for l in range(LANES)]
        rt = [sb(f"rt{l}", [C, 6, 2, E]) for l in range(LANES)]
        rt_i = [sb(f"rt_i{l}", [C, 2, E], U32) for l in range(LANES)]
        bank = [[ctx.enter_context(nc.psum_tensor(f"bank{l}{b}", [P, 512], F32)) for b in range(4)]
                for l in range(LANES)]

        VE, RSTD, R2, TMP, AMAX, DQ, RR, SUM, NMAX, RSUM, QS, D12, E12, W1, W2, SQ = range(16)
        LOGIT, TOP, IDX, OH1, OH2, WSEL = range(6)
        G1, B1, G2, B2, BQ, BK, CBQ, CBK = range(8)

        def col(n, t):
            return cols[:, n, t:t + 1]

        def small(l, n, c=None):
            return sm[l][:, n, :] if c is None else sm[l][:, n, c:c + 1]

        def tm(b):
            return b[0:C, :].rearrange("p (c d) -> p c d", c=2)

        def fm(b):
            return b[:, 0:KT * T].rearrange("p (k t) -> p k t", k=KT)

        def chunk(c):
            return slice(c * C, (c + 1) * C)

        keys = (slice(0, C), slice(C, 3 * C))

        def both(bias):
            return bias[:, :].unsqueeze(1).broadcast_to([C, 2, D])

        def feat(l, u):
            s = (u % 2) * 2048
            return arena[l][:, s:s + 1024].rearrange("p (f n) -> p f n", f=2)

        def frac(l, u):
            s = (u % 2) * 2048 + 1024
            return arena[l][:, s:s + 512], arena[l][:, s + 512:s + 1024]

        def hidT(l):
            return arena[l][:, 0:HT * T].rearrange("p (m t) -> p m t", m=HT)

        def hid(l):
            return arena[l][0:C, 0:2 * HID].rearrange("p (c n) -> p c n", c=2)

        def squares(l, c):
            return arena[l][0:C, (2 + c) * HID:(3 + c) * HID]

        def qhid(l):
            return arena[l][0:C, 2 * HID:3 * HID].bitcast(BF16).rearrange("p (c n) -> p c n", c=2)

        def qhidT(l):
            return arena[l][:, 3 * HID:3 * HID + HT * T // 2].bitcast(BF16).rearrange("p (m t) -> p m t", m=HT)

        def qin(l):
            return a[l][:, 0, :].bitcast(BF16).rearrange("p (c d) -> p c d", c=2)

        def qinT(l):
            return xT[l][:, 0, :].bitcast(BF16).rearrange("p (k t) -> p k t", k=KT)

        def score(l):
            return arena[l][0:C, 0:3 * C]

        def prob(l):
            return arena[l][0:C, 512:512 + 3 * C]

        def probT(l):
            return arena[l][0:C, 1024:1024 + 3 * C].rearrange("p (b t) -> p b t", b=3)

        def silu(l):
            return arena[l][:, 0:KT * T]

        def gated(l):
            return arena[l][:, 512:512 + KT * T].rearrange("p (k t) -> p k t", k=KT)

        f1_in = arena[0][:, 0:2048].rearrange("p (t d) -> p t d", t=HT)
        f2_in = arena[0][:, 2048:4096].rearrange("p (t n) -> p t n", t=KT)
        tok_in = arena[1][:, 0:KT * CH * PATCH * PATCH].rearrange("p (t f) -> p t f", t=KT)
        c_in = [arena[1][:, 1536 + 512 * n:2048 + 512 * n].rearrange("p (t d) -> p t d", t=KT) for n in range(3)]
        f1_t = [sb("f1_q", [P, HT, D], BF16), sb("f2_q", [P, KT, HID], BF16)]

        weights_in = sem("weights_in")
        staged_in = sem("staged_in")
        proj_clear = sem("proj_clear")
        consts = sem("consts")
        pool_start = sem("pool_start")
        dve_start = sem("dve_start")
        wsum_ready = sem("wsum_ready")
        wsum_all = sem("wsum_all")
        ternary = sem("ternary")
        ordered = sem("ordered")
        turned = sem("turned")
        waits_passed = sem("waits_passed")
        turned_out = sem("turned_out")
        scales_ready = sem("scales_ready")

        patches_in = signal("patches_in", 16 * XP // PATCH)
        patches_used = signal("patches_used", 1, credit=True)
        stored = signal("stored", 16, credit=True)
        tok_done = signal("tok_done", 1)
        h_ready = signal("h_ready", 4)
        bn_done = signal("bn_done", 5)
        mean_ready = signal("mean_ready", 5)
        var_ready = signal("var_ready", 5)
        pool_step = signal("pool_step", 11)
        rstd_ready = signal("rstd_ready", 5)
        a_ready = signal("a_ready", 1)
        ab_ready = signal("ab_ready", 1)
        zn_ready = signal("zn_ready", 5)
        xT_done = signal("xT_done", 4)
        xT_ready = signal("xT_ready", 4)
        q_done, k_done, v_done = (signal(n, 2) for n in ("q_done", "k_done", "v_done"))
        q_ready, k_ready, v_ready = (signal(n, 2) for n in ("q_ready", "k_ready", "v_ready"))
        phase_done = signal("phase_done", UNITS)
        turns_ready = signal("turns_ready", UNITS)
        frac_ready = signal("frac_ready", UNITS)
        abs_ready = signal("abs_ready", UNITS)
        feat_ready = signal("feat_ready", UNITS)
        feat_used = signal("feat_used", UNITS)
        kv_done = signal("kv_done", 1)
        kv_ready = signal("kv_ready", 1)
        att_done = signal("att_done", 1)
        att_ready = signal("att_ready", 1)
        wo_done = signal("wo_done", 1)
        x1_ready = signal("x1_ready", 1)
        hx_ready = signal("hx_ready", 2)
        up_done = signal("up_done", 4)
        relu_ready = signal("relu_ready", 4)
        mlp_done = signal("mlp_done", 1)
        quant_step = signal("quant_step", 13)
        rms_ready = signal("rms_ready", 1)
        qin_ready = signal("qin_ready", 1)
        qinT_done = signal("qinT_done", 1)
        qinT_ready = signal("qinT_ready", 1)
        f1_done = signal("f1_done", 4)
        pre_ready = signal("pre_ready", 4)
        gelu_ready = signal("gelu_ready", 2)
        sq_ready = signal("sq_ready", 1)
        qhid_ready = signal("qhid_ready", 1)
        qhidT_done = signal("qhidT_done", 2)
        qhidT_ready = signal("qhidT_ready", 2)
        f2_done = signal("f2_done", 1)
        score_done = signal("score_done", 1)
        score_ready = signal("score_ready", 1)
        nmax_ready = signal("nmax_ready", 1)
        prob_ready = signal("prob_ready", 1)
        probT_done = signal("probT_done", 1)
        probT_ready = signal("probT_ready", 1)
        rsum_ready = signal("rsum_ready", 1)
        pv_done = signal("pv_done", 1)
        logit_done = signal("logit_done", 1)
        route_step = signal("route_step", 9)
        gap_ready = signal("gap_ready", 1)
        gap_exp = signal("gap_exp", 1)
        gu_done = signal("gu_done", E)
        silu_ready = signal("silu_ready", E)
        gated_ready = signal("gated_ready", E)
        down_done = signal("down_done", E)
        acc_ready = signal("acc_ready", E)

        PAIRS_OF_IMAGES = IMAGES // LANES
        lanes = range(LANES)

        tok_feat = tok_in.rearrange("m t (p j q c) -> m t j q c p", p=PATCH, j=2, c=CH)
        tok_order = patches[0][:, 0:KT * HALF * XP].rearrange("m (t q j c p) -> m t j q c p", t=KT, q=HALF, j=2, c=CH)

        block = ctx.enter_context(nc.Block())

        @block.sync
        def _(sp):
            sp.dma_start(f1_in, ffn_w1.rearrange("(t p) d -> p t d", p=P)).then_inc(staged_in, 16)
            sp.dma_start(f2_in, ffn_w2.rearrange("(t p) n -> p t n", p=P)).then_inc(staged_in, 16)
            sp.dma_start(tok_in, tok_W.rearrange("(t p) f -> p t f", p=P)).then_inc(staged_in, 16)
            for stage, w in zip(c_in, (Wq, Wk, Wv)):
                sp.dma_start(stage, w.rearrange("(t p) d -> p t d", p=P)).then_inc(staged_in, 16)
            sp.wait_ge(proj_clear, 1)
            for r in range(P // (2 * DH)):
                for s in range(2):
                    sp.dma_start(proj_s[32 * r + DH * s:32 * r + DH * s + DH, s, :], proj_mat).then_inc(staged_in, 16)

            def image(i, l):
                sp.wait_ge(patches_used[l], patches_used.before(i))
                for half in range(2):
                    for c in range(CH):
                        q0 = half * HALF
                        sp.dma_start(
                            patches[l][half * PR + c * PATCH:half * PR + (c + 1) * PATCH, :]
                            .rearrange("p (g w) -> p g w", g=GRID)[:, :, 0:SIDE - q0],
                            x[i * LANES + l, c].rearrange("(g p) w -> p g w", p=PATCH)[:, :, q0:SIDE],
                        ).then_inc(patches_in[l], 16)

            for dst, src in ((wq_s, wq), (wk_s, wk), (wv_s, wv), (wo_s, wo), (w1_s, w1), (w2_s, w2),
                             (router_s, router_w)):
                sp.dma_start(dst[:, :, :], src.rearrange("(t p) n -> p t n", p=P)).then_inc(weights_in, 16)
            for n, src in ((G1, ln1_g), (B1, ln1_b), (G2, ln2_g), (B2, ln2_b), (BQ, bq), (BK, bk), (CBQ, cbq), (CBK, cbk)):
                sp.dma_start(cols[:, n, :], src.rearrange("(t p) -> p t", p=P), allow_slow_non_contiguous=True).then_inc(weights_in, 16)
            sp.dma_start(b1_col[:, :], b1.rearrange("(t p) -> p t", p=P), allow_slow_non_contiguous=True).then_inc(weights_in, 16)
            for dst, src in ((tok_b_s, tok_b), (bv_s, bv), (bo_s, bo), (b2_s, b2), (fb2_s, ffn_b2), (cbv_s, cbv), (fb1_s, ffn_b1)):
                sp.dma_start(dst[:, :], src.rearrange("(o n) -> o n", o=1).broadcast_to([C, src.shape[0]])).then_inc(weights_in, 16)
            for c in range(2):
                sp.dma_start(rb_s[:, c, :], router_b.rearrange("(o n) -> o n", o=1).broadcast_to([C, E])).then_inc(weights_in, 16)
            for dst, src in ((gate_s, we_gate), (up_s, we_up), (down_s, we_down)):
                for e in range(E):
                    sp.dma_start(dst[:, e, :, :], src[e].rearrange("(t p) n -> p t n", p=P)).then_inc(weights_in, 16)
            with sp.Fori(0, PAIRS_OF_IMAGES) as i:
                for l in lanes:
                    image(i, l)
        POOL_START = 11
        WEIGHTS = 16 * (7 + 8 + 1 + 7 + 2 + 3 * E)
        STAGED = 16 * (2 + 1 + 3 + 8)

        @block.tensor
        def _(pe):
            pe.wait_ge(consts, 1)
            pe.wait_ge(wsum_ready, 1)
            pe.matmul(bank[0][0][:, 0:2], ones[:, :], wsum[:, :], start=True, stop=True).then_inc(wsum_all, 1)
            pe.wait_ge(staged_in, STAGED)
            pe.wait_ge(ordered, 1)
            group = 0
            for q in range(HALF):
                b = bank[1][group % 4]
                if group >= 4:
                    pe.wait_ge(turned_out, group - 3)
                for t in range(KT):
                    last = pe.transpose(b[0:XP, t * P:(t + 1) * P], patches[0][:, (t * HALF + q) * XP:(t * HALF + q + 1) * XP], ident[:, :])
                last.then_inc(turned, 1)
                group += 1
            for l in lanes:
                pe.drain().then_inc(patches_used[l], patches_used.credit)
            for n in range(3):
                b = bank[1][group % 4]
                pe.wait_ge(turned_out, group - 3)
                for kt in range(KT):
                    for t in range(KT):
                        last = pe.transpose(b[:, kt * D + t * P:kt * D + (t + 1) * P], c_in[n][:, t, kt * P:(kt + 1) * P], ident[:, :])
                last.then_inc(turned, 1)
                group += 1
            for n, (src, KN, ON) in enumerate(((f1_t[0], KT, HT), (f1_t[1], HT, KT))):
                pe.wait_ge(ternary, n + 1)
                for kt in range(KN):
                    b = bank[1][group % 4].bitcast(BF16)
                    pe.wait_ge(turned_out, group - 3)
                    for t in range(ON):
                        last = pe.transpose(b[:, t * P:(t + 1) * P], src[:, t, kt * P:(kt + 1) * P], ident_b[:, :])
                    last.then_inc(turned, 1)
                    group += 1
            pe.wait_ge(turned_out, group)
            pe.wait_ge(weights_in, WEIGHTS)
            pe.wait_ge(scales_ready, 3)

            def turn(i, l, b, src, n):
                pe.wait_ge(zn_ready[l], zn_ready.at(i, n + 1))
                for kt in range(KT):
                    for c in range(2):
                        last = pe.transpose(fm(b)[:, kt, chunk(c)], src[:, c, kt * P:(kt + 1) * P], ident[0:C, 0:C])
                return last

            def by_feature(dst, w, src, nk=KT):
                for m in range(dst.shape[1]):
                    for kt in range(nk):
                        last = pe.matmul(dst[:, m, :], w[:, kt, m * P:(m + 1) * P], src[:, kt, :],
                                         start=(kt == 0), stop=(kt == nk - 1))
                return last

            def by_token(dst, src, w, nk=KT):
                for c in range(2):
                    for kt in range(nk):
                        last = pe.matmul(dst[:, c, :], src[:, kt, chunk(c)], w[:, kt, :],
                                         start=(kt == 0), stop=(kt == nk - 1))
                return last

            def embed(i, l):
                pe.wait_ge(patches_in[l], patches_in.at(i))
                pix = patches[l][0:XP, :].rearrange("p (t q) -> p t q", q=PATCH)
                for c in range(2):
                    for q in range(HALF):
                        last = pe.matmul(tm(bank[l][0])[:, c, :], pix[:, chunk(c), q], tok_w[:, q, :],
                                         start=(q == 0), stop=(q == HALF - 1))
                last.then_inc(tok_done[l], 1)
                pe.drain().then_inc(patches_used[l], 1)

            def project(i, l, n, x_n, ws, banks):
                pe.wait_ge(xT_ready[l], xT_ready.at(i, x_n))
                by_feature(fm(banks[0]), ws[0], xT[l]).then_inc(q_done[l], 1)
                by_feature(fm(banks[1]), ws[1], xT[l]).then_inc(k_done[l], 1)
                by_token(tm(banks[2]), xT[l], ws[2]).then_inc(v_done[l], 1)

            def phases(i, l, u):
                b = bank[l][1 + u % 2]
                if u >= 2:
                    pe.wait_ge(frac_ready[l], frac_ready.at(i, u - 1))
                pair = u % PAIRS
                kt, r = divmod(pair, 4)
                rows = slice(32 * r, 32 * r + 32)
                if u == 0:
                    pe.wait_ge(k_ready[l], k_ready.at(i, 1))
                if u == PAIRS:
                    pe.wait_ge(q_ready[l], q_ready.at(i, 1))
                for s in range(2):
                    if u < PAIRS:
                        last = pe.matmul(tm(b)[:, s, :], kT[l][rows, kt, chunk(s)], proj_s[rows, :, :].rearrange("p s m -> p (s m)"),
                                         start=True, stop=True)
                    else:
                        last = pe.matmul(fm(b)[:, s, :], proj_s[rows, s, :], qT[l][rows, kt, :], start=True, stop=True)
                last.then_inc(phase_done[l], 1)

            def attend(i, l, u):
                pe.wait_ge(feat_ready[l], feat_ready.at(i, u + 1))
                pair = u % PAIRS
                if u < PAIRS:
                    if u == 0:
                        pe.wait_ge(v_ready[l], v_ready.at(i, 1))
                    f = feat(l, u)[0:C].rearrange("p f (c s m) -> p f c s m", c=2, s=2)
                    for s in range(2):
                        for g in range(2):
                            at = ((pair * 2 + s) * 2 + g) * DH
                            for c in range(2):
                                last = pe.matmul(bank[l][3][:, at:at + DH], f[:, g, c, s, :],
                                                 v[l][:, c, (2 * pair + s) * DH:(2 * pair + s + 1) * DH],
                                                 start=(c == 0), stop=(c == 1))
                    last.then_inc(feat_used[l], 1)
                    if u == PAIRS - 1:
                        pe.drain().then_inc(kv_done[l], 1)
                else:
                    if u == PAIRS:
                        pe.wait_ge(kv_ready[l], kv_ready.at(i))
                    kt, r = divmod(pair, 4)
                    f = feat(l, u)[:, :, 0:KT * T].rearrange("p f (s t) -> p f s t", s=2)
                    for n in range(4):
                        s, g = divmod(n, 2)
                        last = pe.matmul(fm(bank[l][0])[32 * r:32 * r + 32, kt, :], kv[l][:, pair, s, g, :], f[:, g, s, :],
                                         start=(n == 0), stop=(n == 3))
                    last.then_inc(feat_used[l], 1)
                    if u == UNITS - 1:
                        pe.drain().then_inc(att_done[l], 1)

            def mlp_up(i, l):
                pe.wait_ge(xT_ready[l], xT_ready.at(i, 2))
                for n, b in enumerate((1, 2, 3, 0)):
                    by_feature(fm(bank[l][b]), w1_s[:, :, n * 2 * P:(n + 1) * 2 * P], xT[l]).then_inc(up_done[l], 1)

            with pe.Fori(0, PAIRS_OF_IMAGES) as i:
                for l in lanes:
                    embed(i, l)
                for l in lanes:
                    turn(i, l, bank[l][1], zn[l], 0).then_inc(xT_done[l], 1)
                for l in lanes:
                    project(i, l, 0, 1, (wq_s, wk_s, wv_s), (bank[l][2], bank[l][3], bank[l][0]))
                for u in range(UNITS + 1):
                    for l in lanes:
                        if u < UNITS:
                            phases(i, l, u)
                    for l in lanes:
                        if u >= 1:
                            attend(i, l, u - 1)
                for l in lanes:
                    pe.wait_ge(att_ready[l], att_ready.at(i))
                    by_token(tm(bank[l][3]), xT[l], wo_s).then_inc(wo_done[l], 1)
                for l in lanes:
                    turn(i, l, bank[l][0], zn[l], 1).then_inc(xT_done[l], 1)
                for l in lanes:
                    mlp_up(i, l)
                for l in lanes:
                    pe.wait_ge(relu_ready[l], relu_ready.at(i))
                    by_token(tm(bank[l][1]), hidT(l), w2_s, HT).then_inc(mlp_done[l], 1)
                for l in lanes:
                    pe.wait_ge(qin_ready[l], qin_ready.at(i))
                    b = bank[l][2].bitcast(BF16)[:, 0:KT * T].rearrange("p (k t) -> p k t", k=KT)
                    for kt in range(KT):
                        for c in range(2):
                            last = pe.transpose(b[:, kt, chunk(c)], qin(l)[:, c, kt * P:(kt + 1) * P], ident_b[0:C, 0:C])
                    last.then_inc(qinT_done[l], 1)
                for l in lanes:
                    pe.wait_ge(qinT_ready[l], qinT_ready.at(i))
                    for n, b in enumerate((3, 0, 1, 2)):
                        c, half = divmod(n, 2)
                        for kt in range(KT):
                            last = pe.matmul(bank[l][b][0:C, :], qinT(l)[:, kt, chunk(c)], f1_s[:, kt, half * 512:(half + 1) * 512],
                                             start=(kt == 0), stop=(kt == KT - 1))
                        last.then_inc(f1_done[l], 1)
                for l in lanes:
                    pe.wait_ge(qhid_ready[l], qhid_ready.at(i))
                    for n, b in enumerate((3, 0)):
                        bb = bank[l][b].bitcast(BF16)[:, 0:4 * T].rearrange("p (k t) -> p k t", k=4)
                        for kt in range(4):
                            for c in range(2):
                                last = pe.transpose(bb[:, kt, chunk(c)], qhid(l)[:, c, (4 * n + kt) * P:(4 * n + kt + 1) * P], ident_b[0:C, 0:C])
                        last.then_inc(qhidT_done[l], 1)
                for l in lanes:
                    pe.wait_ge(qhidT_ready[l], qhidT_ready.at(i))
                    by_token(tm(bank[l][1]), qhidT(l), f2_s, HT).then_inc(f2_done[l], 1)
                for l in lanes:
                    turn(i, l, bank[l][2], zn[l], 3).then_inc(xT_done[l], 1)
                for l in lanes:
                    project(i, l, 1, 3, (cq_s, ck_s, cv_s), (bank[l][3], bank[l][0], bank[l][1]))
                for l in lanes:
                    pe.wait_ge(q_ready[l], q_ready.at(i, 2))
                    pe.wait_ge(k_ready[l], k_ready.at(i, 2))
                    for c in range(2):
                        for kt in range(KT):
                            last = pe.matmul(bank[l][2][0:C, keys[c]], qT[l][:, kt, chunk(c)], kT[l][:, kt, 0:(c + 1) * C],
                                             start=(kt == 0), stop=(kt == KT - 1))
                    last.then_inc(score_done[l], 1)
                for l in lanes:
                    pe.wait_ge(prob_ready[l], prob_ready.at(i))
                    for n in range(3):
                        last = pe.transpose(bank[l][3][0:C, n * C:(n + 1) * C], prob(l)[:, n * C:(n + 1) * C], ident[0:C, 0:C])
                    last.then_inc(probT_done[l], 1)
                for l in lanes:
                    pe.wait_ge(probT_ready[l], probT_ready.at(i))
                    pe.wait_ge(v_ready[l], v_ready.at(i, 2))
                    pe.matmul(tm(bank[l][0])[:, 0, :], probT(l)[:, 0, :], v[l][:, 0, :], start=True, stop=True)
                    for c in range(2):
                        last = pe.matmul(tm(bank[l][0])[:, 1, :], probT(l)[:, 1 + c, :], v[l][:, c, :], start=(c == 0), stop=(c == 1))
                    last.then_inc(pv_done[l], 1)
                for l in lanes:
                    turn(i, l, bank[l][1], zn[l], 4).then_inc(xT_done[l], 1)
                for l in lanes:
                    pe.wait_ge(xT_ready[l], xT_ready.at(i, 4))
                    for c in range(2):
                        for kt in range(KT):
                            last = pe.matmul(bank[l][2][0:C, c * E:(c + 1) * E], xT[l][:, kt, chunk(c)], router_s[:, kt, :],
                                             start=(kt == 0), stop=(kt == KT - 1))
                    last.then_inc(logit_done[l], 1)
                for e in range(E):
                    for l in lanes:
                        by_feature(fm(bank[l][3]), gate_s[:, e], xT[l])
                        by_feature(fm(bank[l][0]), up_s[:, e], xT[l]).then_inc(gu_done[l], 1)
                    for l in lanes:
                        pe.wait_ge(gated_ready[l], gated_ready.at(i, e + 1))
                        by_token(tm(bank[l][1 + e % 2]), gated(l), down_s[:, e]).then_inc(down_done[l], 1)

        @block.gpsimd
        def _(pool):
            pool.memset(proj_s[:, :, :], 0.0).then_inc(proj_clear, 1)
            pool.memset(ones[:, :], 1.0).then_inc(pool_start, 1)
            pool.memset(mask[:, :], 0.0).then_inc(pool_start, 1)
            pool.memset(half_pi[:, :], float(np.pi / 2)).then_inc(pool_start, 1)
            for value, pair in pair_of.items():
                pool.memset(pair[:, :], value).then_inc(pool_start, 1)
            pool.wait_ge(pool_start, 7)
            pool.affine_select(out=ident[:, :], in_=ones[:, :], compare_op=ALU.is_equal, fill=0.0, base=0,
                               pattern=[[-1, P]], channel_multiplier=1).then_inc(pool_start, 1)
            for n in (0, 2):
                pool.affine_select(out=mask[:, n * C:(n + 1) * C], in_=mask[:, n * C:(n + 1) * C], compare_op=ALU.is_ge,
                                   fill=NEG, base=0, pattern=[[-1, C]], channel_multiplier=1).then_inc(pool_start, 1)
            pool.iota(expert_no[:, :], pattern=[[1, E]], base=0, channel_multiplier=0,
                      allow_small_or_imprecise_dtypes=True).then_inc(pool_start, 1)
            pool.wait_ge(pool_start, POOL_START)
            pool.tensor_copy(ident_b[:, :], ident[:, :]).then_inc(consts, 1)
            pool.wait_ge(weights_in, WEIGHTS)

            def inverse_root(i, l, n, k, second=None):
                def step(ins):
                    nonlocal k
                    k += 1
                    ins.then_inc(pool_step[l], 1)
                    pool.wait_ge(pool_step[l], pool_step.at(i, k))

                pool.wait_ge(var_ready[l], var_ready.at(i, n + 1))
                root = pool.tensor_tensor(small(l, RSTD), small(l, VE), pair_of[-0.5][:, :], ALU.pow)
                if second is None:
                    root.then_inc(rstd_ready[l], 1)
                    return k
                step(root)
                step(pool.tensor_tensor(small(l, TMP), small(l, RSTD), small(l, RSTD), ALU.mult))
                step(pool.tensor_tensor(small(l, TMP), mv[l][:, :, 1], small(l, TMP), ALU.mult))
                step(pool.tensor_tensor(small(l, TMP), small(l, TMP), pair_of[second][:, :], ALU.add))
                pool.tensor_tensor(small(l, R2), small(l, TMP), pair_of[-0.5][:, :], ALU.pow).then_inc(rstd_ready[l], 1)
                return k

            with pool.Fori(0, PAIRS_OF_IMAGES) as i:
                for l in lanes:
                    inverse_root(i, l, 0, 0, EPS)
                for l in lanes:
                    pool.wait_ge(zn_ready[l], zn_ready.at(i, 1))
                    pool.tensor_tensor(a[l][:, :, :], a[l][:, :, :], both(bo_s), ALU.add).then_inc(ab_ready[l], 1)
                for l in lanes:
                    pool.wait_ge(x1_ready[l], x1_ready.at(i))
                    pool.tensor_tensor(h[l][:, :, :], h[l][:, :, :], a[l][:, :, :], ALU.add).then_inc(pool_step[l], 1)
                    pool.wait_ge(pool_step[l], pool_step.at(i, 5))
                    pool.tensor_tensor(h[l][:, :, :], h[l][:, :, :], both(b2_s), ALU.add).then_inc(hx_ready[l], 1)
                    inverse_root(i, l, 1, 5)
                for l in lanes:
                    inverse_root(i, l, 2, 5, RMS_EPS)
                for l in lanes:
                    pool.wait_ge(qin_ready[l], qin_ready.at(i))
                    pool.tensor_tensor(h[l][:, :, :], h[l][:, :, :], both(fb2_s), ALU.add).then_inc(hx_ready[l], 1)
                for l in lanes:
                    pool.wait_ge(sq_ready[l], sq_ready.at(i))
                    pool.tensor_tensor(small(l, TMP), small(l, SQ), pair_of[1.0 / HID][:, :], ALU.mult).then_inc(pool_step[l], 1)
                    pool.wait_ge(pool_step[l], pool_step.at(i, 10))
                    pool.tensor_tensor(small(l, TMP), small(l, TMP), pair_of[RMS_EPS][:, :], ALU.add).then_inc(pool_step[l], 1)
                    pool.wait_ge(pool_step[l], pool_step.at(i, 11))
                    pool.tensor_tensor(small(l, RR), small(l, TMP), pair_of[-0.5][:, :], ALU.pow).then_inc(rms_ready[l], 1)
                for l in lanes:
                    inverse_root(i, l, 3, 11)
                for l in lanes:
                    inverse_root(i, l, 4, 11)

        @block.scalar
        def _(act):
            act.wait_ge(weights_in, WEIGHTS)
            act.wait_ge(pool_start, POOL_START)

            def turned_norm(i, l, b, n, g=None, beta=None):
                act.wait_ge(xT_done[l], xT_done.at(i, n))
                if g is None:
                    act.activation(xT[l][:, :, :], fm(b), ACT.Copy).then_inc(xT_ready[l], 1)
                    return
                for kt in range(KT):
                    last = act.activation(xT[l][:, kt, :], fm(b)[:, kt, :], ACT.Identity, bias=col(beta, kt), scale=col(g, kt))
                last.then_inc(xT_ready[l], 1)

            def biased(i, l, b, n, dst, done, ready, bias):
                act.wait_ge(done[l], done.at(i, n))
                for kt in range(KT):
                    last = act.activation(dst[l][:, kt, :], fm(b)[:, kt, :], ACT.Identity, bias=col(bias, kt))
                last.then_inc(ready[l], 1)

            def waves(i, l, u):
                rows, n = (C, 512) if u < PAIRS else (P, KT * T)
                near, dist = frac(l, u)
                f = feat(l, u)
                act.wait_ge(frac_ready[l], frac_ready.at(i, u + 1))
                if u >= 2:
                    act.wait_ge(feat_used[l], feat_used.at(i, u - 1))
                act.activation(f[0:rows, 1, 0:n], near[0:rows, 0:n], ACT.Sin, scale=TURN)
                act.wait_ge(abs_ready[l], abs_ready.at(i, u + 1))
                act.activation(f[0:rows, 0, 0:n], dist[0:rows, 0:n], ACT.Sin, bias=half_pi[0:rows, :], scale=-TURN).then_inc(feat_ready[l], 1)

            with act.Fori(0, PAIRS_OF_IMAGES) as i:
                for l in lanes:
                    turned_norm(i, l, bank[l][1], 1, G1, B1)
                for l in lanes:
                    biased(i, l, bank[l][2], 1, qT, q_done, q_ready, BQ)
                    biased(i, l, bank[l][3], 1, kT, k_done, k_ready, BK)
                for u in range(UNITS):
                    for l in lanes:
                        waves(i, l, u)
                for l in lanes:
                    act.wait_ge(att_done[l], att_done.at(i))
                    act.activation(xT[l][:, :, :], fm(bank[l][0]), ACT.Copy).then_inc(att_ready[l], 1)
                for l in lanes:
                    turned_norm(i, l, bank[l][0], 2, G2, B2)
                for l in lanes:
                    for n, b in enumerate((1, 2, 3, 0)):
                        act.wait_ge(up_done[l], up_done.at(i, n + 1))
                        for m in range(2):
                            last = act.activation(hidT(l)[:, 2 * n + m, :], fm(bank[l][b])[:, m, :], ACT.Relu,
                                                  bias=b1_col[:, 2 * n + m:2 * n + m + 1])
                        last.then_inc(relu_ready[l], 1)
                for l in lanes:
                    for c in range(2):
                        act.wait_ge(pre_ready[l], pre_ready.at(i, 2 * c + 2))
                        act.activation(hid(l)[:, c, :], hid(l)[:, c, :], ACT.Gelu).then_inc(gelu_ready[l], 1)
                    for c in range(2):
                        act.wait_ge(gelu_ready[l], gelu_ready.at(i, c + 1))
                        last = act.activation(squares(l, c), hid(l)[:, c, :], ACT.Square, accum_out=small(l, SQ, c))
                    last.then_inc(sq_ready[l], 1)
                for l in lanes:
                    turned_norm(i, l, bank[l][2], 3)
                for l in lanes:
                    biased(i, l, bank[l][3], 2, qT, q_done, q_ready, CBQ)
                    biased(i, l, bank[l][0], 2, kT, k_done, k_ready, CBK)
                for l in lanes:
                    act.wait_ge(nmax_ready[l], nmax_ready.at(i))
                    for c in range(2):
                        last = act.activation(prob(l)[:, keys[c]], score(l)[:, keys[c]], ACT.Exp, bias=small(l, NMAX, c), accum_out=small(l, SUM, c))
                    last.then_inc(prob_ready[l], 1)
                for l in lanes:
                    turned_norm(i, l, bank[l][1], 4)
                for l in lanes:
                    act.wait_ge(gap_ready[l], gap_ready.at(i))
                    act.activation(small(l, E12), small(l, D12), ACT.Exp).then_inc(gap_exp[l], 1)
                for e in range(E):
                    for l in lanes:
                        act.wait_ge(gu_done[l], gu_done.at(i, e + 1))
                        if e >= 1:
                            act.wait_ge(gated_ready[l], gated_ready.at(i, e))
                        act.activation(silu(l), bank[l][3][:, 0:KT * T], ACT.Silu).then_inc(silu_ready[l], 1)
                for l in lanes:
                    act.wait_ge(acc_ready[l], acc_ready.at(i))
                    act.dma_start(out[i * LANES + l].rearrange("(c p) d -> p c d", c=2), h[l][:, :, :]).then_inc(stored[l], 16)
            for l in lanes:
                act.wait_ge(stored[l], stored.credit + 16 * PAIRS_OF_IMAGES)

        @block.vector
        def _(dve):
            for l in lanes:
                dve.sem_inc(stored[l], stored.credit)
            for l in lanes:
                dve.memset(kv[l][:, :, :, :, :], 0.0).then_inc(dve_start, 1)

            dve.wait_ge(staged_in, STAGED)
            for t in range(KT):
                for j in range(2):
                    last = dve.tensor_copy(tok_order[:, t, j], tok_feat[:, t, j])
            last.then_inc(ordered, 1)
            dve.tensor_reduce(wsum[:, 0:1], f1_in, AX.XY, ALU.add, apply_absolute_value=True)
            dve.tensor_reduce(wsum[:, 1:2], f2_in, AX.XY, ALU.add, apply_absolute_value=True).then_inc(wsum_ready, 1)
            dve.wait_ge(wsum_all, 1)
            dve.tensor_scalar(wscale[:, :], bank[0][0][:, 0:2], 1.0 / (HID * D), QUANT_EPS, ALU.mult, ALU.max).then_inc(scales_ready, 1)
            dve.wait_ge(scales_ready, 1)
            dve.reciprocal(wrecip[:, :], wscale[:, :]).then_inc(scales_ready, 1)
            dve.wait_ge(scales_ready, 2)
            for n, (src, dst) in enumerate(((f1_in, f1_t[0]), (f2_in, f1_t[1]))):
                dve.tensor_scalar(src, src, wrecip[:, n:n + 1], ROUND, ALU.mult, ALU.add).then_inc(dve_start, 1)
                dve.wait_ge(dve_start, 3 + 2 * n)
                dve.tensor_scalar(src, src, -ROUND, 1.0, ALU.add, ALU.min).then_inc(dve_start, 1)
                dve.wait_ge(dve_start, 4 + 2 * n)
                dve.tensor_scalar(dst[:, :, :], src, -1.0, None, ALU.max).then_inc(ternary, 1)
            group = 0
            for q in range(HALF):
                dve.wait_ge(turned, group + 1)
                dve.tensor_copy(tok_w[:, q, :], bank[1][group % 4][0:XP, 0:D]).then_inc(turned_out, 1)
                group += 1
            for w in (cq_s, ck_s, cv_s):
                dve.wait_ge(turned, group + 1)
                dve.tensor_copy(w[:, :, :], bank[1][group % 4][:, :].rearrange("p (k m) -> p k m", k=KT)).then_inc(turned_out, 1)
                group += 1
            for w, KN in ((f1_s, KT), (f2_s, HT)):
                for kt in range(KN):
                    dve.wait_ge(turned, group + 1)
                    n = w.shape[2]
                    dve.tensor_copy(w[:, kt, :], bank[1][group % 4].bitcast(BF16)[:, 0:n]).then_inc(turned_out, 1)
                    group += 1
            dve.tensor_scalar(proj_s[:, :, :], proj_s[:, :, :], 1.0 / (float(np.sqrt(DH)) * 2 * float(np.pi)), None,
                              ALU.mult).then_inc(scales_ready, 1)
            dve.wait_ge(dve_start, 6)
            dve.wait_ge(turned_out, group)
            dve.wait_ge(weights_in, WEIGHTS)
            dve.wait_ge(pool_start, POOL_START)

            def pass_wait():
                dve.sem_inc(waits_passed, 1)

            def moments(i, l, n, src):
                for c in range(2):
                    last = dve.bn_stats(stats[l][:, c, :], src[:, c, :])
                last.then_inc(bn_done[l], 1)
                dve.wait_ge(bn_done[l], bn_done.at(i, n + 1))
                pass_wait()
                for c in range(2):
                    last = dve.bn_aggr(mv[l][:, c, :], stats[l][:, c, :])
                last.then_inc(mean_ready[l], 1)
                dve.wait_ge(mean_ready[l], mean_ready.at(i, n + 1))
                dve.tensor_scalar(small(l, VE), mv[l][:, :, 1], EPS, None, ALU.add).then_inc(var_ready[l], 1)

            def normalise(i, l, n, dst, src):
                dve.wait_ge(rstd_ready[l], rstd_ready.at(i, n + 1))
                for c in range(2):
                    last = dve.tensor_scalar(dst[:, c, :], src[:, c, :], mv[l][:, c, 0:1], small(l, RSTD, c), ALU.subtract, ALU.mult)
                return last

            def quantise(i, l, k, src, dst, root_ready, root_k, w):
                def step(ins):
                    nonlocal k
                    k += 1
                    ins.then_inc(quant_step[l], 1)
                    dve.wait_ge(quant_step[l], quant_step.at(i, k))

                step(dve.tensor_reduce(small(l, AMAX), src, AX.X, ALU.max, apply_absolute_value=True))
                dve.wait_ge(root_ready[l], root_ready.at(i, root_k))
                if w == 0:
                    step(dve.tensor_tensor(small(l, RR), small(l, RSTD), small(l, R2), ALU.mult))
                step(dve.tensor_tensor(small(l, AMAX), small(l, AMAX), small(l, RR), ALU.mult))
                step(dve.tensor_scalar(small(l, AMAX), small(l, AMAX), QUANT_EPS, None, ALU.max))
                step(dve.reciprocal(small(l, QS), small(l, AMAX)))
                dve.tensor_scalar(small(l, DQ), small(l, AMAX), 1.0 / 127, wscale[0:C, w:w + 1], ALU.mult, ALU.mult)
                step(dve.scalar_tensor_tensor(small(l, QS), small(l, QS), 127.0, small(l, RR), ALU.mult, ALU.mult))
                for c in range(2):
                    last = dve.tensor_scalar(src[:, c, :], src[:, c, :], small(l, QS, c), ROUND, ALU.mult, ALU.add)
                step(last)
                return dve.tensor_scalar(dst, src, -ROUND, 127.0, ALU.add, ALU.min), k

            def to_whole_turns(i, l, u):
                rows, n = (C, 512) if u < PAIRS else (P, KT * T)
                near, _ = frac(l, u)
                dve.wait_ge(phase_done[l], phase_done.at(i, u + 1))
                if u >= 2:
                    dve.wait_ge(feat_ready[l], feat_ready.at(i, u - 1))
                dve.tensor_scalar(near[0:rows, 0:n], bank[l][1 + u % 2][0:rows, 0:n], ROUND, -ROUND, ALU.add, ALU.add).then_inc(turns_ready[l], 1)

            def off_whole_turns(i, l, u):
                rows, n = (C, 512) if u < PAIRS else (P, KT * T)
                near, _ = frac(l, u)
                dve.wait_ge(turns_ready[l], turns_ready.at(i, u + 1))
                dve.tensor_tensor(near[0:rows, 0:n], bank[l][1 + u % 2][0:rows, 0:n], near[0:rows, 0:n], ALU.subtract).then_inc(frac_ready[l], 1)

            def distance(i, l, u):
                rows, n = (C, 512) if u < PAIRS else (P, KT * T)
                near, dist = frac(l, u)
                dve.wait_ge(frac_ready[l], frac_ready.at(i, u + 1))
                dve.tensor_scalar(dist[0:rows, 0:n].bitcast(U32), near[0:rows, 0:n].bitcast(U32), 0x7FFFFFFF, None, ALU.bitwise_and).then_inc(abs_ready[l], 1)

            def route(i, l):
                k = 0

                def step(ins):
                    nonlocal k
                    k += 1
                    ins.then_inc(route_step[l], 1)
                    dve.wait_ge(route_step[l], route_step.at(i, k))

                r = rt[l]
                dve.wait_ge(logit_done[l], logit_done.at(i))
                step(dve.tensor_tensor(r[:, LOGIT], bank[l][2][0:C, 0:2 * E].rearrange("p (c e) -> p c e", c=2), rb_s[:, :, :], ALU.add))
                pass_wait()
                for c in range(2):
                    last = dve.max(r[:, TOP, c, :], r[:, LOGIT, c, :])
                step(last)
                dve.tensor_tensor(small(l, D12), r[:, TOP, :, 1], r[:, TOP, :, 0], ALU.subtract).then_inc(gap_ready[l], 1)
                for c in range(2):
                    last = dve.max_index(rt_i[l][:, c, :], r[:, TOP, c, :], r[:, LOGIT, c, :])
                step(last)
                step(dve.tensor_copy(r[:, IDX], rt_i[l][:, :, :]))
                dve.wait_ge(gap_exp[l], gap_exp.at(i))
                step(dve.tensor_scalar(small(l, W2), small(l, E12), 1.0, None, ALU.add))
                step(dve.reciprocal(small(l, W1), small(l, W2)))
                step(dve.tensor_tensor(small(l, W2), small(l, E12), small(l, W1), ALU.mult))
                for c in range(2):
                    for n, (oh, w) in enumerate(((OH1, W1), (OH2, W2))):
                        last = dve.tensor_scalar(r[:, oh, c, :], expert_no[:, :], r[:, IDX, c, n:n + 1], small(l, w, c), ALU.is_equal, ALU.mult)
                step(last)
                step(dve.tensor_tensor(r[:, WSEL], r[:, OH1], r[:, OH2], ALU.add))

            with dve.Fori(0, PAIRS_OF_IMAGES) as i:
                for l in lanes:
                    dve.wait_ge(tok_done[l], tok_done.at(i))
                    dve.wait_ge(stored[l], stored.before(i))
                    dve.tensor_tensor(h[l][:, :, :], tm(bank[l][0]), both(tok_b_s), ALU.add).then_inc(h_ready[l], 1)
                    dve.wait_ge(h_ready[l], h_ready.at(i, 1))
                    moments(i, l, 0, h[l])
                for l in lanes:
                    normalise(i, l, 0, a[l], h[l]).then_inc(a_ready[l], 1)
                    dve.wait_ge(a_ready[l], a_ready.at(i))
                    for c in range(2):
                        last = dve.tensor_scalar(zn[l][:, c, :], a[l][:, c, :], small(l, R2, c), None, ALU.mult)
                    last.then_inc(zn_ready[l], 1)
                for l in lanes:
                    dve.wait_ge(v_done[l], v_done.at(i, 1))
                    dve.tensor_tensor(v[l][:, :, :], tm(bank[l][0]), both(bv_s), ALU.add).then_inc(v_ready[l], 1)
                for u in range(UNITS):
                    for l in lanes:
                        to_whole_turns(i, l, u)
                    for l in lanes:
                        off_whole_turns(i, l, u)
                    for l in lanes:
                        distance(i, l, u)
                    if u == PAIRS:
                        for l in lanes:
                            dve.wait_ge(kv_done[l], kv_done.at(i))
                            sums = bank[l][3][:, :].rearrange("p (j s g d) -> p j s g d", j=PAIRS, s=2, g=2)
                            for s in range(2):
                                last = dve.tensor_scalar(kv[l][:, :, s, :, s * DH:(s + 1) * DH], sums[:, :, s, :, :], 1.0 / M, None, ALU.mult)
                            last.then_inc(kv_ready[l], 1)
                for l in lanes:
                    dve.wait_ge(wo_done[l], wo_done.at(i))
                    dve.wait_ge(ab_ready[l], ab_ready.at(i))
                    dve.tensor_tensor(a[l][:, :, :], tm(bank[l][3]), a[l][:, :, :], ALU.add).then_inc(x1_ready[l], 1)
                    dve.wait_ge(x1_ready[l], x1_ready.at(i))
                    moments(i, l, 1, a[l])
                for l in lanes:
                    normalise(i, l, 1, zn[l], a[l]).then_inc(zn_ready[l], 1)
                for l in lanes:
                    dve.wait_ge(mlp_done[l], mlp_done.at(i))
                    dve.wait_ge(hx_ready[l], hx_ready.at(i, 1))
                    dve.tensor_tensor(h[l][:, :, :], tm(bank[l][1]), h[l][:, :, :], ALU.add).then_inc(h_ready[l], 1)
                    dve.wait_ge(h_ready[l], h_ready.at(i, 2))
                    moments(i, l, 2, h[l])
                    for c in range(2):
                        last = dve.tensor_scalar(zn[l][:, c, :], h[l][:, c, :], mv[l][:, c, 0:1], None, ALU.subtract)
                    last.then_inc(zn_ready[l], 1)
                steps = 0
                for l in lanes:
                    dve.wait_ge(zn_ready[l], zn_ready.at(i, 3))
                    last, steps = quantise(i, l, 0, zn[l][:, :, :], qin(l), rstd_ready, 3, 0)
                    last.then_inc(qin_ready[l], 1)
                for l in lanes:
                    dve.wait_ge(qinT_done[l], qinT_done.at(i))
                    dve.tensor_copy(qinT(l), bank[l][2].bitcast(BF16)[:, 0:KT * T].rearrange("p (k t) -> p k t", k=KT)).then_inc(qinT_ready[l], 1)
                for l in lanes:
                    for n, b in enumerate((3, 0, 1, 2)):
                        c, half = divmod(n, 2)
                        dve.wait_ge(f1_done[l], f1_done.at(i, n + 1))
                        dve.scalar_tensor_tensor(hid(l)[:, c, half * 512:(half + 1) * 512], bank[l][b][0:C, :], small(l, DQ, c),
                                                 fb1_s[:, half * 512:(half + 1) * 512], ALU.mult, ALU.add).then_inc(pre_ready[l], 1)
                for l in lanes:
                    dve.wait_ge(gelu_ready[l], gelu_ready.at(i))
                    last, total = quantise(i, l, steps, hid(l), qhid(l), rms_ready, 1, 1)
                    last.then_inc(qhid_ready[l], 1)
                assert total == quant_step.per
                for l in lanes:
                    for n, b in enumerate((3, 0)):
                        dve.wait_ge(qhidT_done[l], qhidT_done.at(i, n + 1))
                        dve.tensor_copy(qhidT(l)[:, 4 * n:4 * n + 4, :],
                                        bank[l][b].bitcast(BF16)[:, 0:4 * T].rearrange("p (k t) -> p k t", k=4)).then_inc(qhidT_ready[l], 1)
                for l in lanes:
                    dve.wait_ge(f2_done[l], f2_done.at(i))
                    dve.wait_ge(hx_ready[l], hx_ready.at(i, 2))
                    for c in range(2):
                        last = dve.scalar_tensor_tensor(h[l][:, c, :], tm(bank[l][1])[:, c, :], small(l, DQ, c), h[l][:, c, :], ALU.mult, ALU.add)
                    last.then_inc(h_ready[l], 1)
                    dve.wait_ge(h_ready[l], h_ready.at(i, 3))
                    moments(i, l, 3, h[l])
                for l in lanes:
                    normalise(i, l, 3, zn[l], h[l]).then_inc(zn_ready[l], 1)
                for l in lanes:
                    dve.wait_ge(v_done[l], v_done.at(i, 2))
                    dve.tensor_tensor(v[l][:, :, :], tm(bank[l][1]), both(cbv_s), ALU.add).then_inc(v_ready[l], 1)
                for l in lanes:
                    dve.wait_ge(score_done[l], score_done.at(i))
                    dve.scalar_tensor_tensor(score(l), bank[l][2][0:C, 0:3 * C], SCORE_SCALE, mask[:, :], ALU.mult, ALU.add).then_inc(score_ready[l], 1)
                    dve.wait_ge(score_ready[l], score_ready.at(i))
                    for c in range(2):
                        last = dve.tensor_reduce(small(l, NMAX, c), score(l)[:, keys[c]], AX.X, ALU.max, negate=True)
                    last.then_inc(nmax_ready[l], 1)
                for l in lanes:
                    dve.wait_ge(prob_ready[l], prob_ready.at(i))
                    dve.reciprocal(small(l, RSUM), small(l, SUM)).then_inc(rsum_ready[l], 1)
                    dve.wait_ge(probT_done[l], probT_done.at(i))
                    dve.tensor_copy(probT(l), bank[l][3][0:C, 0:3 * C].rearrange("p (b t) -> p b t", b=3)).then_inc(probT_ready[l], 1)
                for l in lanes:
                    dve.wait_ge(pv_done[l], pv_done.at(i))
                    dve.wait_ge(rsum_ready[l], rsum_ready.at(i))
                    for c in range(2):
                        last = dve.scalar_tensor_tensor(h[l][:, c, :], tm(bank[l][0])[:, c, :], small(l, RSUM, c), h[l][:, c, :], ALU.mult, ALU.add)
                    last.then_inc(h_ready[l], 1)
                    dve.wait_ge(h_ready[l], h_ready.at(i, 4))
                    moments(i, l, 4, h[l])
                for l in lanes:
                    normalise(i, l, 4, zn[l], h[l]).then_inc(zn_ready[l], 1)
                for l in lanes:
                    route(i, l)
                for e in range(E):
                    for l in lanes:
                        dve.wait_ge(silu_ready[l], silu_ready.at(i, e + 1))
                        if e >= 1:
                            dve.wait_ge(down_done[l], down_done.at(i, e))
                        dve.tensor_tensor(gated(l), silu(l).rearrange("p (k t) -> p k t", k=KT), fm(bank[l][0]), ALU.mult).then_inc(gated_ready[l], 1)
                    for l in lanes:
                        dve.wait_ge(down_done[l], down_done.at(i, e + 1))
                        if e >= 1:
                            dve.wait_ge(acc_ready[l], acc_ready.at(i, e))
                        for c in range(2):
                            last = dve.scalar_tensor_tensor(h[l][:, c, :], tm(bank[l][1 + e % 2])[:, c, :], rt[l][:, WSEL, c, e:e + 1], h[l][:, c, :],
                                                            ALU.mult, ALU.add)
                        last.then_inc(acc_ready[l], 1)


_INS = ['x', 'L0_tok_W', 'L0_tok_b', 'L0_attn_proj_mat', 'L0_attn_wq', 'L0_attn_bq', 'L0_attn_wk', 'L0_attn_bk',
        'L0_attn_wv', 'L0_attn_bv', 'L0_attn_wo', 'L0_attn_bo', 'L0_attn_ln1_g', 'L0_attn_ln1_b', 'L0_attn_w1',
        'L0_attn_b1', 'L0_attn_w2', 'L0_attn_b2', 'L0_attn_ln2_g', 'L0_attn_ln2_b', 'L0_ffn_w1', 'L0_ffn_b1',
        'L0_ffn_w2', 'L0_ffn_b2', 'L1_attn_Wq', 'L1_attn_bq', 'L1_attn_Wk', 'L1_attn_bk', 'L1_attn_Wv', 'L1_attn_bv',
        'L1_ffn_router_w', 'L1_ffn_router_b', 'L1_ffn_we_gate', 'L1_ffn_we_up', 'L1_ffn_we_down']
_OUTS = [((64, 196, 256), 'float32')]


def kernel(**inputs):
    import numpy as _np
    import concourse.bacc as _bacc
    from concourse import mybir as _mybir
    from concourse.bass_utils import run_bass_kernel_spmd as _run

    nc = _bacc.Bacc("TRN2", target_bir_lowering=False, num_devices=1)
    arrays, args = {}, []
    for name in _INS:
        a = _np.ascontiguousarray(inputs[name])
        arrays[f"in_{name}_dram"] = a
        args.append(nc.dram_tensor(f"in_{name}_dram", a.shape, _mybir.dt.from_np(a.dtype), kind="ExternalInput").ap())
    for i, (shape, dtype) in enumerate(_OUTS):
        dt = _mybir.dt.from_np(_np.dtype(dtype))
        args.append(nc.dram_tensor(f"out_{i}_dram", shape, dt, kind="ExternalOutput").ap())
    vit_tower(nc, *args)
    r = _run(nc, [arrays], core_ids=[0])
    return r.results[0]["out_0_dram"]
```

```python
from contextlib import ExitStack

import numpy as np

import concourse.bass as bass
from concourse import mybir

ALU = mybir.AluOpType
ACT = mybir.ActivationFunctionType
AX = mybir.AxisListType
F32 = mybir.dt.float32
BF16 = mybir.dt.bfloat16
U32 = mybir.dt.uint32

P = 128
EPS = 1e-5
RMS_EPS = 1e-6
QUANT_EPS = 1e-5
ROUND = 1.5 * 2.0 ** 23
TURN = float(np.nextafter(np.float32(2 * np.pi), np.float32(0)))
NEG = -1e30
TILE_SLOTS = 4
OUT_SLOTS = 4


class Signal:

    def __init__(self, ctx, nc, name, per, credit=0):
        self.sem = ctx.enter_context(nc.semaphore(name))
        self.per = per
        self.credit = per * credit

    def at(self, n, k=None):
        return n * self.per + (self.per if k is None else k) + self.credit


def vit_tower(nc, x, tok_W, tok_b, proj_mat, wq, bq, wk, bk, wv, bv, wo, bo, ln1_g, ln1_b, w1, b1, w2, b2,
              ln2_g, ln2_b, ffn_w1, ffn_b1, ffn_w2, ffn_b2, Wq, cbq, Wk, cbk, Wv, cbv,
              router_w, router_b, we_gate, we_up, we_down, out):
    IMAGES, CH, SIDE, _ = x.shape
    D = tok_W.shape[0]
    PATCH = 16
    GRID = SIDE // PATCH
    T = GRID * GRID
    C = T // 2
    KT = D // P
    DH, M = proj_mat.shape
    HEADS = D // DH
    PAIRS = HEADS // 2
    HID = w1.shape[1]
    HT = HID // P
    E = router_w.shape[1]
    HALF = PATCH // 2
    PR = CH * PATCH
    XP = 2 * PR
    UNITS = 2 * PAIRS
    FEATS = 8
    SCORE_SCALE = 1.0 / float(np.sqrt(D))
    TOKENS = IMAGES * T
    REGION = TOKENS + P
    TILES = -(-(2 * TOKENS // P + E - 1) // TILE_SLOTS) * TILE_SLOTS
    SPARE = (TILES - 2 * TOKENS // P) * P
    IMG_DMA = 16 * CH * 2

    with ExitStack() as ctx:
        def sb(name, shape, dt=F32):
            return ctx.enter_context(nc.sbuf_tensor(name, shape, dt))

        def sem(name):
            return ctx.enter_context(nc.semaphore(name))

        def signal(name, per, credit=0):
            return Signal(ctx, nc, name, per, credit)

        rows = nc.dram_tensor("expert_rows", (E * REGION + SPARE, D), F32, kind="Internal").ap()
        results = nc.dram_tensor("expert_results", (TILES * P, D), F32, kind="Internal").ap()
        resid = nc.dram_tensor("residual", (IMAGES, T, D), F32, kind="Internal").ap()

        tok_w = sb("tok_w", [XP, HALF, D])
        wq_s, wk_s, wv_s, wo_s = (sb(n, [P, KT, D]) for n in ("wq_s", "wk_s", "wv_s", "wo_s"))
        w1_s = sb("w1_s", [P, KT, HID])
        w2_s = sb("w2_s", [P, HT, D])
        f1_s = sb("f1_s", [P, KT, HID], BF16)
        f2_s = sb("f2_s", [P, HT, D], BF16)
        cq_s, ck_s, cv_s = (sb(n, [P, KT, D]) for n in ("cq_s", "ck_s", "cv_s"))
        router_s = sb("router_s", [P, KT, E])
        proj_s = sb("proj_s", [P, P // DH, M])
        cols = sb("cols", [P, 8, KT])
        b1_col = sb("b1_col", [P, HT])
        tok_b_s, bv_s, bo_s, b2_s, fb2_s, cbv_s = (
            sb(n, [C, D]) for n in ("tok_b_s", "bv_s", "bo_s", "b2_s", "fb2_s", "cbv_s"))
        fb1_s = sb("fb1_s", [C, HID])
        rb_s = sb("rb_s", [C, 2, E])
        mask = sb("mask", [C, 3 * C])
        ident = sb("ident", [P, P])
        ident_b = sb("ident_b", [P, P], BF16)
        ones = sb("ones", [P, P])
        earlier = sb("earlier", [P, P])
        expert_no = sb("expert_no", [C, E])
        half_pi = sb("half_pi", [P, 1])
        pair_of = {n: sb(name, [C, 2]) for n, name in
                   ((-0.5, "minus_half"), (EPS, "eps_pair"), (RMS_EPS, "rms_eps_pair"), (1.0 / HID, "hid_share"))}
        wsum = sb("wsum", [P, 2])
        wscale = sb("wscale", [P, 2])
        wrecip = sb("wrecip", [P, 2])
        base = sb("base", [P, E])
        region0 = sb("region0", [P, E])
        place = sb("place", [C, IMAGES, 4])
        weigh = sb("weigh", [C, IMAGES, 4])

        PATCHES, ARENA_F, ARENA_B = GRID * SIDE, (FEATS + 2) * 1024, 4096
        work = sb("work", [P, 2 * PATCHES + ARENA_F + ARENA_B])
        patches = [work[:, p * PATCHES:(p + 1) * PATCHES] for p in range(2)]
        arena_f = work[:, 2 * PATCHES:2 * PATCHES + ARENA_F]
        arena_b = work[:, 2 * PATCHES + ARENA_F:2 * PATCHES + ARENA_F + ARENA_B]
        h, a, xs = ([sb(f"{n}{p}", [C, 2, D]) for p in range(2)] for n in ("h", "a", "xs"))
        zn_f, zn_b, v_b = (sb(n, [C, 2, D]) for n in ("zn_f", "zn_b", "v_b"))
        xT_f, qT_f, kT_f, xT_b, qT_b, kT_b = (sb(n, [P, KT, T]) for n in ("xT_f", "qT_f", "kT_f", "xT_b", "qT_b", "kT_b"))
        v_f = sb("v_f", [C, 2, HEADS, 2 * DH])
        kvT = sb("kvT", [P, PAIRS, M])
        kv = sb("kv", [P, PAIRS, 4 * 2 * DH])
        stats_f, stats_b = (sb(n, [C, 2, 6]) for n in ("stats_f", "stats_b"))
        mv_f, mv_b = (sb(n, [C, 2, 2]) for n in ("mv_f", "mv_b"))
        sm_f, sm_b = (sb(n, [C, 16, 2]) for n in ("sm_f", "sm_b"))
        rt = sb("rt", [C, 9, 2, E])
        rt_i = sb("rt_i", [C, 2, E], U32)
        pos_f = sb("pos_f", [C, 4])
        pos = [sb(f"pos{p}", [C, 4], U32) for p in range(2)]
        fb = [ctx.enter_context(nc.psum_tensor(f"front_bank{b}", [P, 512], F32)) for b in range(4)]
        bb = [ctx.enter_context(nc.psum_tensor(f"back_bank{b}", [P, 512], F32)) for b in range(4)]

        VE, RSTD, R2, TMP, AMAX, DQ, RR, SUM, NMAX, RSUM, QS, D12, E12, W1, W2, SQ = range(16)
        LOGIT, TOP, IDX, OH1, OH2, CNT, POS, PICK1, PICK2 = range(9)
        G1, B1, G2, B2, BQ, BK, CBQ, CBK = range(8)

        def col(n, t):
            return cols[:, n, t:t + 1]

        def of(sm, n, c=None):
            return sm[:, n, :] if c is None else sm[:, n, c:c + 1]

        def tm(b):
            return b[0:C, :].rearrange("p (c d) -> p c d", c=2)

        def fm(b):
            return b[:, 0:KT * T].rearrange("p (k t) -> p k t", k=KT)

        def fm16(b, k):
            return b[:, :].bitcast(BF16)[:, 0:k * T].rearrange("p (k t) -> p k t", k=k)

        def chunk(c):
            return slice(c * C, (c + 1) * C)

        keys = (slice(0, C), slice(C, 3 * C))

        def both(bias):
            return bias[:, :].unsqueeze(1).broadcast_to([C, 2, D])

        def feat(u):
            s = (u % FEATS) * 1024
            return arena_f[:, s:s + 1024].rearrange("p (f n) -> p f n", f=2)

        def near(u):
            s = (FEATS + u % 2) * 1024
            return arena_f[:, s:s + 512]

        def dist(u):
            s = (FEATS + u % 2) * 1024 + 512
            return arena_f[:, s:s + 512]

        def extent(u):
            return (C, 512) if u < PAIRS else (P, KT * T)

        def rounds_on_act(u):
            return u % 2 == 1

        hidT = arena_b[:, 0:HT * T].rearrange("p (m t) -> p m t", m=HT)
        hid = arena_b[0:C, 0:2 * HID].rearrange("p (c n) -> p c n", c=2)
        squares = [arena_b[0:C, (2 + c) * HID:(3 + c) * HID] for c in range(2)]
        qhid = arena_b[0:C, 2 * HID:3 * HID].bitcast(BF16).rearrange("p (c n) -> p c n", c=2)
        qhidT = arena_b[:, 3 * HID:3 * HID + HT * T // 2].bitcast(BF16).rearrange("p (m t) -> p m t", m=HT)
        qin = [a[p][:, 0, :].bitcast(BF16).rearrange("p (c d) -> p c d", c=2) for p in range(2)]
        qinT = xT_b[:, 0, :].bitcast(BF16).rearrange("p (k t) -> p k t", k=KT)
        score = arena_b[0:C, 0:3 * C]
        prob = arena_b[0:C, 512:512 + 3 * C]
        probT = arena_b[0:C, 1024:1024 + 3 * C].rearrange("p (b t) -> p b t", b=3)

        f1_in = arena_f[:, 0:2048].rearrange("p (t d) -> p t d", t=HT)
        f2_in = arena_f[:, 2048:4096].rearrange("p (t n) -> p t n", t=KT)
        f1_q = arena_f[:, 4096:5120].bitcast(BF16).rearrange("p (t d) -> p t d", t=HT)
        f2_q = arena_f[:, 5120:6144].bitcast(BF16).rearrange("p (t n) -> p t n", t=KT)
        tok_in = arena_f[:, 6144:6144 + KT * CH * PATCH * PATCH].rearrange("p (t f) -> p t f", t=KT)
        tok_order = arena_f[:, 7680:7680 + KT * HALF * XP]
        c_in = [arena_b[:, 512 * n:512 * (n + 1)].rearrange("p (t d) -> p t d", t=KT) for n in range(3)]
        tok_feat = tok_in.rearrange("m t (p j q c) -> m t j q c p", p=PATCH, j=2, c=CH)
        tok_by_part = tok_order.rearrange("m (t q j c p) -> m t j q c p", t=KT, q=HALF, j=2, c=CH)

        GU = E * KT * 2 * D
        gu_s = work[:, 0:GU].rearrange("p (e k n) -> p (e k) n", e=E, k=KT)
        down_s = work[:, GU:GU + E * KT * D].rearrange("p (e n) -> p e n", e=E)
        tiles = work[:, GU + E * KT * D:]
        assert tiles.shape[1] >= (TILE_SLOTS + 10) * D
        tile_in = [tiles[:, n * D:(n + 1) * D] for n in range(TILE_SLOTS)]
        tile_xT, tile_silu, tile_act, tile_actT, tile_y = (
            [tiles[:, (TILE_SLOTS + 2 * k + n) * D:(TILE_SLOTS + 2 * k + n + 1) * D] for n in range(2)] for k in range(5))
        TAB = sb("TAB", [1, 4, TILES])
        tab_i = sb("tab_i", [1, 2, TILES], U32)
        few = sb("few", [P, 4, E])
        later, found = (sb(n, [C, IMAGES, 4]) for n in ("later", "found"))
        found_i = sb("found_i", [C, IMAGES, 4], U32)
        pad_row = sb("pad_row", [P, E])
        pad_idx = sb("pad_idx", [P, E], U32)
        part_no = sb("part_no", [P, 1])
        blank = sb("blank", [P, D])
        IMG = 2 * D
        out_y1, out_y2, out_h = (
            [work[0:C, (3 * n + k) * IMG:(3 * n + k + 1) * IMG] for n in range(OUT_SLOTS)] for k in range(3))

        names = ("weights_in staged_in proj_clear consts pool_start dve_start wsum_ready wsum_all ternary ordered "
                 "turned turned_out scales_ready waits_passed pool_passed experts_in blank_done rows_clear pad_ready pads_in "
                 "table_step table_ready").split()
        S = {n: sem(n) for n in names}

        patches_in = [sem(f"patches_in{p}") for p in range(2)]
        stored = [sem(f"stored{p}") for p in range(2)]
        scattered = [sem(f"scattered{p}") for p in range(2)]
        rows_gone = signal("rows_gone", 1, credit=2)
        patches_used = signal("patches_used", 1, credit=2)
        tok_done = signal("tok_done", 1)
        h_ready = signal("h_ready", 1)
        bn_f, mean_f, var_f, rstd_f = (signal(n, 2) for n in ("bn_f", "mean_f", "var_f", "rstd_f"))
        bn_b, mean_b, var_b, rstd_b = (signal(n, 3) for n in ("bn_b", "mean_b", "var_b", "rstd_b"))
        pool_f = signal("pool_f", 5)
        pool_b = signal("pool_b", 6)
        a_ready = signal("a_ready", 1)
        ab_ready = signal("ab_ready", 1)
        znf_ready = signal("znf_ready", 1)
        xTf_done, xTf_ready = signal("xTf_done", 1), signal("xTf_ready", 1)
        qf_done, kf_done, vf_done = (signal(n, 1) for n in ("qf_done", "kf_done", "vf_done"))
        qf_ready, kf_ready, vf_ready = (signal(n, 1) for n in ("qf_ready", "kf_ready", "vf_ready"))
        phase_done = signal("phase_done", UNITS)
        turns_ready = signal("turns_ready", UNITS // 2)
        whole_ready = signal("whole_ready", UNITS // 2)
        near_ready = signal("near_ready", UNITS)
        dist_ready = signal("dist_ready", UNITS)
        feat_ready = signal("feat_ready", UNITS)
        feat_used = signal("feat_used", UNITS, credit=0)
        kvT_done, kvT_ready, kv_done, kv_ready = (signal(n, 2) for n in ("kvT_done", "kvT_ready", "kv_done", "kv_ready"))
        att_done, att_ready, wo_done, x1_ready, hx_ready = (signal(n, 1) for n in ("att_done", "att_ready", "wo_done", "x1_ready", "hx_ready"))
        zn2_ready = signal("zn2_ready", 1)
        xTb_done, xTb_ready = signal("xTb_done", 3), signal("xTb_ready", 3)
        up_done, relu_ready = signal("up_done", 4), signal("relu_ready", 4)
        mlp_done, h1_ready, z3_ready, hb_ready = (signal(n, 1) for n in ("mlp_done", "h1_ready", "z3_ready", "hb_ready"))
        quant_step = signal("quant_step", 13)
        rms_ready, qin_ready, qinT_done, qinT_ready = (signal(n, 1) for n in ("rms_ready", "qin_ready", "qinT_done", "qinT_ready"))
        f1_done, pre_ready, gelu_ready = signal("f1_done", 4), signal("pre_ready", 4), signal("gelu_ready", 2)
        sq_ready, qhid_ready, f2_done, h2_ready, z4_ready = (signal(n, 1) for n in ("sq_ready", "qhid_ready", "f2_done", "h2_ready", "z4_ready"))
        qhidT_done, qhidT_ready = signal("qhidT_done", 2), signal("qhidT_ready", 2)
        qb_done, kb_done, vb_done = (signal(n, 1) for n in ("qb_done", "kb_done", "vb_done"))
        qb_ready, kb_ready, vb_ready = (signal(n, 1) for n in ("qb_ready", "kb_ready", "vb_ready"))
        score_done, score_ready, nmax_ready, prob_ready, probT_done, probT_ready, rsum_ready, pv_done, h3_ready, z5_ready = (
            signal(n, 1) for n in ("score_done", "score_ready", "nmax_ready", "prob_ready", "probT_done", "probT_ready",
                                   "rsum_ready", "pv_done", "h3_ready", "z5_ready"))
        logit_done, gap_ready, gap_exp, count_ready, prefix_done, pos_ready = (
            signal(n, 1) for n in ("logit_done", "gap_ready", "gap_exp", "count_ready", "prefix_done", "pos_ready"))
        route_step = signal("route_step", 11)
        base_ready = signal("base_ready", 1, credit=1)
        picked, placed = (signal(n, 1) for n in ("picked", "placed"))

        tile_here = [sem(f"tile_here{n}") for n in range(TILE_SLOTS)]
        tile_stored = [sem(f"tile_stored{n}") for n in range(2)]
        tx_done, tx_ready, gu_done, silu_ready, act_ready, ta_done, ta_ready, dn_done, y_ready = (
            signal(n, 1) for n in ("tx_done", "tx_ready", "gu_done", "silu_ready", "act_ready", "ta_done", "ta_ready", "dn_done", "y_ready"))
        idx_set = [signal(f"idx_set{n}", 1) for n in range(OUT_SLOTS)]
        rows_here = [sem(f"rows_here{n}") for n in range(OUT_SLOTS)]
        resid_here = [sem(f"resid_here{n}") for n in range(OUT_SLOTS)]
        out_stored = [sem(f"out_stored{n}") for n in range(OUT_SLOTS)]
        sum_step = signal("sum_step", 1)
        sum_ready = signal("sum_ready", 1)
        idx_o = [sb(f"idx_o{n}", [C, 4], U32) for n in range(OUT_SLOTS)]

        POOL_START = 14
        WEIGHTS = 16 * (7 + 8 + 1 + 7 + 2)
        STAGED = 16 * (2 + 1 + 3 + P // DH)
        EXPERTS = 16 * 3 * E

        SLOTS = 20
        QIN_TURN, F1, GELU, QHID, QHID_TURN, F2, LN4, TURN4, PROJ, SCORE, SOFTMAX, PROB_TURN, PV, LN5, TURN5, LOGITS, PREFIX = (
            0, 1, 2, 3, 5, 6, 7, 8, 9, 10, 11, 13, 14, 15, 16, 17, 19)
        KV_TURN = {7: 0, 10: 1}
        ATTEND_Q = {13: 0, 18: 1}

        def steps(eng, step):
            step((0, 0), None)
            with eng.Fori(0, IMAGES - 3, 2) as i:
                step((i + 1, 1), (i, 0))
                step((i + 2, 0), (i + 1, 1))
            step((IMAGES - 1, 1), (IMAGES - 2, 0))
            step(None, (IMAGES - 1, 1))

        def of_parity(n, p):
            return n * 8 + 16 - 8 * p

        block = ctx.enter_context(nc.Block())

        @block.sync
        def _(sp):
            sp.dma_start(f1_in, ffn_w1.rearrange("(t p) d -> p t d", p=P)).then_inc(S["staged_in"], 16)
            sp.dma_start(f2_in, ffn_w2.rearrange("(t p) n -> p t n", p=P)).then_inc(S["staged_in"], 16)
            sp.dma_start(tok_in, tok_W.rearrange("(t p) f -> p t f", p=P)).then_inc(S["staged_in"], 16)
            for stage, w in zip(c_in, (Wq, Wk, Wv)):
                sp.dma_start(stage, w.rearrange("(t p) d -> p t d", p=P)).then_inc(S["staged_in"], 16)
            sp.wait_ge(S["proj_clear"], 1)
            for r in range(P // DH):
                sp.dma_start(proj_s[DH * r:DH * (r + 1), r, :], proj_mat).then_inc(S["staged_in"], 16)

            def load_image(n, p):
                sp.wait_ge(patches_used.sem, n * patches_used.per + 1)
                for half in range(2):
                    for c in range(CH):
                        q0 = half * HALF
                        sp.dma_start(
                            patches[p][half * PR + c * PATCH:half * PR + (c + 1) * PATCH, :]
                            .rearrange("p (g w) -> p g w", g=GRID)[:, :, 0:SIDE - q0],
                            x[n, c].rearrange("(g p) w -> p g w", p=PATCH)[:, :, q0:SIDE],
                        ).then_inc(patches_in[p], 16)

            load_image(0, 0)
            for dst, src in ((wq_s, wq), (wk_s, wk), (wv_s, wv), (wo_s, wo), (w1_s, w1), (w2_s, w2), (router_s, router_w)):
                sp.dma_start(dst[:, :, :], src.rearrange("(t p) n -> p t n", p=P)).then_inc(S["weights_in"], 16)
            for n, src in ((G1, ln1_g), (B1, ln1_b), (G2, ln2_g), (B2, ln2_b), (BQ, bq), (BK, bk), (CBQ, cbq), (CBK, cbk)):
                sp.dma_start(cols[:, n, :], src.rearrange("(t p) -> p t", p=P), allow_slow_non_contiguous=True).then_inc(S["weights_in"], 16)
            sp.dma_start(b1_col[:, :], b1.rearrange("(t p) -> p t", p=P), allow_slow_non_contiguous=True).then_inc(S["weights_in"], 16)
            for dst, src in ((tok_b_s, tok_b), (bv_s, bv), (bo_s, bo), (b2_s, b2), (fb2_s, ffn_b2), (cbv_s, cbv), (fb1_s, ffn_b1)):
                sp.dma_start(dst[:, :], src.rearrange("(o n) -> o n", o=1).broadcast_to([C, src.shape[0]])).then_inc(S["weights_in"], 16)
            for c in range(2):
                sp.dma_start(rb_s[:, c, :], router_b.rearrange("(o n) -> o n", o=1).broadcast_to([C, E])).then_inc(S["weights_in"], 16)
            sp.wait_ge(S["blank_done"], 1)
            for r in range(SPARE // P):
                sp.dma_start(rows[E * REGION + r * P:E * REGION + (r + 1) * P, :], blank[:, :]).then_inc(S["rows_clear"], 16)

            def store_resid(n, p):
                sp.wait_ge(h3_ready.sem, h3_ready.at(n))
                sp.dma_start(resid[n].rearrange("(c p) d -> p c d", c=2), h[p][:, :, :]).then_inc(stored[p], 16)
                sp.wait_ge(scattered[p], 4 * of_parity(n, p))
                sp.sem_inc(rows_gone.sem, 1)

            load_image(1, 1)
            with sp.Fori(0, IMAGES - 3, 2) as i:
                load_image(i + 2, 0)
                store_resid(i, 0)
                load_image(i + 3, 1)
                store_resid(i + 1, 1)
            store_resid(IMAGES - 2, 0)
            store_resid(IMAGES - 1, 1)

            sp.wait_ge(pos_ready.sem, pos_ready.at(IMAGES - 1))
            for e in range(E):
                for n, w in enumerate((we_gate, we_up)):
                    sp.dma_start(gu_s[:, e * KT:(e + 1) * KT, n * D:(n + 1) * D], w[e].rearrange("(t p) n -> p t n", p=P)).then_inc(S["experts_in"], 16)
                sp.dma_start(down_s[:, e, :].rearrange("p (t n) -> p t n", t=KT), we_down[e].rearrange("(t p) n -> p t n", p=P)).then_inc(S["experts_in"], 16)
            sp.wait_ge(S["table_ready"], 1)
            sp.wait_ge(S["pads_in"], 16 * E)
            sp.wait_ge(S["rows_clear"], SPARE // P * 16)
            for p in range(2):
                sp.wait_ge(scattered[p], 4 * 16 * IMAGES // 2)
                sp.wait_ge(stored[p], 16 * IMAGES // 2 + 16)

            def first_row(t):
                return sp.value_load(tab_i[0:1, 1, bass.ds(t, 1)], min_val=0, max_val=E * REGION + SPARE - P)

            def load_tile(t, slot):
                r = first_row(t)
                sp.dma_start(tile_in[slot], rows[bass.ds(r, P), :]).then_inc(tile_here[slot], 16)

            def store_tile(t, q):
                sp.wait_ge(y_ready.sem, y_ready.at(t))
                sp.dma_start(results[bass.ds(t * P, P), :], tile_y[q]).then_inc(tile_stored[q], 16)

            for t in range(TILE_SLOTS):
                load_tile(t, t)
            with sp.Fori(0, TILES - 2 * TILE_SLOTS + 1, TILE_SLOTS) as t:
                for k in range(TILE_SLOTS):
                    store_tile(t + k, k % 2)
                    load_tile(t + k + TILE_SLOTS, k)
            for k in range(TILE_SLOTS):
                store_tile(TILES - TILE_SLOTS + k, k % 2)
            for q in range(2):
                sp.wait_ge(tile_stored[q], 16 * (TILES // 2) + 16)

            def load_resid(j, n):
                sp.dma_start(out_h[n].rearrange("p (c d) -> p c d", c=2), resid[j].rearrange("(c p) d -> p c d", c=2)).then_inc(resid_here[n], 16)

            def store_out(j, n):
                sp.wait_ge(sum_ready.sem, sum_ready.at(j))
                sp.dma_start(out[j].rearrange("(c p) d -> p c d", c=2), out_h[n].rearrange("p (c d) -> p c d", c=2)).then_inc(out_stored[n], 16)

            for n in range(OUT_SLOTS):
                load_resid(n, n)
            with sp.Fori(0, IMAGES - 2 * OUT_SLOTS + 1, OUT_SLOTS) as j:
                for n in range(OUT_SLOTS):
                    store_out(j + n, n)
                for n in range(OUT_SLOTS):
                    sp.wait_ge(out_stored[n], j * (16 // OUT_SLOTS) + 16)
                    load_resid(j + OUT_SLOTS + n, n)
            for n in range(OUT_SLOTS):
                store_out(IMAGES - OUT_SLOTS + n, n)
            for n in range(OUT_SLOTS):
                sp.wait_ge(out_stored[n], 16 * IMAGES // OUT_SLOTS)

        @block.tensor
        def _(pe):
            pe.drain().then_inc(patches_used.sem, patches_used.credit)
            pe.wait_ge(S["consts"], 1)
            pe.wait_ge(S["wsum_ready"], 1)
            pe.matmul(fb[0][:, 0:2], ones[:, :], wsum[:, :], start=True, stop=True).then_inc(S["wsum_all"], 1)
            pe.wait_ge(S["ordered"], 1)
            group = 0
            for q in range(HALF):
                if group >= 4:
                    pe.wait_ge(S["turned_out"], group - 3)
                for t in range(KT):
                    last = pe.transpose(bb[group % 4][0:XP, t * P:(t + 1) * P], tok_order[:, (t * HALF + q) * XP:(t * HALF + q + 1) * XP], ident[:, :])
                last.then_inc(S["turned"], 1)
                group += 1
            for n in range(3):
                pe.wait_ge(S["turned_out"], group - 3)
                for kt in range(KT):
                    for t in range(KT):
                        last = pe.transpose(bb[group % 4][:, kt * D + t * P:kt * D + (t + 1) * P], c_in[n][:, t, kt * P:(kt + 1) * P], ident[:, :])
                last.then_inc(S["turned"], 1)
                group += 1
            for n, (src, KN, ON) in enumerate(((f1_q, KT, HT), (f2_q, HT, KT))):
                pe.wait_ge(S["ternary"], n + 1)
                for kt in range(KN):
                    pe.wait_ge(S["turned_out"], group - 3)
                    for t in range(ON):
                        last = pe.transpose(bb[group % 4][:, :].bitcast(BF16)[:, t * P:(t + 1) * P], src[:, t, kt * P:(kt + 1) * P], ident_b[:, :])
                    last.then_inc(S["turned"], 1)
                    group += 1
            pe.wait_ge(S["turned_out"], group)
            pe.wait_ge(S["weights_in"], WEIGHTS)
            pe.wait_ge(S["scales_ready"], 3)

            def turn(dst, src):
                for kt in range(KT):
                    for c in range(2):
                        last = pe.transpose(dst[:, kt, chunk(c)], src[:, c, kt * P:(kt + 1) * P], ident[0:C, 0:C])
                return last

            def by_feature(dst, w, src, nk=KT):
                for m in range(dst.shape[1]):
                    for kt in range(nk):
                        last = pe.matmul(dst[:, m, :], w[:, kt, m * P:(m + 1) * P], src[:, kt, :], start=(kt == 0), stop=(kt == nk - 1))
                return last

            def by_token(dst, src, w, nk=KT):
                for c in range(2):
                    for kt in range(nk):
                        last = pe.matmul(dst[:, c, :], src[:, kt, chunk(c)], w[:, kt, :], start=(kt == 0), stop=(kt == nk - 1))
                return last

            def embed(n, p):
                pe.wait_ge(patches_in[p], n * (IMG_DMA // 2) + IMG_DMA - p * (IMG_DMA // 2))
                pix = patches[p][0:XP, :].rearrange("p (t q) -> p t q", q=PATCH)
                for c in range(2):
                    for q in range(HALF):
                        last = pe.matmul(tm(fb[2])[:, c, :], pix[:, chunk(c), q], tok_w[:, q, :], start=(q == 0), stop=(q == HALF - 1))
                last.then_inc(tok_done.sem, 1)
                pe.drain().then_inc(patches_used.sem, 1)

            def phases(n, u):
                if u >= 2:
                    pe.wait_ge(near_ready.sem, near_ready.at(n, u - 1))
                pair = u % PAIRS
                kt, r = divmod(pair, 4)
                if u == 0:
                    pe.wait_ge(kf_ready.sem, kf_ready.at(n))
                if u == 1:
                    pe.wait_ge(qf_ready.sem, qf_ready.at(n))
                b = fb[1 + u % 2]
                for s in range(2):
                    if u < PAIRS:
                        last = pe.matmul(tm(b)[:, s, :], kT_f[:, kt, chunk(s)], proj_s[:, 2 * r:2 * r + 2, :].rearrange("p s m -> p (s m)"),
                                         start=True, stop=True)
                    else:
                        last = pe.matmul(fm(b)[:, s, :], proj_s[:, 2 * r + s, :], qT_f[:, kt, :], start=True, stop=True)
                last.then_inc(phase_done.sem, 1)

            def attend_k(n, u):
                pe.wait_ge(feat_ready.sem, feat_ready.at(n, u + 1))
                if u == 0:
                    pe.wait_ge(vf_ready.sem, vf_ready.at(n))
                b = fb[3] if u < PAIRS // 2 else fb[0]
                f = feat(u)[0:C].rearrange("p f (c s m) -> p f c s m", c=2, s=2)
                for c in range(2):
                    for s in range(2):
                        for g in range(2):
                            at = 32 * (2 * s + g)
                            last = pe.matmul(b[at:at + 32, (u % 4) * M:(u % 4 + 1) * M], v_f[:, c, 2 * u + s, :], f[:, g, c, s, :],
                                             start=(c == 0), stop=(c == 1))
                last.then_inc(feat_used.sem, 1)
                if u % 4 == 3:
                    pe.drain().then_inc(kvT_done.sem, 1)

            def turn_kv(n, half):
                pe.wait_ge(kvT_ready.sem, kvT_ready.at(n, half + 1))
                b = (fb[3], fb[0])[half]
                for j in range(4):
                    last = pe.transpose(b[:, j * P:(j + 1) * P], kvT[:, 4 * half + j, :], ident[:, :])
                last.then_inc(kv_done.sem, 1)

            def attend_q(n, half):
                if half == 0:
                    pe.wait_ge(kv_ready.sem, kv_ready.at(n))
                u0 = PAIRS + 4 * half
                pe.wait_ge(feat_ready.sem, feat_ready.at(n, u0 + 4))
                for k in range(4):
                    s, g = divmod(k, 2)
                    for r in range(4):
                        f = feat(u0 + r)[:, :, 0:KT * T].rearrange("p f (s t) -> p f s t", s=2)
                        last = pe.matmul(fm(fb[3])[32 * r:32 * r + 32, half, :], kv[:, 4 * half + r, k * 32:(k + 1) * 32], f[:, g, s, :],
                                         start=(k == 0), stop=(k == 3))
                last.then_inc(feat_used.sem, 4)
                if half == 1:
                    pe.drain().then_inc(att_done.sem, 1)

            def back(n, p, s):
                if s == QIN_TURN:
                    pe.wait_ge(qin_ready.sem, qin_ready.at(n))
                    for kt in range(KT):
                        for c in range(2):
                            last = pe.transpose(fm16(bb[2], KT)[:, kt, chunk(c)], qin[p][:, c, kt * P:(kt + 1) * P], ident_b[0:C, 0:C])
                    last.then_inc(qinT_done.sem, 1)
                elif s == F1:
                    pe.wait_ge(qinT_ready.sem, qinT_ready.at(n))
                    for k, b in enumerate((3, 0, 1, 2)):
                        c, half = divmod(k, 2)
                        for kt in range(KT):
                            last = pe.matmul(bb[b][0:C, :], qinT[:, kt, chunk(c)], f1_s[:, kt, half * 512:(half + 1) * 512], start=(kt == 0), stop=(kt == KT - 1))
                        last.then_inc(f1_done.sem, 1)
                elif s == QHID_TURN:
                    pe.wait_ge(qhid_ready.sem, qhid_ready.at(n))
                    for k, b in enumerate((3, 0)):
                        for kt in range(4):
                            for c in range(2):
                                last = pe.transpose(fm16(bb[b], 4)[:, kt, chunk(c)], qhid[:, c, (4 * k + kt) * P:(4 * k + kt + 1) * P], ident_b[0:C, 0:C])
                        last.then_inc(qhidT_done.sem, 1)
                elif s == F2:
                    pe.wait_ge(qhidT_ready.sem, qhidT_ready.at(n))
                    by_token(tm(bb[1]), qhidT, f2_s, HT).then_inc(f2_done.sem, 1)
                elif s == TURN4:
                    pe.wait_ge(z4_ready.sem, z4_ready.at(n))
                    turn(fm(bb[2]), zn_b).then_inc(xTb_done.sem, 1)
                elif s == PROJ:
                    pe.wait_ge(xTb_ready.sem, xTb_ready.at(n, 2))
                    by_feature(fm(bb[3]), cq_s, xT_b).then_inc(qb_done.sem, 1)
                    by_feature(fm(bb[0]), ck_s, xT_b).then_inc(kb_done.sem, 1)
                    by_token(tm(bb[1]), xT_b, cv_s).then_inc(vb_done.sem, 1)
                elif s == SCORE:
                    pe.wait_ge(qb_ready.sem, qb_ready.at(n))
                    pe.wait_ge(kb_ready.sem, kb_ready.at(n))
                    for c in range(2):
                        for kt in range(KT):
                            last = pe.matmul(bb[2][0:C, keys[c]], qT_b[:, kt, chunk(c)], kT_b[:, kt, 0:(c + 1) * C], start=(kt == 0), stop=(kt == KT - 1))
                    last.then_inc(score_done.sem, 1)
                elif s == PROB_TURN:
                    pe.wait_ge(prob_ready.sem, prob_ready.at(n))
                    for k in range(3):
                        last = pe.transpose(bb[3][0:C, k * C:(k + 1) * C], prob[:, k * C:(k + 1) * C], ident[0:C, 0:C])
                    last.then_inc(probT_done.sem, 1)
                elif s == PV:
                    pe.wait_ge(probT_ready.sem, probT_ready.at(n))
                    pe.wait_ge(vb_ready.sem, vb_ready.at(n))
                    pe.matmul(tm(bb[0])[:, 0, :], probT[:, 0, :], v_b[:, 0, :], start=True, stop=True)
                    for c in range(2):
                        last = pe.matmul(tm(bb[0])[:, 1, :], probT[:, 1 + c, :], v_b[:, c, :], start=(c == 0), stop=(c == 1))
                    last.then_inc(pv_done.sem, 1)
                elif s == TURN5:
                    pe.wait_ge(z5_ready.sem, z5_ready.at(n))
                    turn(fm(bb[1]), xs[p]).then_inc(xTb_done.sem, 1)
                elif s == LOGITS:
                    pe.wait_ge(xTb_ready.sem, xTb_ready.at(n, 3))
                    for c in range(2):
                        for kt in range(KT):
                            last = pe.matmul(bb[2][0:C, c * E:(c + 1) * E], xT_b[:, kt, chunk(c)], router_s[:, kt, :], start=(kt == 0), stop=(kt == KT - 1))
                    last.then_inc(logit_done.sem, 1)
                elif s == PREFIX:
                    pe.wait_ge(count_ready.sem, count_ready.at(n))
                    pe.matmul(bb[3][0:C, 0:E], earlier[0:C, 0:C], rt[:, CNT, 0, :], start=True, stop=True)
                    pe.matmul(bb[3][0:C, E:2 * E], earlier[0:C, 0:C], rt[:, CNT, 1, :], start=True, stop=False)
                    pe.matmul(bb[3][0:C, E:2 * E], ones[0:C, 0:C], rt[:, CNT, 0, :], start=False, stop=True)
                    pe.matmul(bb[2][:, 0:E], ones[0:C, :], rt[:, CNT, 0, :], start=True, stop=False)
                    pe.matmul(bb[2][:, 0:E], ones[0:C, :], rt[:, CNT, 1, :], start=False, stop=True).then_inc(prefix_done.sem, 1)

            def step(f, b):
                if f:
                    embed(*f)
                if b:
                    pe.wait_ge(zn2_ready.sem, zn2_ready.at(b[0]))
                    turn(fm(bb[0]), zn_b).then_inc(xTb_done.sem, 1)
                    pe.wait_ge(xTb_ready.sem, xTb_ready.at(b[0], 1))
                    for k, bank in enumerate((1, 2, 3, 0)):
                        by_feature(fm(bb[bank]), w1_s[:, :, k * 2 * P:(k + 1) * 2 * P], xT_b).then_inc(up_done.sem, 1)
                if f:
                    pe.wait_ge(znf_ready.sem, znf_ready.at(f[0]))
                    turn(fm(fb[1]), zn_f).then_inc(xTf_done.sem, 1)
                if b:
                    pe.wait_ge(relu_ready.sem, relu_ready.at(b[0]))
                    by_token(tm(bb[1]), hidT, w2_s, HT).then_inc(mlp_done.sem, 1)
                if f:
                    pe.wait_ge(xTf_ready.sem, xTf_ready.at(f[0]))
                    by_feature(fm(fb[3]), wk_s, xT_f).then_inc(kf_done.sem, 1)
                    by_feature(fm(fb[2]), wq_s, xT_f).then_inc(qf_done.sem, 1)
                    by_token(tm(fb[0]), xT_f, wv_s).then_inc(vf_done.sem, 1)
                    phases(f[0], 0)
                for s in range(SLOTS):
                    if f:
                        if s + 1 < UNITS:
                            phases(f[0], s + 1)
                        if 2 <= s < PAIRS + 2:
                            attend_k(f[0], s - 2)
                        if s in KV_TURN:
                            turn_kv(f[0], KV_TURN[s])
                        if s in ATTEND_Q:
                            attend_q(f[0], ATTEND_Q[s])
                    if b:
                        back(*b, s)
                if f:
                    pe.wait_ge(att_ready.sem, att_ready.at(f[0]))
                    by_token(tm(fb[0]), xT_f, wo_s).then_inc(wo_done.sem, 1)

            steps(pe, step)

            pe.wait_ge(S["experts_in"], EXPERTS)
            pe.wait_ge(S["table_ready"], 1)

            def bank(t2, k):
                return (fb, bb)[t2][k]

            def turn_rows(t, slot, here):
                q = slot % 2
                pe.wait_ge(tile_here[slot], here)
                for kt in range(KT):
                    last = pe.transpose(bank(q, 0)[:, kt * P:(kt + 1) * P], tile_in[slot][:, kt * P:(kt + 1) * P], ident[:, :])
                last.then_inc(tx_done.sem, 1)

            def gate_up(t, q):
                e = pe.value_load(tab_i[0:1, 0, bass.ds(t, 1)], min_val=0, max_val=E - 1)
                pe.wait_ge(tx_ready.sem, tx_ready.at(t))
                for kt in range(KT):
                    last = pe.matmul(bank(q, 1)[:, :], tile_xT[q][:, kt * P:(kt + 1) * P], gu_s[:, bass.ds(e * KT + kt, 1), :].rearrange("p o n -> p (o n)"),
                                     start=(kt == 0), stop=(kt == KT - 1))
                last.then_inc(gu_done.sem, 1)

            def turn_act(t, q):
                pe.wait_ge(act_ready.sem, act_ready.at(t))
                for kt in range(KT):
                    last = pe.transpose(bank(q, 2)[:, kt * P:(kt + 1) * P], tile_act[q][:, kt * P:(kt + 1) * P], ident[:, :])
                last.then_inc(ta_done.sem, 1)

            def down(t, q):
                e = pe.value_load(tab_i[0:1, 0, bass.ds(t, 1)], min_val=0, max_val=E - 1)
                pe.wait_ge(ta_ready.sem, ta_ready.at(t))
                w = down_s[:, bass.ds(e, 1), :].rearrange("p o n -> p (o n)")
                for kt in range(KT):
                    last = pe.matmul(bank(q, 3)[:, 0:D], tile_actT[q][:, kt * P:(kt + 1) * P], w[:, kt * D:(kt + 1) * D], start=(kt == 0), stop=(kt == KT - 1))
                last.then_inc(dn_done.sem, 1)

            turn_rows(0, 0, 16)
            gate_up(0, 0)
            turn_rows(1, 1, 16)

            def tile_step(t, k, more):
                turn_act(t - 1, (k - 1) % 2)
                gate_up(t, k % 2)
                down(t - 1, (k - 1) % 2)
                if more:
                    slot = (k + 1) % TILE_SLOTS
                    turn_rows(t + 1, slot, (t - k) * (16 // TILE_SLOTS) + 16 * ((k + 1) // TILE_SLOTS) + 16)

            with pe.Fori(0, TILES - 2 * TILE_SLOTS + 1, TILE_SLOTS) as t:
                for k in range(1, TILE_SLOTS + 1):
                    tile_step(t + k, k, True)
            for k in range(1, TILE_SLOTS):
                tile_step(TILES - TILE_SLOTS + k, k, k + 1 < TILE_SLOTS)
            turn_act(TILES - 1, (TILES - 1) % 2)
            down(TILES - 1, (TILES - 1) % 2)

        @block.gpsimd
        def _(pool):
            pool.memset(proj_s[:, :, :], 0.0).then_inc(S["proj_clear"], 1)
            pool.memset(blank[:, :], 0.0).then_inc(S["blank_done"], 1)
            pool.memset(ones[:, :], 1.0).then_inc(S["pool_start"], 1)
            pool.memset(mask[:, :], 0.0).then_inc(S["pool_start"], 1)
            pool.memset(half_pi[:, :], float(np.pi / 2)).then_inc(S["pool_start"], 1)
            for value, pair in pair_of.items():
                pool.memset(pair[:, :], value).then_inc(S["pool_start"], 1)
            pool.wait_ge(S["pool_start"], 7)
            pool.affine_select(out=ident[:, :], in_=ones[:, :], compare_op=ALU.is_equal, fill=0.0, base=0,
                               pattern=[[-1, P]], channel_multiplier=1).then_inc(S["pool_start"], 1)
            for k in (0, 2):
                pool.affine_select(out=mask[:, k * C:(k + 1) * C], in_=mask[:, k * C:(k + 1) * C], compare_op=ALU.is_ge,
                                   fill=NEG, base=0, pattern=[[-1, C]], channel_multiplier=1).then_inc(S["pool_start"], 1)
            pool.affine_select(out=earlier[:, :], in_=ones[:, :], compare_op=ALU.is_ge, fill=0.0, base=-1,
                               pattern=[[1, P]], channel_multiplier=-1).then_inc(S["pool_start"], 1)
            pool.iota(expert_no[:, :], pattern=[[1, E]], base=0, channel_multiplier=0,
                      allow_small_or_imprecise_dtypes=True).then_inc(S["pool_start"], 1)
            pool.iota(region0[:, :], pattern=[[REGION, E]], base=0, channel_multiplier=0,
                      allow_small_or_imprecise_dtypes=True).then_inc(S["pool_start"], 1)
            pool.iota(part_no[:, :], pattern=[[0, 1]], base=0, channel_multiplier=1,
                      allow_small_or_imprecise_dtypes=True).then_inc(S["pool_start"], 1)
            pool.wait_ge(S["pool_start"], POOL_START)
            pool.tensor_copy(ident_b[:, :], ident[:, :]).then_inc(S["consts"], 1)
            pool.iota(TAB[:, 0, :], pattern=[[1, TILES]], base=0, channel_multiplier=0,
                      allow_small_or_imprecise_dtypes=True).then_inc(S["pool_start"], 1)
            pool.wait_ge(S["weights_in"], WEIGHTS)

            def inverse_root(n, sm, mv, var, rstd, k, chain, c0, second=None):
                def one(ins):
                    nonlocal c0
                    c0 += 1
                    ins.then_inc(chain.sem, 1)
                    pool.wait_ge(chain.sem, chain.at(n, c0))

                pool.wait_ge(var.sem, var.at(n, k))
                root = pool.tensor_tensor(of(sm, RSTD), of(sm, VE), pair_of[-0.5][:, :], ALU.pow)
                if second is None:
                    root.then_inc(rstd.sem, 1)
                    return
                one(root)
                one(pool.tensor_tensor(of(sm, TMP), of(sm, RSTD), of(sm, RSTD), ALU.mult))
                one(pool.tensor_tensor(of(sm, TMP), mv[:, :, 1], of(sm, TMP), ALU.mult))
                one(pool.tensor_tensor(of(sm, TMP), of(sm, TMP), pair_of[second][:, :], ALU.add))
                pool.tensor_tensor(of(sm, R2), of(sm, TMP), pair_of[-0.5][:, :], ALU.pow).then_inc(rstd.sem, 1)

            def step(f, b):
                if f:
                    inverse_root(f[0], sm_f, mv_f, var_f, rstd_f, 1, pool_f, 0, EPS)
                    pool.wait_ge(znf_ready.sem, znf_ready.at(f[0]))
                    ap = a[f[1]][:, :, :]
                    pool.tensor_tensor(ap, ap, both(bo_s), ALU.add).then_inc(ab_ready.sem, 1)
                if b:
                    n, p = b
                    hp = h[p][:, :, :]
                    inverse_root(n, sm_b, mv_b, var_b, rstd_b, 1, pool_b, 0, RMS_EPS)
                    pool.wait_ge(z3_ready.sem, z3_ready.at(n))
                    pool.tensor_tensor(hp, hp, both(fb2_s), ALU.add).then_inc(hb_ready.sem, 1)
                    pool.wait_ge(sq_ready.sem, sq_ready.at(n))
                    pool.tensor_tensor(of(sm_b, TMP), of(sm_b, SQ), pair_of[1.0 / HID][:, :], ALU.mult).then_inc(pool_b.sem, 1)
                    pool.wait_ge(pool_b.sem, pool_b.at(n, 5))
                    pool.tensor_tensor(of(sm_b, TMP), of(sm_b, TMP), pair_of[RMS_EPS][:, :], ALU.add).then_inc(pool_b.sem, 1)
                    pool.wait_ge(pool_b.sem, pool_b.at(n, 6))
                    pool.tensor_tensor(of(sm_b, RR), of(sm_b, TMP), pair_of[-0.5][:, :], ALU.pow).then_inc(rms_ready.sem, 1)
                    inverse_root(n, sm_b, mv_b, var_b, rstd_b, 2, pool_b, 6)
                    inverse_root(n, sm_b, mv_b, var_b, rstd_b, 3, pool_b, 6)
                if f:
                    n, p = f
                    hp = h[p][:, :, :]
                    pool.wait_ge(x1_ready.sem, x1_ready.at(n))
                    pool.tensor_tensor(hp, hp, a[p][:, :, :], ALU.add).then_inc(pool_f.sem, 1)
                    inverse_root(n, sm_f, mv_f, var_f, rstd_f, 2, pool_f, 5)
                    pool.wait_ge(pool_f.sem, pool_f.at(n, 5))
                    pool.tensor_tensor(hp, hp, both(b2_s), ALU.add).then_inc(hx_ready.sem, 1)
                if b:
                    n, p = b
                    pool.wait_ge(pos_ready.sem, pos_ready.at(n))
                    pool.sem_inc(S["pool_passed"], 1)
                    for k in range(4):
                        pool.indirect_dma_start(rows, bass.IndirectOffsetOnAxis(ap=pos[p][:, k:k + 1], axis=0),
                                                xs[p][:, k % 2, :], None).then_inc(scattered[p], 16)

            steps(pool, step)

            pool.wait_ge(S["pad_ready"], 1)
            pool.sem_inc(S["pool_passed"], 1)
            for e in range(E):
                pool.indirect_dma_start(rows, bass.IndirectOffsetOnAxis(ap=pad_idx[:, e:e + 1], axis=0), blank[:, :], None).then_inc(S["pads_in"], 16)

            for q in range(2):
                pool.wait_ge(tile_stored[q], 16 * (TILES // 2) + 16)

            def fetch(n, value):
                pool.wait_ge(idx_set[n].sem, value)
                pool.sem_inc(S["pool_passed"], 1)
                for k in range(4):
                    dst = (out_y1, out_y2)[k // 2][n][:, (k % 2) * D:(k % 2 + 1) * D]
                    pool.indirect_dma_start(dst, None, results, bass.IndirectOffsetOnAxis(ap=idx_o[n][:, k:k + 1], axis=0)).then_inc(rows_here[n], 16)

            with pool.Fori(0, IMAGES // OUT_SLOTS) as r:
                for n in range(OUT_SLOTS):
                    fetch(n, idx_set[n].at(r))

        @block.scalar
        def _(act):
            act.wait_ge(S["weights_in"], WEIGHTS)
            act.wait_ge(S["pool_start"], POOL_START)

            def scaled(dst, src, g, beta):
                for kt in range(KT):
                    last = act.activation(dst[:, kt, :], fm(src)[:, kt, :], ACT.Identity, bias=col(beta, kt), scale=col(g, kt))
                return last

            def biased(n, dst, src, done, ready, bias):
                act.wait_ge(done.sem, done.at(n))
                for kt in range(KT):
                    last = act.activation(dst[:, kt, :], fm(src)[:, kt, :], ACT.Identity, bias=col(bias, kt))
                last.then_inc(ready.sem, 1)

            def round_unit(n, u):
                r, w = extent(u)
                act.wait_ge(phase_done.sem, phase_done.at(n, u + 1))
                if u >= 2:
                    act.wait_ge(feat_ready.sem, feat_ready.at(n, u - 1))
                act.activation(near(u)[0:r, 0:w], fb[1 + u % 2][0:r, 0:w], ACT.Copy, bias=ROUND).then_inc(turns_ready.sem, 1)

            def waves(n, u):
                r, w = extent(u)
                f = feat(u)
                act.wait_ge(near_ready.sem, near_ready.at(n, u + 1))
                if u >= FEATS:
                    act.wait_ge(feat_used.sem, feat_used.at(n, u - FEATS + 1))
                act.activation(f[0:r, 1, 0:w], near(u)[0:r, 0:w], ACT.Sin, scale=-TURN if rounds_on_act(u) else TURN)
                act.wait_ge(dist_ready.sem, dist_ready.at(n, u + 1))
                act.activation(f[0:r, 0, 0:w], dist(u)[0:r, 0:w], ACT.Sin, bias=half_pi[0:r, :], scale=-TURN).then_inc(feat_ready.sem, 1)

            def back(n, p, s):
                if s == GELU:
                    for c in range(2):
                        act.wait_ge(pre_ready.sem, pre_ready.at(n, 2 * c + 2))
                        act.activation(hid[:, c, :], hid[:, c, :], ACT.Gelu).then_inc(gelu_ready.sem, 1)
                    for c in range(2):
                        act.wait_ge(gelu_ready.sem, gelu_ready.at(n, c + 1))
                        last = act.activation(squares[c], hid[:, c, :], ACT.Square, accum_out=of(sm_b, SQ, c))
                    last.then_inc(sq_ready.sem, 1)
                elif s == TURN4:
                    act.wait_ge(xTb_done.sem, xTb_done.at(n, 2))
                    act.activation(xT_b[:, :, :], fm(bb[2]), ACT.Copy).then_inc(xTb_ready.sem, 1)
                elif s == PROJ:
                    biased(n, qT_b, bb[3], qb_done, qb_ready, CBQ)
                    biased(n, kT_b, bb[0], kb_done, kb_ready, CBK)
                elif s == SOFTMAX:
                    act.wait_ge(nmax_ready.sem, nmax_ready.at(n))
                    for c in range(2):
                        last = act.activation(prob[:, keys[c]], score[:, keys[c]], ACT.Exp, bias=of(sm_b, NMAX, c), accum_out=of(sm_b, SUM, c))
                    last.then_inc(prob_ready.sem, 1)
                elif s == TURN5:
                    act.wait_ge(xTb_done.sem, xTb_done.at(n, 3))
                    act.activation(xT_b[:, :, :], fm(bb[1]), ACT.Copy).then_inc(xTb_ready.sem, 1)
                elif s == LOGITS:
                    act.wait_ge(gap_ready.sem, gap_ready.at(n))
                    act.activation(of(sm_b, E12), of(sm_b, D12), ACT.Exp).then_inc(gap_exp.sem, 1)

            def step(f, b):
                if b:
                    act.wait_ge(xTb_done.sem, xTb_done.at(b[0], 1))
                    scaled(xT_b, bb[0], G2, B2).then_inc(xTb_ready.sem, 1)
                    for k, bank in enumerate((1, 2, 3, 0)):
                        act.wait_ge(up_done.sem, up_done.at(b[0], k + 1))
                        for m in range(2):
                            last = act.activation(hidT[:, 2 * k + m, :], fm(bb[bank])[:, m, :], ACT.Relu, bias=b1_col[:, 2 * k + m:2 * k + m + 1])
                        last.then_inc(relu_ready.sem, 1)
                if f:
                    act.wait_ge(xTf_done.sem, xTf_done.at(f[0]))
                    scaled(xT_f, fb[1], G1, B1).then_inc(xTf_ready.sem, 1)
                    biased(f[0], kT_f, fb[3], kf_done, kf_ready, BK)
                    biased(f[0], qT_f, fb[2], qf_done, qf_ready, BQ)
                for s in range(SLOTS):
                    if f:
                        if s + 1 < UNITS and rounds_on_act(s + 1):
                            round_unit(f[0], s + 1)
                        if s < UNITS:
                            waves(f[0], s)
                        for slot, half in KV_TURN.items():
                            if s == slot - 1:
                                act.wait_ge(kvT_done.sem, kvT_done.at(f[0], half + 1))
                                act.activation(kvT[:, 4 * half:4 * half + 4, :], (fb[3], fb[0])[half][:, :].rearrange("p (j m) -> p j m", j=4),
                                               ACT.Copy, scale=1.0 / M).then_inc(kvT_ready.sem, 1)
                    if b:
                        back(*b, s)
                if f:
                    act.wait_ge(att_done.sem, att_done.at(f[0]))
                    act.activation(xT_f[:, :, :], fm(fb[3]), ACT.Copy).then_inc(att_ready.sem, 1)

            steps(act, step)

            def bank(q, k):
                return (fb, bb)[q][k]

            def silu_tile(t, q):
                act.wait_ge(gu_done.sem, gu_done.at(t))
                act.activation(tile_silu[q], bank(q, 1)[:, 0:D], ACT.Silu).then_inc(silu_ready.sem, 1)

            def turned_act(t, q):
                act.wait_ge(ta_done.sem, ta_done.at(t))
                act.activation(tile_actT[q], bank(q, 2)[:, 0:D], ACT.Copy).then_inc(ta_ready.sem, 1)

            silu_tile(0, 0)
            with act.Fori(0, TILES - 3, 2) as t:
                for k in range(2):
                    turned_act(t + k, k)
                    silu_tile(t + k + 1, (k + 1) % 2)
            turned_act(TILES - 2, 0)
            silu_tile(TILES - 1, 1)
            turned_act(TILES - 1, 1)

        @block.vector
        def _(dve):
            dve.sem_inc(rows_gone.sem, rows_gone.credit)
            for p in range(2):
                dve.sem_inc(stored[p], 16)
                dve.sem_inc(tile_stored[p], 16)
            dve.memset(v_f[:, :, :, :], 0.0).then_inc(S["dve_start"], 1)

            dve.wait_ge(S["staged_in"], STAGED)
            for t in range(KT):
                for j in range(2):
                    last = dve.tensor_copy(tok_by_part[:, t, j], tok_feat[:, t, j])
            last.then_inc(S["ordered"], 1)
            dve.tensor_reduce(wsum[:, 0:1], f1_in, AX.XY, ALU.add, apply_absolute_value=True)
            dve.tensor_reduce(wsum[:, 1:2], f2_in, AX.XY, ALU.add, apply_absolute_value=True).then_inc(S["wsum_ready"], 1)
            dve.wait_ge(S["wsum_all"], 1)
            dve.tensor_scalar(wscale[:, :], fb[0][:, 0:2], 1.0 / (HID * D), QUANT_EPS, ALU.mult, ALU.max).then_inc(S["scales_ready"], 1)
            dve.wait_ge(S["scales_ready"], 1)
            dve.reciprocal(wrecip[:, :], wscale[:, :]).then_inc(S["scales_ready"], 1)
            dve.wait_ge(S["scales_ready"], 2)
            for n, (src, dst) in enumerate(((f1_in, f1_q), (f2_in, f2_q))):
                dve.tensor_scalar(src, src, wrecip[:, n:n + 1], ROUND, ALU.mult, ALU.add).then_inc(S["dve_start"], 1)
                dve.wait_ge(S["dve_start"], 2 + 2 * n)
                dve.tensor_scalar(src, src, -ROUND, 1.0, ALU.add, ALU.min).then_inc(S["dve_start"], 1)
                dve.wait_ge(S["dve_start"], 3 + 2 * n)
                dve.tensor_scalar(dst, src, -1.0, None, ALU.max).then_inc(S["ternary"], 1)
            group = 0
            for q in range(HALF):
                dve.wait_ge(S["turned"], group + 1)
                dve.tensor_copy(tok_w[:, q, :], bb[group % 4][0:XP, 0:D]).then_inc(S["turned_out"], 1)
                group += 1
            for w in (cq_s, ck_s, cv_s):
                dve.wait_ge(S["turned"], group + 1)
                dve.tensor_copy(w[:, :, :], bb[group % 4][:, :].rearrange("p (k m) -> p k m", k=KT)).then_inc(S["turned_out"], 1)
                group += 1
            for w, KN in ((f1_s, KT), (f2_s, HT)):
                for kt in range(KN):
                    dve.wait_ge(S["turned"], group + 1)
                    n = w.shape[2]
                    dve.tensor_copy(w[:, kt, :], bb[group % 4][:, :].bitcast(BF16)[:, 0:n]).then_inc(S["turned_out"], 1)
                    group += 1
            dve.tensor_scalar(proj_s[:, :, :], proj_s[:, :, :], 1.0 / (float(np.sqrt(DH)) * 2 * float(np.pi)), None,
                              ALU.mult).then_inc(S["scales_ready"], 1)
            dve.wait_ge(S["pool_start"], POOL_START + 1)
            dve.tensor_copy(base[:, :], region0[:, :]).then_inc(base_ready.sem, base_ready.credit)
            dve.wait_ge(S["dve_start"], 5)
            dve.wait_ge(S["turned_out"], group)
            dve.wait_ge(S["weights_in"], WEIGHTS)

            def pass_wait():
                dve.sem_inc(S["waits_passed"], 1)

            def moments(n, k, src, stats, mv, sm, bn, mean, var):
                for c in range(2):
                    last = dve.bn_stats(stats[:, c, :], src[:, c, :])
                last.then_inc(bn.sem, 1)
                dve.wait_ge(bn.sem, bn.at(n, k))
                pass_wait()
                for c in range(2):
                    last = dve.bn_aggr(mv[:, c, :], stats[:, c, :])
                last.then_inc(mean.sem, 1)
                dve.wait_ge(mean.sem, mean.at(n, k))
                dve.tensor_scalar(of(sm, VE), mv[:, :, 1], EPS, None, ALU.add).then_inc(var.sem, 1)

            def moments_f(n, k, src):
                moments(n, k, src, stats_f, mv_f, sm_f, bn_f, mean_f, var_f)

            def moments_b(n, k, src):
                moments(n, k, src, stats_b, mv_b, sm_b, bn_b, mean_b, var_b)

            def normalise(n, k, dst, src, mv, sm, rstd):
                dve.wait_ge(rstd.sem, rstd.at(n, k))
                for c in range(2):
                    last = dve.tensor_scalar(dst[:, c, :], src[:, c, :], mv[:, c, 0:1], of(sm, RSTD, c), ALU.subtract, ALU.mult)
                return last

            def quantise(n, k, src, dst, root_ready, root_k, w):
                def one(ins):
                    nonlocal k
                    k += 1
                    ins.then_inc(quant_step.sem, 1)
                    dve.wait_ge(quant_step.sem, quant_step.at(n, k))

                one(dve.tensor_reduce(of(sm_b, AMAX), src, AX.X, ALU.max, apply_absolute_value=True))
                dve.wait_ge(root_ready.sem, root_ready.at(n, root_k))
                if w == 0:
                    one(dve.tensor_tensor(of(sm_b, RR), of(sm_b, RSTD), of(sm_b, R2), ALU.mult))
                one(dve.tensor_tensor(of(sm_b, AMAX), of(sm_b, AMAX), of(sm_b, RR), ALU.mult))
                one(dve.tensor_scalar(of(sm_b, AMAX), of(sm_b, AMAX), QUANT_EPS, None, ALU.max))
                one(dve.reciprocal(of(sm_b, QS), of(sm_b, AMAX)))
                dve.tensor_scalar(of(sm_b, DQ), of(sm_b, AMAX), 1.0 / 127, wscale[0:C, w:w + 1], ALU.mult, ALU.mult)
                one(dve.scalar_tensor_tensor(of(sm_b, QS), of(sm_b, QS), 127.0, of(sm_b, RR), ALU.mult, ALU.mult))
                for c in range(2):
                    last = dve.tensor_scalar(src[:, c, :], src[:, c, :], of(sm_b, QS, c), ROUND, ALU.mult, ALU.add)
                one(last)
                return dve.tensor_scalar(dst, src, -ROUND, 127.0, ALU.add, ALU.min), k

            def take_phases(n, u):
                r, w = extent(u)
                nr, ph = near(u)[0:r, 0:w], fb[1 + u % 2][0:r, 0:w]
                if rounds_on_act(u):
                    dve.wait_ge(turns_ready.sem, turns_ready.at(n, u // 2 + 1))
                    if u >= 2:
                        dve.wait_ge(feat_ready.sem, feat_ready.at(n, u - 1))
                    dve.scalar_tensor_tensor(nr, nr, -ROUND, ph, ALU.add, ALU.subtract).then_inc(near_ready.sem, 1)
                else:
                    dve.wait_ge(phase_done.sem, phase_done.at(n, u + 1))
                    if u >= 2:
                        dve.wait_ge(feat_ready.sem, feat_ready.at(n, u - 1))
                    dve.tensor_scalar(nr, ph, ROUND, -ROUND, ALU.add, ALU.add).then_inc(whole_ready.sem, 1)
                    dve.wait_ge(whole_ready.sem, whole_ready.at(n, u // 2 + 1))
                    dve.tensor_tensor(nr, ph, nr, ALU.subtract).then_inc(near_ready.sem, 1)
                dve.wait_ge(near_ready.sem, near_ready.at(n, u + 1))
                dve.tensor_scalar(dist(u)[0:r, 0:w].bitcast(U32), nr.bitcast(U32), 0x7FFFFFFF, None, ALU.bitwise_and).then_inc(dist_ready.sem, 1)

            def route(n, p):
                k = 0

                def one(ins):
                    nonlocal k
                    k += 1
                    ins.then_inc(route_step.sem, 1)
                    dve.wait_ge(route_step.sem, route_step.at(n, k))

                dve.wait_ge(logit_done.sem, logit_done.at(n))
                one(dve.tensor_tensor(rt[:, LOGIT], bb[2][0:C, 0:2 * E].rearrange("p (c e) -> p c e", c=2), rb_s[:, :, :], ALU.add))
                pass_wait()
                for c in range(2):
                    last = dve.max(rt[:, TOP, c, :], rt[:, LOGIT, c, :])
                one(last)
                dve.tensor_tensor(of(sm_b, D12), rt[:, TOP, :, 1], rt[:, TOP, :, 0], ALU.subtract).then_inc(gap_ready.sem, 1)
                for c in range(2):
                    last = dve.max_index(rt_i[:, c, :], rt[:, TOP, c, :], rt[:, LOGIT, c, :])
                one(last)
                one(dve.tensor_copy(rt[:, IDX], rt_i[:, :, :]))
                for c in range(2):
                    for j, oh in enumerate((OH1, OH2)):
                        last = dve.tensor_scalar(rt[:, oh, c, :], expert_no[:, :], rt[:, IDX, c, j:j + 1], None, ALU.is_equal)
                one(last)
                dve.tensor_tensor(rt[:, CNT], rt[:, OH1], rt[:, OH2], ALU.add).then_inc(count_ready.sem, 1)
                dve.wait_ge(gap_exp.sem, gap_exp.at(n))
                one(dve.tensor_scalar(of(sm_b, W2), of(sm_b, E12), 1.0, None, ALU.add))
                one(dve.reciprocal(of(sm_b, W1), of(sm_b, W2)))
                one(dve.tensor_tensor(of(sm_b, W2), of(sm_b, E12), of(sm_b, W1), ALU.mult))
                one(dve.tensor_copy(weigh[:, bass.ds(n, 1), :].rearrange("p o (j c) -> p (o j) c", j=2), sm_b[:, W1:W2 + 1, :]))
                return k

            def place_tokens(n, p, k):
                def one(ins):
                    nonlocal k
                    k += 1
                    ins.then_inc(route_step.sem, 1)
                    dve.wait_ge(route_step.sem, route_step.at(n, k))

                dve.wait_ge(prefix_done.sem, prefix_done.at(n))
                dve.wait_ge(base_ready.sem, base_ready.at(n, 0))
                one(dve.tensor_tensor(rt[:, POS], bb[3][0:C, 0:2 * E].rearrange("p (c e) -> p c e", c=2),
                                      base[0:C, :].unsqueeze(1).broadcast_to([C, 2, E]), ALU.add))
                dve.tensor_tensor(base[:, :], bb[2][:, 0:E], base[:, :], ALU.add).then_inc(base_ready.sem, 1)
                for oh, pick in ((OH1, PICK1), (OH2, PICK2)):
                    last = dve.tensor_tensor(rt[:, pick], rt[:, oh], rt[:, POS], ALU.mult)
                one(last)
                for j, pick in enumerate((PICK1, PICK2)):
                    last = dve.tensor_reduce(pos_f[:, 2 * j:2 * j + 2], rt[:, pick], AX.X, ALU.add)
                last.then_inc(picked.sem, 1)
                dve.wait_ge(picked.sem, picked.at(n))
                dve.wait_ge(rows_gone.sem, n * rows_gone.per + 1)
                dve.tensor_copy(pos[p][:, :], pos_f[:, :]).then_inc(pos_ready.sem, 1)
                dve.tensor_copy(place[:, bass.ds(n, 1), :].rearrange("p o k -> p (o k)"), pos_f[:, :]).then_inc(placed.sem, 1)
                assert k == route_step.per

            def back(n, p, s):
                hp = h[p]
                if s == QIN_TURN:
                    dve.wait_ge(qinT_done.sem, qinT_done.at(n))
                    dve.tensor_copy(qinT, fm16(bb[2], KT)).then_inc(qinT_ready.sem, 1)
                elif s == F1:
                    for k, b in enumerate((3, 0, 1, 2)):
                        c, half = divmod(k, 2)
                        dve.wait_ge(f1_done.sem, f1_done.at(n, k + 1))
                        dve.scalar_tensor_tensor(hid[:, c, half * 512:(half + 1) * 512], bb[b][0:C, :], of(sm_b, DQ, c),
                                                 fb1_s[:, half * 512:(half + 1) * 512], ALU.mult, ALU.add).then_inc(pre_ready.sem, 1)
                elif s == QHID:
                    dve.wait_ge(gelu_ready.sem, gelu_ready.at(n))
                    last, k = quantise(n, 7, hid, qhid, rms_ready, 1, 1)
                    last.then_inc(qhid_ready.sem, 1)
                    assert k == quant_step.per
                elif s == QHID_TURN:
                    for k, b in enumerate((3, 0)):
                        dve.wait_ge(qhidT_done.sem, qhidT_done.at(n, k + 1))
                        dve.tensor_copy(qhidT[:, 4 * k:4 * k + 4, :], fm16(bb[b], 4)).then_inc(qhidT_ready.sem, 1)
                elif s == F2:
                    dve.wait_ge(f2_done.sem, f2_done.at(n))
                    dve.wait_ge(hb_ready.sem, hb_ready.at(n))
                    for c in range(2):
                        last = dve.scalar_tensor_tensor(hp[:, c, :], tm(bb[1])[:, c, :], of(sm_b, DQ, c), hp[:, c, :], ALU.mult, ALU.add)
                    last.then_inc(h2_ready.sem, 1)
                    dve.wait_ge(h2_ready.sem, h2_ready.at(n))
                    moments_b(n, 2, hp)
                elif s == LN4:
                    normalise(n, 2, zn_b, hp, mv_b, sm_b, rstd_b).then_inc(z4_ready.sem, 1)
                elif s == PROJ:
                    dve.wait_ge(vb_done.sem, vb_done.at(n))
                    dve.tensor_tensor(v_b[:, :, :], tm(bb[1]), both(cbv_s), ALU.add).then_inc(vb_ready.sem, 1)
                elif s == SCORE:
                    dve.wait_ge(score_done.sem, score_done.at(n))
                    dve.scalar_tensor_tensor(score, bb[2][0:C, 0:3 * C], SCORE_SCALE, mask[:, :], ALU.mult, ALU.add).then_inc(score_ready.sem, 1)
                    dve.wait_ge(score_ready.sem, score_ready.at(n))
                    for c in range(2):
                        last = dve.tensor_reduce(of(sm_b, NMAX, c), score[:, keys[c]], AX.X, ALU.max, negate=True)
                    last.then_inc(nmax_ready.sem, 1)
                elif s == PROB_TURN:
                    dve.wait_ge(prob_ready.sem, prob_ready.at(n))
                    dve.reciprocal(of(sm_b, RSUM), of(sm_b, SUM)).then_inc(rsum_ready.sem, 1)
                    dve.wait_ge(probT_done.sem, probT_done.at(n))
                    dve.tensor_copy(probT, bb[3][0:C, 0:3 * C].rearrange("p (b t) -> p b t", b=3)).then_inc(probT_ready.sem, 1)
                elif s == PV:
                    dve.wait_ge(pv_done.sem, pv_done.at(n))
                    dve.wait_ge(rsum_ready.sem, rsum_ready.at(n))
                    for c in range(2):
                        last = dve.scalar_tensor_tensor(hp[:, c, :], tm(bb[0])[:, c, :], of(sm_b, RSUM, c), hp[:, c, :], ALU.mult, ALU.add)
                    last.then_inc(h3_ready.sem, 1)
                    dve.wait_ge(h3_ready.sem, h3_ready.at(n))
                    moments_b(n, 3, hp)
                elif s == LN5:
                    dve.wait_ge(rows_gone.sem, n * rows_gone.per + 1)
                    normalise(n, 3, xs[p], hp, mv_b, sm_b, rstd_b).then_inc(z5_ready.sem, 1)
                elif s == LOGITS:
                    k = route(n, p)
                elif s == PREFIX:
                    place_tokens(n, p, 9)

            def step(f, b):
                if f:
                    n, p = f
                    dve.wait_ge(tok_done.sem, tok_done.at(n))
                    dve.wait_ge(stored[p], of_parity(n, p))
                    dve.tensor_tensor(h[p][:, :, :], tm(fb[2]), both(tok_b_s), ALU.add).then_inc(h_ready.sem, 1)
                    dve.wait_ge(h_ready.sem, h_ready.at(n))
                    moments_f(n, 1, h[p])
                    normalise(n, 1, a[p], h[p], mv_f, sm_f, rstd_f).then_inc(a_ready.sem, 1)
                    dve.wait_ge(a_ready.sem, a_ready.at(n))
                    for c in range(2):
                        last = dve.tensor_scalar(zn_f[:, c, :], a[p][:, c, :], of(sm_f, R2, c), None, ALU.mult)
                    last.then_inc(znf_ready.sem, 1)
                if b:
                    n, p = b
                    dve.wait_ge(mlp_done.sem, mlp_done.at(n))
                    dve.wait_ge(hx_ready.sem, hx_ready.at(n))
                    dve.tensor_tensor(h[p][:, :, :], tm(bb[1]), h[p][:, :, :], ALU.add).then_inc(h1_ready.sem, 1)
                    dve.wait_ge(h1_ready.sem, h1_ready.at(n))
                    moments_b(n, 1, h[p])
                    for c in range(2):
                        last = dve.tensor_scalar(zn_b[:, c, :], h[p][:, c, :], mv_b[:, c, 0:1], None, ALU.subtract)
                    last.then_inc(z3_ready.sem, 1)
                    dve.wait_ge(z3_ready.sem, z3_ready.at(n))
                    last, _ = quantise(n, 0, zn_b[:, :, :], qin[p], rstd_b, 1, 0)
                    last.then_inc(qin_ready.sem, 1)
                if f:
                    n, p = f
                    dve.wait_ge(vf_done.sem, vf_done.at(n))
                    for s in range(2):
                        last = dve.tensor_tensor(
                            v_f[:, :, s::2, s * DH:(s + 1) * DH],
                            tm(fb[0]).rearrange("p c (j s d) -> p c j s d", s=2, d=DH)[:, :, :, s, :],
                            bv_s[:, :].rearrange("p (o j s d) -> p o j s d", o=1, s=2, d=DH)[:, :, :, s, :].broadcast_to([C, 2, PAIRS, DH]), ALU.add)
                    last.then_inc(vf_ready.sem, 1)
                for s in range(SLOTS):
                    if f:
                        if s < UNITS:
                            take_phases(f[0], s)
                        if s in KV_TURN:
                            half = KV_TURN[s]
                            dve.wait_ge(kv_done.sem, kv_done.at(f[0], half + 1))
                            dve.tensor_copy(kv[:, 4 * half:4 * half + 4, :], (fb[3], fb[0])[half][:, :].rearrange("p (j m) -> p j m", j=4)).then_inc(kv_ready.sem, 1)
                    if b:
                        back(*b, s)
                if f:
                    n, p = f
                    dve.wait_ge(wo_done.sem, wo_done.at(n))
                    dve.wait_ge(ab_ready.sem, ab_ready.at(n))
                    dve.tensor_tensor(a[p][:, :, :], tm(fb[0]), a[p][:, :, :], ALU.add).then_inc(x1_ready.sem, 1)
                    dve.wait_ge(x1_ready.sem, x1_ready.at(n))
                    moments_f(n, 2, a[p])
                    normalise(n, 2, zn_b, a[p], mv_f, sm_f, rstd_f).then_inc(zn2_ready.sem, 1)

            steps(dve, step)

            dve.wait_ge(base_ready.sem, base_ready.at(IMAGES - 1))
            dve.tensor_scalar(pad_row[:, :], base[:, :], part_no[:, 0:1], None, ALU.add).then_inc(S["table_step"], 1)
            dve.wait_ge(S["table_step"], 1)
            dve.tensor_copy(pad_idx[:, :], pad_row[:, :]).then_inc(S["pad_ready"], 1)
            k = 1

            def one(ins):
                nonlocal_k[0] += 1
                ins.then_inc(S["table_step"], 1)
                dve.wait_ge(S["table_step"], nonlocal_k[0])

            nonlocal_k = [1]
            FULL, WHOLE, END, JUMP = range(4)
            one(dve.tensor_tensor(few[:, FULL, :], base[:, :], region0[:, :], ALU.subtract))
            one(dve.tensor_scalar(few[:, FULL, :], few[:, FULL, :], 1.0 / P, 127.0 / P - 0.5 + 0.5 / P, ALU.mult, ALU.add))
            one(dve.tensor_scalar(few[:, WHOLE, :], few[:, FULL, :], ROUND, -ROUND, ALU.add, ALU.add))
            one(dve.tensor_copy(few[:, END, :], few[:, WHOLE, :]))
            for e in range(1, E):
                one(dve.tensor_tensor(few[:, END, e:e + 1], few[:, END, e:e + 1], few[:, END, e - 1:e], ALU.add))
            one(dve.tensor_scalar(few[:, JUMP, :], few[:, WHOLE, :], -float(P), float(REGION), ALU.mult, ALU.add))
            one(dve.memset(TAB[:, 1, :], 0.0))
            one(dve.tensor_scalar(TAB[:, 2, :], TAB[:, 0, :], float(P), None, ALU.mult))
            for e in range(E):
                one(dve.tensor_scalar(TAB[:, 3, :], TAB[:, 0, :], few[0:1, END, e:e + 1], None, ALU.is_ge))
                one(dve.tensor_tensor(TAB[:, 1, :], TAB[:, 1, :], TAB[:, 3, :], ALU.add))
                one(dve.scalar_tensor_tensor(TAB[:, 2, :], TAB[:, 3, :], few[0:1, JUMP, e:e + 1], TAB[:, 2, :], ALU.mult, ALU.add))
            dve.tensor_scalar(tab_i[:, 0, :], TAB[:, 1, :], float(E - 1), None, ALU.min)
            dve.tensor_copy(tab_i[:, 1, :], TAB[:, 2, :]).then_inc(S["table_ready"], 1)
            dve.wait_ge(placed.sem, placed.at(IMAGES - 1))
            one(dve.tensor_copy(found[:, :, :], place[:, :, :]))
            for e in range(1, E):
                one(dve.tensor_scalar(later[:, :, :], place[:, :, :], float(e * REGION), few[0:C, JUMP, e - 1:e], ALU.is_ge, ALU.mult))
                one(dve.tensor_tensor(found[:, :, :], found[:, :, :], later[:, :, :], ALU.subtract))
            one(dve.tensor_copy(found_i[:, :, :], found[:, :, :]))

            def bank(q, k):
                return (fb, bb)[q][k]

            def turned_rows(t, q):
                dve.wait_ge(tx_done.sem, tx_done.at(t))
                dve.tensor_copy(tile_xT[q], bank(q, 0)[:, 0:D]).then_inc(tx_ready.sem, 1)

            def gated(t, q):
                dve.wait_ge(silu_ready.sem, silu_ready.at(t))
                dve.tensor_tensor(tile_act[q], tile_silu[q], bank(q, 1)[:, D:2 * D], ALU.mult).then_inc(act_ready.sem, 1)

            def result(t, q):
                dve.wait_ge(dn_done.sem, dn_done.at(t))
                dve.wait_ge(tile_stored[q], t * 8 + 16 - 8 * q)
                dve.tensor_copy(tile_y[q], bank(q, 3)[:, 0:D]).then_inc(y_ready.sem, 1)

            turned_rows(0, 0)
            gated(0, 0)
            turned_rows(1, 1)
            with dve.Fori(0, TILES - 3, 2) as t:
                for k in range(2):
                    gated(t + k + 1, (k + 1) % 2)
                    result(t + k, k)
                    turned_rows(t + k + 2, k)
            gated(TILES - 1, 1)
            result(TILES - 2, 0)
            result(TILES - 1, 1)

            for q in range(2):
                dve.wait_ge(tile_stored[q], 16 * (TILES // 2) + 16)

            def set_rows(j, n):
                dve.tensor_copy(idx_o[n][:, :], found_i[:, bass.ds(j, 1), :].rearrange("p o k -> p (o k)")).then_inc(idx_set[n].sem, 1)

            def add_up(j, n, r):
                dve.wait_ge(rows_here[n], r * 64 + 64)
                dve.wait_ge(resid_here[n], r * 16 + 16)
                w = weigh[:, bass.ds(j, 1), :].rearrange("p o k -> p (o k)")
                for c in range(2):
                    s = slice(c * D, (c + 1) * D)
                    last = dve.scalar_tensor_tensor(out_h[n][:, s], out_y1[n][:, s], w[:, c:c + 1], out_h[n][:, s], ALU.mult, ALU.add)
                last.then_inc(sum_step.sem, 1)
                dve.wait_ge(sum_step.sem, sum_step.at(j))
                for c in range(2):
                    s = slice(c * D, (c + 1) * D)
                    last = dve.scalar_tensor_tensor(out_h[n][:, s], out_y2[n][:, s], w[:, 2 + c:3 + c], out_h[n][:, s], ALU.mult, ALU.add)
                last.then_inc(sum_ready.sem, 1)

            for n in range(OUT_SLOTS):
                set_rows(n, n)
            with dve.Fori(0, IMAGES // OUT_SLOTS - 1) as r:
                for n in range(OUT_SLOTS):
                    add_up(r * OUT_SLOTS + n, n, r)
                    dve.wait_ge(sum_ready.sem, sum_ready.at(r * OUT_SLOTS + n))
                    set_rows((r + 1) * OUT_SLOTS + n, n)
            for n in range(OUT_SLOTS):
                add_up(IMAGES - OUT_SLOTS + n, n, IMAGES // OUT_SLOTS - 1)


_INS = ['x', 'L0_tok_W', 'L0_tok_b', 'L0_attn_proj_mat', 'L0_attn_wq', 'L0_attn_bq', 'L0_attn_wk', 'L0_attn_bk',
        'L0_attn_wv', 'L0_attn_bv', 'L0_attn_wo', 'L0_attn_bo', 'L0_attn_ln1_g', 'L0_attn_ln1_b', 'L0_attn_w1',
        'L0_attn_b1', 'L0_attn_w2', 'L0_attn_b2', 'L0_attn_ln2_g', 'L0_attn_ln2_b', 'L0_ffn_w1', 'L0_ffn_b1',
        'L0_ffn_w2', 'L0_ffn_b2', 'L1_attn_Wq', 'L1_attn_bq', 'L1_attn_Wk', 'L1_attn_bk', 'L1_attn_Wv', 'L1_attn_bv',
        'L1_ffn_router_w', 'L1_ffn_router_b', 'L1_ffn_we_gate', 'L1_ffn_we_up', 'L1_ffn_we_down']
_OUTS = [((64, 196, 256), 'float32')]


def kernel(**inputs):
    import numpy as _np
    import concourse.bacc as _bacc
    from concourse import mybir as _mybir
    from concourse.bass_utils import run_bass_kernel_spmd as _run

    nc = _bacc.Bacc("TRN2", target_bir_lowering=False, num_devices=1)
    arrays, args = {}, []
    for name in _INS:
        a = _np.ascontiguousarray(inputs[name])
        arrays[f"in_{name}_dram"] = a
        args.append(nc.dram_tensor(f"in_{name}_dram", a.shape, _mybir.dt.from_np(a.dtype), kind="ExternalInput").ap())
    for i, (shape, dtype) in enumerate(_OUTS):
        dt = _mybir.dt.from_np(_np.dtype(dtype))
        args.append(nc.dram_tensor(f"out_{i}_dram", shape, dt, kind="ExternalOutput").ap())
    vit_tower(nc, *args)
    r = _run(nc, [arrays], core_ids=[0])
    return r.results[0]["out_0_dram"]
```

```python
from contextlib import ExitStack

import numpy as np

import concourse.bass as bass
from concourse import mybir

ALU = mybir.AluOpType
ACT = mybir.ActivationFunctionType
AX = mybir.AxisListType
F32 = mybir.dt.float32
BF16 = mybir.dt.bfloat16
U32 = mybir.dt.uint32

P = 128
EPS = 1e-5
RMS_EPS = 1e-6
QUANT_EPS = 1e-5
ROUND = 1.5 * 2.0 ** 23
TURN = float(np.nextafter(np.float32(2 * np.pi), np.float32(0)))
NEG = -1e30
TILE_SLOTS = 4
OUT_SLOTS = 4


class Signal:

    def __init__(self, ctx, nc, name, per, credit=0):
        self.sem = ctx.enter_context(nc.semaphore(name))
        self.per = per
        self.credit = per * credit

    def at(self, n, k=None):
        return n * self.per + (self.per if k is None else k) + self.credit


def vit_tower(nc, x, tok_W, tok_b, proj_mat, wq, bq, wk, bk, wv, bv, wo, bo, ln1_g, ln1_b, w1, b1, w2, b2,
              ln2_g, ln2_b, ffn_w1, ffn_b1, ffn_w2, ffn_b2, Wq, cbq, Wk, cbk, Wv, cbv,
              router_w, router_b, we_gate, we_up, we_down, out):
    IMAGES, CH, SIDE, _ = x.shape
    D = tok_W.shape[0]
    PATCH = 16
    GRID = SIDE // PATCH
    T = GRID * GRID
    C = T // 2
    KT = D // P
    DH, M = proj_mat.shape
    HEADS = D // DH
    PAIRS = HEADS // 2
    HID = w1.shape[1]
    HT = HID // P
    E = router_w.shape[1]
    HALF = PATCH // 2
    PR = CH * PATCH
    XP = 2 * PR
    UNITS = 2 * PAIRS
    FEATS = 8
    SCORE_SCALE = 1.0 / float(np.sqrt(D))
    TOKENS = IMAGES * T
    REGION = TOKENS + P
    TILES = -(-(2 * TOKENS // P + E - 1) // TILE_SLOTS) * TILE_SLOTS
    SPARE = (TILES - 2 * TOKENS // P) * P
    IMG_DMA = 16 * CH * 2

    with ExitStack() as ctx:
        def sb(name, shape, dt=F32):
            return ctx.enter_context(nc.sbuf_tensor(name, shape, dt))

        def sem(name):
            return ctx.enter_context(nc.semaphore(name))

        def signal(name, per, credit=0):
            return Signal(ctx, nc, name, per, credit)

        rows = nc.dram_tensor("expert_rows", (E * REGION + SPARE, D), F32, kind="Internal").ap()
        results = nc.dram_tensor("expert_results", (TILES * P, D), F32, kind="Internal").ap()
        resid = nc.dram_tensor("residual", (IMAGES, T, D), F32, kind="Internal").ap()

        tok_w = sb("tok_w", [XP, HALF, D])
        wq_s, wk_s, wv_s, wo_s = (sb(n, [P, KT, D]) for n in ("wq_s", "wk_s", "wv_s", "wo_s"))
        w1_s = sb("w1_s", [P, KT, HID])
        w2_s = sb("w2_s", [P, HT, D])
        f1_s = sb("f1_s", [P, KT, HID], BF16)
        f2_s = sb("f2_s", [P, HT, D], BF16)
        cq_s, ck_s, cv_s = (sb(n, [P, KT, D]) for n in ("cq_s", "ck_s", "cv_s"))
        router_s = sb("router_s", [P, KT, E])
        proj_s = sb("proj_s", [P, P // DH, M])
        cols = sb("cols", [P, 8, KT])
        b1_col = sb("b1_col", [P, HT])
        tok_b_s, bv_s, bo_s, b2_s, fb2_s, cbv_s = (
            sb(n, [C, D]) for n in ("tok_b_s", "bv_s", "bo_s", "b2_s", "fb2_s", "cbv_s"))
        fb1_s = sb("fb1_s", [C, HID])
        rb_s = sb("rb_s", [C, 2, E])
        mask = sb("mask", [C, 3 * C])
        ident = sb("ident", [P, P])
        ident_b = sb("ident_b", [P, P], BF16)
        ones = sb("ones", [P, P])
        earlier = sb("earlier", [P, P])
        expert_no = sb("expert_no", [C, E])
        half_pi = sb("half_pi", [P, 1])
        pair_of = {n: sb(name, [C, 2]) for n, name in
                   ((-0.5, "minus_half"), (EPS, "eps_pair"), (RMS_EPS, "rms_eps_pair"), (1.0 / HID, "hid_share"))}
        wsum = sb("wsum", [P, 2])
        wscale = sb("wscale", [P, 2])
        wrecip = sb("wrecip", [P, 2])
        base = sb("base", [P, E])
        region0 = sb("region0", [P, E])
        place = sb("place", [C, IMAGES, 4])
        weigh = sb("weigh", [C, IMAGES, 4])

        PATCHES, ARENA_F, ARENA_B = GRID * SIDE, (FEATS + 2) * 1024, 4096
        work = sb("work", [P, 2 * PATCHES + ARENA_F + ARENA_B])
        patches = [work[:, p * PATCHES:(p + 1) * PATCHES] for p in range(2)]
        arena_f = work[:, 2 * PATCHES:2 * PATCHES + ARENA_F]
        arena_b = work[:, 2 * PATCHES + ARENA_F:2 * PATCHES + ARENA_F + ARENA_B]
        emb, a, xs = ([sb(f"{n}{p}", [C, 2, D]) for p in range(2)] for n in ("emb", "a", "xs"))
        h = sb("h", [C, 2, D])
        zn_f, zn_b, v_b = (sb(n, [C, 2, D]) for n in ("zn_f", "zn_b", "v_b"))
        xT_f, qT_f, kT_f, attT, xT_b, qT_b, kT_b = (
            sb(n, [P, KT, T]) for n in ("xT_f", "qT_f", "kT_f", "attT", "xT_b", "qT_b", "kT_b"))
        v_f = sb("v_f", [C, 2, HEADS, 2 * DH])
        kvT = sb("kvT", [P, PAIRS, M])
        kv = sb("kv", [P, PAIRS, 4 * 2 * DH])
        stats_e, stats_f, stats_b = (sb(n, [C, 2, 6]) for n in ("stats_e", "stats_f", "stats_b"))
        mv_e, mv_f, mv_b = (sb(n, [C, 2, 2]) for n in ("mv_e", "mv_f", "mv_b"))
        sm_e, sm_f, sm_b = (sb(n, [C, 16, 2]) for n in ("sm_e", "sm_f", "sm_b"))
        rt = sb("rt", [C, 9, 2, E])
        rt_i = sb("rt_i", [C, 2, E], U32)
        pos_f = sb("pos_f", [C, 4])
        pos = [sb(f"pos{p}", [C, 4], U32) for p in range(2)]
        fb = [ctx.enter_context(nc.psum_tensor(f"front_bank{b}", [P, 512], F32)) for b in range(4)]
        bb = [ctx.enter_context(nc.psum_tensor(f"back_bank{b}", [P, 512], F32)) for b in range(4)]

        FULL, WHOLE, END, JUMP = range(4)
        VE, RSTD, R2, TMP, AMAX, DQ, RR, SUM, NMAX, RSUM, QS, D12, E12, W1, W2, SQ = range(16)
        LOGIT, TOP, IDX, OH1, OH2, CNT, POS, PICK1, PICK2 = range(9)
        G1, B1, G2, B2, BQ, BK, CBQ, CBK = range(8)

        def col(n, t):
            return cols[:, n, t:t + 1]

        def of(sm, n, c=None):
            return sm[:, n, :] if c is None else sm[:, n, c:c + 1]

        def tm(b):
            return b[0:C, :].rearrange("p (c d) -> p c d", c=2)

        def fm(b):
            return b[:, 0:KT * T].rearrange("p (k t) -> p k t", k=KT)

        def fm16(b, k):
            return b[:, :].bitcast(BF16)[:, 0:k * T].rearrange("p (k t) -> p k t", k=k)

        def chunk(c):
            return slice(c * C, (c + 1) * C)

        keys = (slice(0, C), slice(C, 3 * C))

        def both(bias):
            return bias[:, :].unsqueeze(1).broadcast_to([C, 2, D])

        def feat(u):
            s = (u % FEATS) * 1024
            return arena_f[:, s:s + 1024].rearrange("p (f n) -> p f n", f=2)

        def near(u):
            s = (FEATS + u % 2) * 1024
            return arena_f[:, s:s + 512]

        def dist(u):
            s = (FEATS + u % 2) * 1024 + 512
            return arena_f[:, s:s + 512]

        def extent(u):
            return (C, 512) if u < PAIRS else (P, KT * T)

        def rounds_on_act(u):
            return u % 2 == 1

        hidT = arena_b[:, 0:HT * T].rearrange("p (m t) -> p m t", m=HT)
        hid = arena_b[0:C, 0:2 * HID].rearrange("p (c n) -> p c n", c=2)
        squares = [arena_b[0:C, (2 + c) * HID:(3 + c) * HID] for c in range(2)]
        qhid = arena_b[0:C, 2 * HID:3 * HID].bitcast(BF16).rearrange("p (c n) -> p c n", c=2)
        qhidT = arena_b[:, 3 * HID:3 * HID + HT * T // 2].bitcast(BF16).rearrange("p (m t) -> p m t", m=HT)
        qin = [a[p][:, 0, :].bitcast(BF16).rearrange("p (c d) -> p c d", c=2) for p in range(2)]
        qinT = xT_b[:, 0, :].bitcast(BF16).rearrange("p (k t) -> p k t", k=KT)
        score = arena_b[0:C, 0:3 * C]
        prob = arena_b[0:C, 512:512 + 3 * C]
        probT = arena_b[0:C, 1024:1024 + 3 * C].rearrange("p (b t) -> p b t", b=3)

        f1_in = arena_f[:, 0:2048].rearrange("p (t d) -> p t d", t=HT)
        f2_in = arena_f[:, 2048:4096].rearrange("p (t n) -> p t n", t=KT)
        f1_q = arena_f[:, 4096:5120].bitcast(BF16).rearrange("p (t d) -> p t d", t=HT)
        f2_q = arena_f[:, 5120:6144].bitcast(BF16).rearrange("p (t n) -> p t n", t=KT)
        tok_in = arena_f[:, 6144:6144 + KT * CH * PATCH * PATCH].rearrange("p (t f) -> p t f", t=KT)
        tok_order = arena_f[:, 7680:7680 + KT * HALF * XP]
        c_in = [arena_b[:, 512 * n:512 * (n + 1)].rearrange("p (t d) -> p t d", t=KT) for n in range(3)]
        tok_feat = tok_in.rearrange("m t (p j q c) -> m t j q c p", p=PATCH, j=2, c=CH)
        tok_by_part = tok_order.rearrange("m (t q j c p) -> m t j q c p", t=KT, q=HALF, j=2, c=CH)

        GU = E * KT * 2 * D
        gu_s = work[:, 0:GU].rearrange("p (e k n) -> p (e k) n", e=E, k=KT)
        down_s = work[:, GU:GU + E * KT * D].rearrange("p (e n) -> p e n", e=E)
        assert GU + E * KT * D <= 2 * PATCHES + ARENA_F
        tiles = work[:, GU + E * KT * D:]
        assert tiles.shape[1] >= (TILE_SLOTS + 10) * D
        tile_in = [tiles[:, n * D:(n + 1) * D] for n in range(TILE_SLOTS)]
        tile_xT, tile_silu, tile_act, tile_actT, tile_y = (
            [tiles[:, (TILE_SLOTS + 2 * k + n) * D:(TILE_SLOTS + 2 * k + n + 1) * D] for n in range(2)] for k in range(5))
        TAB = sb("TAB", [1, 4, TILES])
        tab_i = sb("tab_i", [1, 2, TILES], U32)
        few = sb("few", [P, 4, E])
        later, found = (sb(n, [C, IMAGES, 4]) for n in ("later", "found"))
        found_i = sb("found_i", [C, IMAGES, 4], U32)
        pad_row = sb("pad_row", [P, E])
        pad_idx = sb("pad_idx", [P, E], U32)
        part_no = sb("part_no", [P, 1])
        blank = sb("blank", [P, D])
        IMG = 2 * D
        out_y1, out_y2, out_h = (
            [work[0:C, (3 * n + k) * IMG:(3 * n + k + 1) * IMG] for n in range(OUT_SLOTS)] for k in range(3))

        names = ("weights_in staged_in proj_clear consts pool_start dve_start wsum_ready wsum_all ternary ordered "
                 "turned turned_out scales_ready waits_passed pool_passed experts_in blank_done rows_clear pad_ready pads_in "
                 "table_step table_ready found_step found_ready").split()
        S = {n: sem(n) for n in names}

        patches_in = [sem(f"patches_in{p}") for p in range(2)]
        stored = [sem(f"stored{p}") for p in range(2)]
        scattered = [sem(f"scattered{p}") for p in range(2)]
        rows_gone = signal("rows_gone", 1, credit=2)
        patches_used = signal("patches_used", 1, credit=2)
        tok_done = signal("tok_done", 1)
        emb_ready = signal("emb_ready", 1)
        bn_e, mean_e, var_e, rstd_e = (signal(n, 1) for n in ("bn_e", "mean_e", "var_e", "rstd_e"))
        bn_f, mean_f, var_f, rstd_f = (signal(n, 1) for n in ("bn_f", "mean_f", "var_f", "rstd_f"))
        bn_b, mean_b, var_b, rstd_b = (signal(n, 3) for n in ("bn_b", "mean_b", "var_b", "rstd_b"))
        pool_e = signal("pool_e", 4)
        sum_f = signal("sum_f", 1)
        pool_b = signal("pool_b", 6)
        a_ready = signal("a_ready", 1)
        ab_ready = signal("ab_ready", 1)
        znf_ready = signal("znf_ready", 1)
        xTf_done, xTf_ready = signal("xTf_done", 1), signal("xTf_ready", 1)
        qf_done, kf_done, vf_done = (signal(n, 1) for n in ("qf_done", "kf_done", "vf_done"))
        qf_ready, kf_ready, vf_ready = (signal(n, 1) for n in ("qf_ready", "kf_ready", "vf_ready"))
        phase_done = signal("phase_done", UNITS)
        turns_ready = signal("turns_ready", UNITS // 2)
        whole_ready = signal("whole_ready", UNITS // 2)
        near_ready = signal("near_ready", UNITS)
        dist_ready = signal("dist_ready", UNITS)
        feat_ready = signal("feat_ready", UNITS)
        feat_used = signal("feat_used", UNITS, credit=0)
        kvT_done, kvT_ready, kv_done, kv_ready = (signal(n, 2) for n in ("kvT_done", "kvT_ready", "kv_done", "kv_ready"))
        att_done, att_ready, wo_done, x1_ready, hx_ready = (signal(n, 1) for n in ("att_done", "att_ready", "wo_done", "x1_ready", "hx_ready"))
        zn2_ready = signal("zn2_ready", 1)
        xTb_done, xTb_ready = signal("xTb_done", 3), signal("xTb_ready", 3)
        up_done, relu_ready = signal("up_done", 4), signal("relu_ready", 4)
        z3_ready, hb_ready = (signal(n, 1) for n in ("z3_ready", "hb_ready"))
        mlp_done, h1_ready = (signal(n, 2) for n in ("mlp_done", "h1_ready"))
        quant_step = signal("quant_step", 13)
        rms_ready, qin_ready, qinT_done, qinT_ready = (signal(n, 1) for n in ("rms_ready", "qin_ready", "qinT_done", "qinT_ready"))
        f1_done, pre_ready, gelu_ready = signal("f1_done", 4), signal("pre_ready", 4), signal("gelu_ready", 2)
        sq_ready, qhid_ready, f2_done, h2_ready, z4_ready = (signal(n, 1) for n in ("sq_ready", "qhid_ready", "f2_done", "h2_ready", "z4_ready"))
        qhidT_done, qhidT_ready = signal("qhidT_done", 2), signal("qhidT_ready", 2)
        qb_done, kb_done, vb_done = (signal(n, 1) for n in ("qb_done", "kb_done", "vb_done"))
        qb_ready, kb_ready, vb_ready = (signal(n, 1) for n in ("qb_ready", "kb_ready", "vb_ready"))
        score_done, score_ready, nmax_ready, prob_ready, probT_done, probT_ready, rsum_ready, pv_done, h3_ready, z5_ready = (
            signal(n, 1) for n in ("score_done", "score_ready", "nmax_ready", "prob_ready", "probT_done", "probT_ready",
                                   "rsum_ready", "pv_done", "h3_ready", "z5_ready"))
        logit_done, gap_ready, gap_exp, count_ready, prefix_done, pos_ready = (
            signal(n, 1) for n in ("logit_done", "gap_ready", "gap_exp", "count_ready", "prefix_done", "pos_ready"))
        route_step = signal("route_step", 11)
        base_ready = signal("base_ready", 1, credit=1)
        picked, placed = (signal(n, 1) for n in ("picked", "placed"))

        tile_here = [sem(f"tile_here{n}") for n in range(TILE_SLOTS)]
        tile_stored = [sem(f"tile_stored{n}") for n in range(2)]
        tx_done, tx_ready, gu_done, silu_ready, act_ready, ta_done, ta_ready, dn_done, y_ready = (
            signal(n, 1) for n in ("tx_done", "tx_ready", "gu_done", "silu_ready", "act_ready", "ta_done", "ta_ready", "dn_done", "y_ready"))
        idx_set = signal("idx_set", 1)
        rows_here = [sem(f"rows_here{n}") for n in range(OUT_SLOTS)]
        resid_here = [sem(f"resid_here{n}") for n in range(OUT_SLOTS)]
        out_stored = [sem(f"out_stored{n}") for n in range(OUT_SLOTS)]
        sum_step = signal("sum_step", 1)
        sum_ready = signal("sum_ready", 1)
        idx_o = [sb(f"idx_o{n}", [C, 4], U32) for n in range(OUT_SLOTS)]

        POOL_START = 14
        WEIGHTS = 16 * (7 + 8 + 1 + 7 + 2)
        STAGED = 16 * (2 + 1 + 3 + P // DH)
        EXPERTS = 16 * 3 * E

        SLOTS = 24
        UP, DOWN, SUM1, QIN, QIN_TURN, F1, GELU, AMAX_HID, QHID, QHID_TURN, F2, LN4, TURN4, PROJ, SCORE = (
            (0, 1), (2, 3), 4, 5, 5, 6, 7, 8, 9, 10, 11, 12, 13, 14, 15)
        SOFTMAX, PROB_TURN, PV, LN5, TURN5, LOGITS, PREFIX = 16, 17, 18, 19, 20, 21, 23
        KV_TURN, ATTEND_Q, WO, LN2 = {7: 0, 10: 1}, {12: 0, 17: 1}, 19, 20
        ATTEND_K = {4: (0, 1, 2), 5: (3,), 6: (4,), 7: (5,), 8: (6,), 9: (7,)}
        EMBED, EMB, LN0, TURN1, KEYS, VALUES, QUERIES = {8: 0, 9: 1}, 10, 12, 13, 16, 18, 20

        def steps(eng, step):
            step((0, 0), None, None)
            step((1, 1), (0, 0), None)
            with eng.Fori(0, IMAGES - 3, 2) as i:
                step((i + 2, 0), (i + 1, 1), (i, 0))
                step((i + 3, 1), (i + 2, 0), (i + 1, 1))
            step(None, (IMAGES - 1, 1), (IMAGES - 2, 0))
            step(None, None, (IMAGES - 1, 1))

        def of_parity(n, p):
            return n * 8 + 16 - 8 * p

        block = ctx.enter_context(nc.Block())

        @block.sync
        def _(sp):
            sp.dma_start(f1_in, ffn_w1.rearrange("(t p) d -> p t d", p=P)).then_inc(S["staged_in"], 16)
            sp.dma_start(f2_in, ffn_w2.rearrange("(t p) n -> p t n", p=P)).then_inc(S["staged_in"], 16)
            sp.dma_start(tok_in, tok_W.rearrange("(t p) f -> p t f", p=P)).then_inc(S["staged_in"], 16)
            for stage, w in zip(c_in, (Wq, Wk, Wv)):
                sp.dma_start(stage, w.rearrange("(t p) d -> p t d", p=P)).then_inc(S["staged_in"], 16)
            sp.wait_ge(S["proj_clear"], 1)
            for r in range(P // DH):
                sp.dma_start(proj_s[DH * r:DH * (r + 1), r, :], proj_mat).then_inc(S["staged_in"], 16)

            def load_image(n, p):
                sp.wait_ge(patches_used.sem, n * patches_used.per + 1)
                for half in range(2):
                    for c in range(CH):
                        q0 = half * HALF
                        sp.dma_start(
                            patches[p][half * PR + c * PATCH:half * PR + (c + 1) * PATCH, :]
                            .rearrange("p (g w) -> p g w", g=GRID)[:, :, 0:SIDE - q0],
                            x[n, c].rearrange("(g p) w -> p g w", p=PATCH)[:, :, q0:SIDE],
                        ).then_inc(patches_in[p], 16)

            load_image(0, 0)
            for dst, src in ((wq_s, wq), (wk_s, wk), (wv_s, wv), (wo_s, wo), (w1_s, w1), (w2_s, w2), (router_s, router_w)):
                sp.dma_start(dst[:, :, :], src.rearrange("(t p) n -> p t n", p=P)).then_inc(S["weights_in"], 16)
            for n, src in ((G1, ln1_g), (B1, ln1_b), (G2, ln2_g), (B2, ln2_b), (BQ, bq), (BK, bk), (CBQ, cbq), (CBK, cbk)):
                sp.dma_start(cols[:, n, :], src.rearrange("(t p) -> p t", p=P), allow_slow_non_contiguous=True).then_inc(S["weights_in"], 16)
            sp.dma_start(b1_col[:, :], b1.rearrange("(t p) -> p t", p=P), allow_slow_non_contiguous=True).then_inc(S["weights_in"], 16)
            for dst, src in ((tok_b_s, tok_b), (bv_s, bv), (bo_s, bo), (b2_s, b2), (fb2_s, ffn_b2), (cbv_s, cbv), (fb1_s, ffn_b1)):
                sp.dma_start(dst[:, :], src.rearrange("(o n) -> o n", o=1).broadcast_to([C, src.shape[0]])).then_inc(S["weights_in"], 16)
            for c in range(2):
                sp.dma_start(rb_s[:, c, :], router_b.rearrange("(o n) -> o n", o=1).broadcast_to([C, E])).then_inc(S["weights_in"], 16)
            sp.wait_ge(S["blank_done"], 1)
            for r in range(SPARE // P):
                sp.dma_start(rows[E * REGION + r * P:E * REGION + (r + 1) * P, :], blank[:, :]).then_inc(S["rows_clear"], 16)

            def store_resid(n, p):
                sp.wait_ge(h3_ready.sem, h3_ready.at(n))
                sp.dma_start(resid[n].rearrange("(c p) d -> p c d", c=2), h[:, :, :]).then_inc(stored[p], 16)
                sp.wait_ge(scattered[p], 4 * of_parity(n, p))
                sp.sem_inc(rows_gone.sem, 1)

            load_image(1, 1)
            with sp.Fori(0, IMAGES - 3, 2) as i:
                load_image(i + 2, 0)
                store_resid(i, 0)
                load_image(i + 3, 1)
                store_resid(i + 1, 1)
            store_resid(IMAGES - 2, 0)

            sp.wait_ge(wo_done.sem, wo_done.at(IMAGES - 1))
            for e in range(E):
                for n, w in enumerate((we_gate, we_up)):
                    sp.dma_start(gu_s[:, e * KT:(e + 1) * KT, n * D:(n + 1) * D], w[e].rearrange("(t p) n -> p t n", p=P)).then_inc(S["experts_in"], 16)
                sp.dma_start(down_s[:, e, :].rearrange("p (t n) -> p t n", t=KT), we_down[e].rearrange("(t p) n -> p t n", p=P)).then_inc(S["experts_in"], 16)
            store_resid(IMAGES - 1, 1)
            sp.wait_ge(pos_ready.sem, pos_ready.at(IMAGES - 1))
            sp.wait_ge(S["table_ready"], 1)
            sp.wait_ge(S["pads_in"], 16 * E)
            sp.wait_ge(S["rows_clear"], SPARE // P * 16)
            for p in range(2):
                sp.wait_ge(scattered[p], 4 * 16 * IMAGES // 2)
                sp.wait_ge(stored[p], 16 * IMAGES // 2 + 16)

            def first_row(t):
                return sp.value_load(tab_i[0:1, 1, bass.ds(t, 1)], min_val=0, max_val=E * REGION + SPARE - P)

            def load_tile(t, slot):
                r = first_row(t)
                sp.dma_start(tile_in[slot], rows[bass.ds(r, P), :]).then_inc(tile_here[slot], 16)

            def store_tile(t, q):
                sp.wait_ge(y_ready.sem, y_ready.at(t))
                sp.dma_start(results[bass.ds(t * P, P), :], tile_y[q]).then_inc(tile_stored[q], 16)

            def refill(t):
                sp.wait_ge(tx_done.sem, tx_done.at(t, 1 - TILE_SLOTS))

            AHEAD = TILE_SLOTS + 2
            LOOPED = (TILES - AHEAD) // TILE_SLOTS * TILE_SLOTS
            for t in range(AHEAD):
                if t >= TILE_SLOTS:
                    refill(t)
                load_tile(t, t % TILE_SLOTS)
            with sp.Fori(0, LOOPED - TILE_SLOTS + 1, TILE_SLOTS) as t:
                for k in range(TILE_SLOTS):
                    store_tile(t + k, k % 2)
                    refill(t + k + AHEAD)
                    load_tile(t + k + AHEAD, (k + AHEAD) % TILE_SLOTS)
            for t in range(LOOPED, TILES):
                store_tile(t, t % 2)
                if t + AHEAD < TILES:
                    refill(t + AHEAD)
                    load_tile(t + AHEAD, (t + AHEAD) % TILE_SLOTS)
            for q in range(2):
                sp.wait_ge(tile_stored[q], 16 * (TILES // 2) + 16)

            def load_resid(j, n):
                sp.dma_start(out_h[n].rearrange("p (c d) -> p c d", c=2), resid[j].rearrange("(c p) d -> p c d", c=2)).then_inc(resid_here[n], 16)

            def store_out(j, n):
                sp.wait_ge(sum_ready.sem, sum_ready.at(j))
                sp.dma_start(out[j].rearrange("(c p) d -> p c d", c=2), out_h[n].rearrange("p (c d) -> p c d", c=2)).then_inc(out_stored[n], 16)

            for n in range(OUT_SLOTS):
                load_resid(n, n)
            with sp.Fori(0, IMAGES - 2 * OUT_SLOTS + 1, OUT_SLOTS) as j:
                for n in range(OUT_SLOTS):
                    store_out(j + n, n)
                for n in range(OUT_SLOTS):
                    sp.wait_ge(out_stored[n], j * (16 // OUT_SLOTS) + 16)
                    load_resid(j + OUT_SLOTS + n, n)
            for n in range(OUT_SLOTS):
                store_out(IMAGES - OUT_SLOTS + n, n)
            for n in range(OUT_SLOTS):
                sp.wait_ge(out_stored[n], 16 * IMAGES // OUT_SLOTS)

        @block.tensor
        def _(pe):
            pe.drain().then_inc(patches_used.sem, patches_used.credit)
            pe.wait_ge(S["consts"], 1)
            pe.wait_ge(S["wsum_ready"], 1)
            pe.matmul(fb[0][:, 0:2], ones[:, :], wsum[:, :], start=True, stop=True).then_inc(S["wsum_all"], 1)
            pe.wait_ge(S["ordered"], 1)
            group = 0
            for q in range(HALF):
                if group >= 4:
                    pe.wait_ge(S["turned_out"], group - 3)
                for t in range(KT):
                    last = pe.transpose(bb[group % 4][0:XP, t * P:(t + 1) * P], tok_order[:, (t * HALF + q) * XP:(t * HALF + q + 1) * XP], ident[:, :])
                last.then_inc(S["turned"], 1)
                group += 1
            for n in range(3):
                pe.wait_ge(S["turned_out"], group - 3)
                for kt in range(KT):
                    for t in range(KT):
                        last = pe.transpose(bb[group % 4][:, kt * D + t * P:kt * D + (t + 1) * P], c_in[n][:, t, kt * P:(kt + 1) * P], ident[:, :])
                last.then_inc(S["turned"], 1)
                group += 1
            for n, (src, KN, ON) in enumerate(((f1_q, KT, HT), (f2_q, HT, KT))):
                pe.wait_ge(S["ternary"], n + 1)
                for kt in range(KN):
                    pe.wait_ge(S["turned_out"], group - 3)
                    for t in range(ON):
                        last = pe.transpose(bb[group % 4][:, :].bitcast(BF16)[:, t * P:(t + 1) * P], src[:, t, kt * P:(kt + 1) * P], ident_b[:, :])
                    last.then_inc(S["turned"], 1)
                    group += 1
            pe.wait_ge(S["turned_out"], group)
            pe.wait_ge(S["weights_in"], WEIGHTS)
            pe.wait_ge(S["scales_ready"], 3)

            def turn(dst, src):
                for kt in range(KT):
                    for c in range(2):
                        last = pe.transpose(dst[:, kt, chunk(c)], src[:, c, kt * P:(kt + 1) * P], ident[0:C, 0:C])
                return last

            def by_feature(dst, w, src, nk=KT):
                for m in range(dst.shape[1]):
                    for kt in range(nk):
                        last = pe.matmul(dst[:, m, :], w[:, kt, m * P:(m + 1) * P], src[:, kt, :], start=(kt == 0), stop=(kt == nk - 1))
                return last

            def by_token(dst, src, w, nk=KT, chunks=(0, 1)):
                for c in chunks:
                    for kt in range(nk):
                        last = pe.matmul(dst[:, c, :], src[:, kt, chunk(c)], w[:, kt, :], start=(kt == 0), stop=(kt == nk - 1))
                return last

            def embed(n, p, c):
                if c == 0:
                    pe.wait_ge(patches_in[p], n * (IMG_DMA // 2) + IMG_DMA - p * (IMG_DMA // 2))
                pix = patches[p][0:XP, :].rearrange("p (t q) -> p t q", q=PATCH)
                for q in range(HALF):
                    last = pe.matmul(tm(bb[2])[:, c, :], pix[:, chunk(c), q], tok_w[:, q, :], start=(q == 0), stop=(q == HALF - 1))
                if c == 1:
                    last.then_inc(tok_done.sem, 1)
                    pe.drain().then_inc(patches_used.sem, 1)

            def phases(n, u):
                if u >= 2:
                    pe.wait_ge(near_ready.sem, near_ready.at(n, u - 1))
                pair = u % PAIRS
                kt, r = divmod(pair, 4)
                if u == 0:
                    pe.wait_ge(kf_ready.sem, kf_ready.at(n))
                if u == 1:
                    pe.wait_ge(qf_ready.sem, qf_ready.at(n))
                b = fb[1 + u % 2]
                for s in range(2):
                    if u < PAIRS:
                        last = pe.matmul(tm(b)[:, s, :], kT_f[:, kt, chunk(s)], proj_s[:, 2 * r:2 * r + 2, :].rearrange("p s m -> p (s m)"),
                                         start=True, stop=True)
                    else:
                        last = pe.matmul(fm(b)[:, s, :], proj_s[:, 2 * r + s, :], qT_f[:, kt, :], start=True, stop=True)
                last.then_inc(phase_done.sem, 1)

            def attend_k(n, u):
                pe.wait_ge(feat_ready.sem, feat_ready.at(n, u + 1))
                if u == 0:
                    pe.wait_ge(vf_ready.sem, vf_ready.at(n))
                b = fb[3] if u < PAIRS // 2 else fb[0]
                f = feat(u)[0:C].rearrange("p f (c s m) -> p f c s m", c=2, s=2)
                for c in range(2):
                    for s in range(2):
                        for g in range(2):
                            at = 32 * (2 * s + g)
                            last = pe.matmul(b[at:at + 32, (u % 4) * M:(u % 4 + 1) * M], v_f[:, c, 2 * u + s, :], f[:, g, c, s, :],
                                             start=(c == 0), stop=(c == 1))
                last.then_inc(feat_used.sem, 1)
                if u % 4 == 3:
                    pe.drain().then_inc(kvT_done.sem, 1)

            def turn_kv(n, half):
                pe.wait_ge(kvT_ready.sem, kvT_ready.at(n, half + 1))
                b = (fb[3], fb[0])[half]
                for j in range(4):
                    last = pe.transpose(b[:, j * P:(j + 1) * P], kvT[:, 4 * half + j, :], ident[:, :])
                last.then_inc(kv_done.sem, 1)

            def attend_q(n, half):
                if half == 0:
                    pe.wait_ge(kv_ready.sem, kv_ready.at(n))
                u0 = PAIRS + 4 * half
                pe.wait_ge(feat_ready.sem, feat_ready.at(n, u0 + 4))
                for k in range(4):
                    s, g = divmod(k, 2)
                    for r in range(4):
                        f = feat(u0 + r)[:, :, 0:KT * T].rearrange("p f (s t) -> p f s t", s=2)
                        last = pe.matmul(fm(fb[3])[32 * r:32 * r + 32, half, :], kv[:, 4 * half + r, k * 32:(k + 1) * 32], f[:, g, s, :],
                                         start=(k == 0), stop=(k == 3))
                last.then_inc(feat_used.sem, 4)
                if half == 1:
                    pe.drain().then_inc(att_done.sem, 1)

            def back(n, p, s):
                if s in UP:
                    if s == UP[0]:
                        pe.wait_ge(xTb_ready.sem, xTb_ready.at(n, 1))
                    for k, bank in ((0, 1), (1, 2)) if s == UP[0] else ((2, 3), (3, 0)):
                        if k == 1:
                            pe.wait_ge(base_ready.sem, base_ready.at(n, 0))
                        by_feature(fm(bb[bank]), w1_s[:, :, k * 2 * P:(k + 1) * 2 * P], xT_b).then_inc(up_done.sem, 1)
                elif s in DOWN:
                    pe.wait_ge(relu_ready.sem, relu_ready.at(n))
                    c = DOWN.index(s)
                    by_token(tm(bb[1 + c]), hidT, w2_s, HT, (c,)).then_inc(mlp_done.sem, 1)
                elif s == QIN_TURN:
                    pe.wait_ge(qin_ready.sem, qin_ready.at(n))
                    for kt in range(KT):
                        for c in range(2):
                            last = pe.transpose(fm16(bb[2], KT)[:, kt, chunk(c)], qin[p][:, c, kt * P:(kt + 1) * P], ident_b[0:C, 0:C])
                    last.then_inc(qinT_done.sem, 1)
                elif s == F1:
                    pe.wait_ge(qinT_ready.sem, qinT_ready.at(n))
                    for k, b in enumerate((3, 0, 1, 2)):
                        c, half = divmod(k, 2)
                        for kt in range(KT):
                            last = pe.matmul(bb[b][0:C, :], qinT[:, kt, chunk(c)], f1_s[:, kt, half * 512:(half + 1) * 512], start=(kt == 0), stop=(kt == KT - 1))
                        last.then_inc(f1_done.sem, 1)
                elif s == QHID_TURN:
                    pe.wait_ge(qhid_ready.sem, qhid_ready.at(n))
                    for k, b in enumerate((3, 0)):
                        for kt in range(4):
                            for c in range(2):
                                last = pe.transpose(fm16(bb[b], 4)[:, kt, chunk(c)], qhid[:, c, (4 * k + kt) * P:(4 * k + kt + 1) * P], ident_b[0:C, 0:C])
                        last.then_inc(qhidT_done.sem, 1)
                elif s == F2:
                    pe.wait_ge(qhidT_ready.sem, qhidT_ready.at(n))
                    by_token(tm(bb[1]), qhidT, f2_s, HT).then_inc(f2_done.sem, 1)
                elif s == TURN4:
                    pe.wait_ge(z4_ready.sem, z4_ready.at(n))
                    turn(fm(bb[2]), zn_b).then_inc(xTb_done.sem, 1)
                elif s == PROJ:
                    pe.wait_ge(xTb_ready.sem, xTb_ready.at(n, 2))
                    by_feature(fm(bb[3]), cq_s, xT_b).then_inc(qb_done.sem, 1)
                    by_feature(fm(bb[0]), ck_s, xT_b).then_inc(kb_done.sem, 1)
                    by_token(tm(bb[1]), xT_b, cv_s).then_inc(vb_done.sem, 1)
                elif s == SCORE:
                    pe.wait_ge(qb_ready.sem, qb_ready.at(n))
                    pe.wait_ge(kb_ready.sem, kb_ready.at(n))
                    for c in range(2):
                        for kt in range(KT):
                            last = pe.matmul(bb[2][0:C, keys[c]], qT_b[:, kt, chunk(c)], kT_b[:, kt, 0:(c + 1) * C], start=(kt == 0), stop=(kt == KT - 1))
                    last.then_inc(score_done.sem, 1)
                elif s == PROB_TURN:
                    pe.wait_ge(prob_ready.sem, prob_ready.at(n))
                    for k in range(3):
                        last = pe.transpose(bb[3][0:C, k * C:(k + 1) * C], prob[:, k * C:(k + 1) * C], ident[0:C, 0:C])
                    last.then_inc(probT_done.sem, 1)
                elif s == PV:
                    pe.wait_ge(probT_ready.sem, probT_ready.at(n))
                    pe.wait_ge(vb_ready.sem, vb_ready.at(n))
                    pe.matmul(tm(bb[0])[:, 0, :], probT[:, 0, :], v_b[:, 0, :], start=True, stop=True)
                    for c in range(2):
                        last = pe.matmul(tm(bb[0])[:, 1, :], probT[:, 1 + c, :], v_b[:, c, :], start=(c == 0), stop=(c == 1))
                    last.then_inc(pv_done.sem, 1)
                elif s == TURN5:
                    pe.wait_ge(z5_ready.sem, z5_ready.at(n))
                    turn(fm(bb[1]), xs[p]).then_inc(xTb_done.sem, 1)
                elif s == LOGITS:
                    pe.wait_ge(xTb_ready.sem, xTb_ready.at(n, 3))
                    for c in range(2):
                        for kt in range(KT):
                            last = pe.matmul(bb[2][0:C, c * E:(c + 1) * E], xT_b[:, kt, chunk(c)], router_s[:, kt, :], start=(kt == 0), stop=(kt == KT - 1))
                    last.then_inc(logit_done.sem, 1)
                elif s == PREFIX:
                    pe.wait_ge(count_ready.sem, count_ready.at(n))
                    pe.matmul(bb[3][0:C, 0:E], earlier[0:C, 0:C], rt[:, CNT, 0, :], start=True, stop=True)
                    pe.matmul(bb[3][0:C, E:2 * E], earlier[0:C, 0:C], rt[:, CNT, 1, :], start=True, stop=False)
                    pe.matmul(bb[3][0:C, E:2 * E], ones[0:C, 0:C], rt[:, CNT, 0, :], start=False, stop=True)
                    pe.matmul(bb[2][:, 0:E], ones[0:C, :], rt[:, CNT, 0, :], start=True, stop=False)
                    pe.matmul(bb[2][:, 0:E], ones[0:C, :], rt[:, CNT, 1, :], start=False, stop=True).then_inc(prefix_done.sem, 1)

            def entry(n, p, s):
                if s in EMBED:
                    embed(n, p, EMBED[s])
                elif s == TURN1:
                    pe.wait_ge(znf_ready.sem, znf_ready.at(n))
                    turn(fm(fb[0]), zn_f).then_inc(xTf_done.sem, 1)
                elif s == KEYS:
                    pe.wait_ge(xTf_ready.sem, xTf_ready.at(n))
                    by_feature(fm(fb[0]), wk_s, xT_f).then_inc(kf_done.sem, 1)
                elif s == QUERIES:
                    by_feature(fm(fb[2]), wq_s, xT_f).then_inc(qf_done.sem, 1)
                elif s == VALUES:
                    pe.wait_ge(kf_ready.sem, kf_ready.at(n))
                    by_token(tm(fb[0]), xT_f, wv_s).then_inc(vf_done.sem, 1)

            def step(e, f, b):
                for s in range(SLOTS):
                    if f:
                        if 2 <= s + 1 < UNITS:
                            phases(f[0], s + 1)
                        for u in ATTEND_K.get(s, ()):
                            attend_k(f[0], u)
                        if s in KV_TURN:
                            turn_kv(f[0], KV_TURN[s])
                        if s in ATTEND_Q:
                            attend_q(f[0], ATTEND_Q[s])
                        if s == WO:
                            pe.wait_ge(att_ready.sem, att_ready.at(f[0]))
                            by_token(tm(fb[3]), attT, wo_s).then_inc(wo_done.sem, 1)
                    if e and s == PREFIX:
                        for u in range(2):
                            phases(e[0], u)
                    if f and s == PREFIX:
                        pe.wait_ge(zn2_ready.sem, zn2_ready.at(f[0]))
                        turn(fm(bb[0]), zn_b).then_inc(xTb_done.sem, 1)
                    if b:
                        back(*b, s)
                    if e:
                        if s == min(EMBED) and b:
                            pe.wait_ge(pre_ready.sem, pre_ready.at(b[0]))
                        if s == TURN1 and f:
                            pe.wait_ge(kv_ready.sem, kv_ready.at(f[0]))
                        entry(*e, s)

            steps(pe, step)

            pe.wait_ge(S["experts_in"], EXPERTS)
            pe.wait_ge(S["table_ready"], 1)

            def bank(t2, k):
                return (fb, bb)[t2][k]

            def turn_rows(t, slot, here):
                q = slot % 2
                pe.wait_ge(tile_here[slot], here)
                for kt in range(KT):
                    last = pe.transpose(bank(q, 0)[:, kt * P:(kt + 1) * P], tile_in[slot][:, kt * P:(kt + 1) * P], ident[:, :])
                last.then_inc(tx_done.sem, 1)

            def expert(t):
                return pe.value_load(tab_i[0:1, 0, bass.ds(t, 1)], min_val=0, max_val=E - 1)

            def gate_up(t, q, e):
                pe.wait_ge(tx_ready.sem, tx_ready.at(t))
                for kt in range(KT):
                    last = pe.matmul(bank(q, 1)[:, :], tile_xT[q][:, kt * P:(kt + 1) * P], gu_s[:, bass.ds(e * KT + kt, 1), :].rearrange("p o n -> p (o n)"),
                                     start=(kt == 0), stop=(kt == KT - 1))
                last.then_inc(gu_done.sem, 1)

            def turn_act(t, q):
                pe.wait_ge(act_ready.sem, act_ready.at(t))
                for kt in range(KT):
                    last = pe.transpose(bank(q, 2)[:, kt * P:(kt + 1) * P], tile_act[q][:, kt * P:(kt + 1) * P], ident[:, :])
                last.then_inc(ta_done.sem, 1)

            def down(t, q, e):
                pe.wait_ge(ta_ready.sem, ta_ready.at(t))
                w = down_s[:, bass.ds(e, 1), :].rearrange("p o n -> p (o n)")
                for kt in range(KT):
                    last = pe.matmul(bank(q, 3)[:, 0:D], tile_actT[q][:, kt * P:(kt + 1) * P], w[:, kt * D:(kt + 1) * D], start=(kt == 0), stop=(kt == KT - 1))
                last.then_inc(dn_done.sem, 1)

            def tile_step(t, k, experts, load_next, more=True):
                gate_up(t, k % 2, experts[-1])
                e_next = (expert(t + 1),) if load_next else ()
                if experts[1:]:
                    turn_act(t - 1, (k - 1) % 2)
                if more:
                    slot = (k + 1) % TILE_SLOTS
                    turn_rows(t + 1, slot, (t - k) * (16 // TILE_SLOTS) + 16 * ((k + 1) // TILE_SLOTS) + 16)
                if experts[2:]:
                    down(t - 2, k % 2, experts[0])
                return (experts + e_next)[-3:]

            turn_rows(0, 0, 16)
            e = (expert(0),)
            e = tile_step(0, 0, e, True)
            e = tile_step(1, 1, e, False)
            with pe.Fori(0, TILES - 2 * TILE_SLOTS + 1, TILE_SLOTS) as t:
                e = expert(t), expert(t + 1), expert(t + 2)
                for k in range(2, TILE_SLOTS + 2):
                    e = tile_step(t + k, k, e, k < TILE_SLOTS + 1)
            t = TILES - TILE_SLOTS
            e = expert(t), expert(t + 1), expert(t + 2)
            for k in range(2, TILE_SLOTS):
                more = k + 1 < TILE_SLOTS
                e = tile_step(t + k, k, e, more, more)
            turn_act(TILES - 1, 1)
            for t in (TILES - 2, TILES - 1):
                pe.wait_ge(y_ready.sem, y_ready.at(t - 2))
                down(t, t % 2, e[t - TILES])

        @block.gpsimd
        def _(pool):
            pool.memset(proj_s[:, :, :], 0.0).then_inc(S["proj_clear"], 1)
            pool.memset(blank[:, :], 0.0).then_inc(S["blank_done"], 1)
            pool.memset(ones[:, :], 1.0).then_inc(S["pool_start"], 1)
            pool.memset(mask[:, :], 0.0).then_inc(S["pool_start"], 1)
            pool.memset(half_pi[:, :], float(np.pi / 2)).then_inc(S["pool_start"], 1)
            for value, pair in pair_of.items():
                pool.memset(pair[:, :], value).then_inc(S["pool_start"], 1)
            pool.wait_ge(S["pool_start"], 7)
            pool.affine_select(out=ident[:, :], in_=ones[:, :], compare_op=ALU.is_equal, fill=0.0, base=0,
                               pattern=[[-1, P]], channel_multiplier=1).then_inc(S["pool_start"], 1)
            for k in (0, 2):
                pool.affine_select(out=mask[:, k * C:(k + 1) * C], in_=mask[:, k * C:(k + 1) * C], compare_op=ALU.is_ge,
                                   fill=NEG, base=0, pattern=[[-1, C]], channel_multiplier=1).then_inc(S["pool_start"], 1)
            pool.affine_select(out=earlier[:, :], in_=ones[:, :], compare_op=ALU.is_ge, fill=0.0, base=-1,
                               pattern=[[1, P]], channel_multiplier=-1).then_inc(S["pool_start"], 1)
            pool.iota(expert_no[:, :], pattern=[[1, E]], base=0, channel_multiplier=0,
                      allow_small_or_imprecise_dtypes=True).then_inc(S["pool_start"], 1)
            pool.iota(region0[:, :], pattern=[[REGION, E]], base=0, channel_multiplier=0,
                      allow_small_or_imprecise_dtypes=True).then_inc(S["pool_start"], 1)
            pool.iota(part_no[:, :], pattern=[[0, 1]], base=0, channel_multiplier=1,
                      allow_small_or_imprecise_dtypes=True).then_inc(S["pool_start"], 1)
            pool.wait_ge(S["pool_start"], POOL_START)
            pool.tensor_copy(ident_b[:, :], ident[:, :]).then_inc(S["consts"], 1)
            pool.iota(TAB[:, 0, :], pattern=[[1, TILES]], base=0, channel_multiplier=0,
                      allow_small_or_imprecise_dtypes=True).then_inc(S["pool_start"], 1)
            pool.wait_ge(S["weights_in"], WEIGHTS)

            def inverse_root(n, sm, mv, var, rstd, k, chain, c0, second=None):
                def one(ins):
                    nonlocal c0
                    c0 += 1
                    ins.then_inc(chain.sem, 1)
                    pool.wait_ge(chain.sem, chain.at(n, c0))

                pool.wait_ge(var.sem, var.at(n, k))
                root = pool.tensor_tensor(of(sm, RSTD), of(sm, VE), pair_of[-0.5][:, :], ALU.pow)
                if second is None:
                    root.then_inc(rstd.sem, 1)
                    return
                one(root)
                one(pool.tensor_tensor(of(sm, TMP), of(sm, RSTD), of(sm, RSTD), ALU.mult))
                one(pool.tensor_tensor(of(sm, TMP), mv[:, :, 1], of(sm, TMP), ALU.mult))
                one(pool.tensor_tensor(of(sm, TMP), of(sm, TMP), pair_of[second][:, :], ALU.add))
                pool.tensor_tensor(of(sm, R2), of(sm, TMP), pair_of[-0.5][:, :], ALU.pow).then_inc(rstd.sem, 1)

            def step(e, f, b):
                if b:
                    n, p = b
                    inverse_root(n, sm_b, mv_b, var_b, rstd_b, 1, pool_b, 0, RMS_EPS)
                    pool.wait_ge(z3_ready.sem, z3_ready.at(n))
                    pool.tensor_tensor(h[:, :, :], h[:, :, :], both(fb2_s), ALU.add).then_inc(hb_ready.sem, 1)
                    pool.wait_ge(sq_ready.sem, sq_ready.at(n))
                    pool.tensor_tensor(of(sm_b, TMP), of(sm_b, SQ), pair_of[1.0 / HID][:, :], ALU.mult).then_inc(pool_b.sem, 1)
                    pool.wait_ge(pool_b.sem, pool_b.at(n, 5))
                    pool.tensor_tensor(of(sm_b, TMP), of(sm_b, TMP), pair_of[RMS_EPS][:, :], ALU.add).then_inc(pool_b.sem, 1)
                    pool.wait_ge(pool_b.sem, pool_b.at(n, 6))
                    pool.tensor_tensor(of(sm_b, RR), of(sm_b, TMP), pair_of[-0.5][:, :], ALU.pow).then_inc(rms_ready.sem, 1)
                if e:
                    inverse_root(e[0], sm_e, mv_e, var_e, rstd_e, 1, pool_e, 0, EPS)
                if b:
                    inverse_root(b[0], sm_b, mv_b, var_b, rstd_b, 2, pool_b, 6)
                if e:
                    pool.wait_ge(znf_ready.sem, znf_ready.at(e[0]))
                    ap = a[e[1]][:, :, :]
                    pool.tensor_tensor(ap, ap, both(bo_s), ALU.add).then_inc(ab_ready.sem, 1)
                if b:
                    inverse_root(b[0], sm_b, mv_b, var_b, rstd_b, 3, pool_b, 6)
                if f:
                    n, p = f
                    pool.wait_ge(stored[1 - p], 8 * n + 16 + 8 * p)
                    pool.wait_ge(x1_ready.sem, x1_ready.at(n))
                    pool.tensor_tensor(h[:, :, :], emb[p][:, :, :], a[p][:, :, :], ALU.add).then_inc(sum_f.sem, 1)
                    inverse_root(n, sm_f, mv_f, var_f, rstd_f, 1, None, 0)
                    pool.wait_ge(sum_f.sem, sum_f.at(n))
                    pool.tensor_tensor(h[:, :, :], h[:, :, :], both(b2_s), ALU.add).then_inc(hx_ready.sem, 1)
                if b:
                    n, p = b
                    pool.wait_ge(pos_ready.sem, pos_ready.at(n))
                    pool.sem_inc(S["pool_passed"], 1)
                    for k in range(4):
                        pool.indirect_dma_start(rows, bass.IndirectOffsetOnAxis(ap=pos[p][:, k:k + 1], axis=0),
                                                xs[p][:, k % 2, :], None).then_inc(scattered[p], 16)

            steps(pool, step)

            pool.wait_ge(S["pad_ready"], 1)
            pool.sem_inc(S["pool_passed"], 1)
            for e in range(E):
                pool.indirect_dma_start(rows, bass.IndirectOffsetOnAxis(ap=pad_idx[:, e:e + 1], axis=0), blank[:, :], None).then_inc(S["pads_in"], 16)

            pool.wait_ge(S["table_ready"], 1)
            pool.wait_ge(placed.sem, placed.at(IMAGES - 1))
            pool.tensor_copy(found[:, :, :], place[:, :, :]).then_inc(S["found_step"], 1)
            for e in range(1, E):
                pool.tensor_scalar(later[:, :, :], place[:, :, :], float(e * REGION), few[0:C, JUMP, e - 1:e],
                                   ALU.is_ge, ALU.mult).then_inc(S["found_step"], 1)
                pool.wait_ge(S["found_step"], 2 * e)
                pool.tensor_tensor(found[:, :, :], found[:, :, :], later[:, :, :], ALU.subtract).then_inc(S["found_step"], 1)
                pool.wait_ge(S["found_step"], 2 * e + 1)
            pool.tensor_copy(found_i[:, :, :], found[:, :, :]).then_inc(S["found_ready"], 1)

            for q in range(2):
                pool.wait_ge(tile_stored[q], 16 * (TILES // 2) + 16)

            def fetch(j, n):
                pool.wait_ge(idx_set.sem, idx_set.at(j))
                pool.sem_inc(S["pool_passed"], 1)
                for k in range(4):
                    dst = (out_y1, out_y2)[k // 2][n][:, (k % 2) * D:(k % 2 + 1) * D]
                    pool.indirect_dma_start(dst, None, results, bass.IndirectOffsetOnAxis(ap=idx_o[n][:, k:k + 1], axis=0)).then_inc(rows_here[n], 16)

            with pool.Fori(0, IMAGES // OUT_SLOTS) as r:
                for n in range(OUT_SLOTS):
                    fetch(r * OUT_SLOTS + n, n)

        @block.scalar
        def _(act):
            act.wait_ge(S["weights_in"], WEIGHTS)
            act.wait_ge(S["pool_start"], POOL_START)

            def scaled(dst, src, g, beta):
                for kt in range(KT):
                    last = act.activation(dst[:, kt, :], fm(src)[:, kt, :], ACT.Identity, bias=col(beta, kt), scale=col(g, kt))
                return last

            def biased(n, dst, src, done, ready, bias):
                act.wait_ge(done.sem, done.at(n))
                for kt in range(KT):
                    last = act.activation(dst[:, kt, :], fm(src)[:, kt, :], ACT.Identity, bias=col(bias, kt))
                last.then_inc(ready.sem, 1)

            def round_unit(n, u):
                r, w = extent(u)
                act.wait_ge(phase_done.sem, phase_done.at(n, u + 1))
                if u >= 2:
                    act.wait_ge(feat_ready.sem, feat_ready.at(n, u - 1))
                act.activation(near(u)[0:r, 0:w], fb[1 + u % 2][0:r, 0:w], ACT.Copy, bias=ROUND).then_inc(turns_ready.sem, 1)

            def waves(n, u):
                r, w = extent(u)
                f = feat(u)
                act.wait_ge(near_ready.sem, near_ready.at(n, u + 1))
                if u >= FEATS:
                    act.wait_ge(feat_used.sem, feat_used.at(n, u - FEATS + 1))
                act.activation(f[0:r, 1, 0:w], near(u)[0:r, 0:w], ACT.Sin, scale=-TURN if rounds_on_act(u) else TURN)
                act.wait_ge(dist_ready.sem, dist_ready.at(n, u + 1))
                act.activation(f[0:r, 0, 0:w], dist(u)[0:r, 0:w], ACT.Sin, bias=half_pi[0:r, :], scale=-TURN).then_inc(feat_ready.sem, 1)

            def back(n, p, s):
                if s == "turned":
                    act.wait_ge(xTb_done.sem, xTb_done.at(n, 1))
                    scaled(xT_b, bb[0], G2, B2).then_inc(xTb_ready.sem, 1)
                elif s in UP:
                    for k, bank in ((0, 1), (1, 2)) if s == UP[0] else ((2, 3), (3, 0)):
                        act.wait_ge(up_done.sem, up_done.at(n, k + 1))
                        for m in range(2):
                            last = act.activation(hidT[:, 2 * k + m, :], fm(bb[bank])[:, m, :], ACT.Relu, bias=b1_col[:, 2 * k + m:2 * k + m + 1])
                        last.then_inc(relu_ready.sem, 1)
                elif s == GELU:
                    for c in range(2):
                        act.wait_ge(pre_ready.sem, pre_ready.at(n, 2 * c + 2))
                        act.activation(hid[:, c, :], hid[:, c, :], ACT.Gelu).then_inc(gelu_ready.sem, 1)
                    for c in range(2):
                        act.wait_ge(gelu_ready.sem, gelu_ready.at(n, c + 1))
                        last = act.activation(squares[c], hid[:, c, :], ACT.Square, accum_out=of(sm_b, SQ, c))
                    last.then_inc(sq_ready.sem, 1)
                elif s == TURN4:
                    act.wait_ge(xTb_done.sem, xTb_done.at(n, 2))
                    act.activation(xT_b[:, :, :], fm(bb[2]), ACT.Copy).then_inc(xTb_ready.sem, 1)
                elif s == PROJ:
                    biased(n, qT_b, bb[3], qb_done, qb_ready, CBQ)
                    biased(n, kT_b, bb[0], kb_done, kb_ready, CBK)
                elif s == SOFTMAX:
                    act.wait_ge(nmax_ready.sem, nmax_ready.at(n))
                    for c in range(2):
                        last = act.activation(prob[:, keys[c]], score[:, keys[c]], ACT.Exp, bias=of(sm_b, NMAX, c), accum_out=of(sm_b, SUM, c))
                    last.then_inc(prob_ready.sem, 1)
                elif s == TURN5:
                    act.wait_ge(xTb_done.sem, xTb_done.at(n, 3))
                    act.activation(xT_b[:, :, :], fm(bb[1]), ACT.Copy).then_inc(xTb_ready.sem, 1)
                elif s == LOGITS:
                    act.wait_ge(gap_ready.sem, gap_ready.at(n))
                    act.activation(of(sm_b, E12), of(sm_b, D12), ACT.Exp).then_inc(gap_exp.sem, 1)

            def step(e, f, b):
                for s in range(SLOTS):
                    if b and s == UP[0]:
                        back(*b, "turned")
                    if f:
                        if s + 1 < UNITS and rounds_on_act(s + 1):
                            round_unit(f[0], s + 1)
                        if s < UNITS:
                            waves(f[0], s)
                        for slot, half in KV_TURN.items():
                            if s == slot - 1:
                                act.wait_ge(kvT_done.sem, kvT_done.at(f[0], half + 1))
                                act.activation(kvT[:, 4 * half:4 * half + 4, :], (fb[3], fb[0])[half][:, :].rearrange("p (j m) -> p j m", j=4),
                                               ACT.Copy, scale=1.0 / M).then_inc(kvT_ready.sem, 1)
                        if s == WO - 1:
                            act.wait_ge(att_done.sem, att_done.at(f[0]))
                            act.activation(attT[:, :, :], fm(fb[3]), ACT.Copy).then_inc(att_ready.sem, 1)
                    if b:
                        back(*b, s)
                    if e:
                        if s == TURN1:
                            act.wait_ge(xTf_done.sem, xTf_done.at(e[0]))
                            scaled(xT_f, fb[0], G1, B1).then_inc(xTf_ready.sem, 1)
                        if s == KEYS:
                            biased(e[0], kT_f, fb[0], kf_done, kf_ready, BK)
                        if s == QUERIES:
                            biased(e[0], qT_f, fb[2], qf_done, qf_ready, BQ)

            steps(act, step)

            def bank(q, k):
                return (fb, bb)[q][k]

            def silu_tile(t, q):
                act.wait_ge(gu_done.sem, gu_done.at(t))
                act.activation(tile_silu[q], bank(q, 1)[:, 0:D], ACT.Silu).then_inc(silu_ready.sem, 1)

            def turned_act(t, q):
                act.wait_ge(ta_done.sem, ta_done.at(t))
                act.activation(tile_actT[q], bank(q, 2)[:, 0:D], ACT.Copy).then_inc(ta_ready.sem, 1)

            silu_tile(0, 0)
            with act.Fori(0, TILES - 3, 2) as t:
                for k in range(2):
                    silu_tile(t + k + 1, (k + 1) % 2)
                    turned_act(t + k, k)
            silu_tile(TILES - 1, 1)
            turned_act(TILES - 2, 0)
            turned_act(TILES - 1, 1)

        @block.vector
        def _(dve):
            dve.sem_inc(rows_gone.sem, rows_gone.credit)
            for p in range(2):
                dve.sem_inc(stored[p], 16)
                dve.sem_inc(tile_stored[p], 16)
            dve.memset(v_f[:, :, :, :], 0.0).then_inc(S["dve_start"], 1)

            dve.wait_ge(S["staged_in"], STAGED)
            for t in range(KT):
                for j in range(2):
                    last = dve.tensor_copy(tok_by_part[:, t, j], tok_feat[:, t, j])
            last.then_inc(S["ordered"], 1)
            dve.tensor_reduce(wsum[:, 0:1], f1_in, AX.XY, ALU.add, apply_absolute_value=True)
            dve.tensor_reduce(wsum[:, 1:2], f2_in, AX.XY, ALU.add, apply_absolute_value=True).then_inc(S["wsum_ready"], 1)
            dve.wait_ge(S["wsum_all"], 1)
            dve.tensor_scalar(wscale[:, :], fb[0][:, 0:2], 1.0 / (HID * D), QUANT_EPS, ALU.mult, ALU.max).then_inc(S["scales_ready"], 1)
            dve.wait_ge(S["scales_ready"], 1)
            dve.reciprocal(wrecip[:, :], wscale[:, :]).then_inc(S["scales_ready"], 1)
            dve.wait_ge(S["scales_ready"], 2)
            for n, (src, dst) in enumerate(((f1_in, f1_q), (f2_in, f2_q))):
                dve.tensor_scalar(src, src, wrecip[:, n:n + 1], ROUND, ALU.mult, ALU.add).then_inc(S["dve_start"], 1)
                dve.wait_ge(S["dve_start"], 2 + 2 * n)
                dve.tensor_scalar(src, src, -ROUND, 1.0, ALU.add, ALU.min).then_inc(S["dve_start"], 1)
                dve.wait_ge(S["dve_start"], 3 + 2 * n)
                dve.tensor_scalar(dst, src, -1.0, None, ALU.max).then_inc(S["ternary"], 1)
            group = 0
            for q in range(HALF):
                dve.wait_ge(S["turned"], group + 1)
                dve.tensor_copy(tok_w[:, q, :], bb[group % 4][0:XP, 0:D]).then_inc(S["turned_out"], 1)
                group += 1
            for w in (cq_s, ck_s, cv_s):
                dve.wait_ge(S["turned"], group + 1)
                dve.tensor_copy(w[:, :, :], bb[group % 4][:, :].rearrange("p (k m) -> p k m", k=KT)).then_inc(S["turned_out"], 1)
                group += 1
            for w, KN in ((f1_s, KT), (f2_s, HT)):
                for kt in range(KN):
                    dve.wait_ge(S["turned"], group + 1)
                    n = w.shape[2]
                    dve.tensor_copy(w[:, kt, :], bb[group % 4][:, :].bitcast(BF16)[:, 0:n]).then_inc(S["turned_out"], 1)
                    group += 1
            dve.tensor_scalar(proj_s[:, :, :], proj_s[:, :, :], 1.0 / (float(np.sqrt(DH)) * 2 * float(np.pi)), None,
                              ALU.mult).then_inc(S["scales_ready"], 1)
            dve.wait_ge(S["pool_start"], POOL_START + 1)
            dve.tensor_copy(base[:, :], region0[:, :]).then_inc(base_ready.sem, base_ready.credit)
            dve.wait_ge(S["dve_start"], 5)
            dve.wait_ge(S["turned_out"], group)
            dve.wait_ge(S["weights_in"], WEIGHTS)

            def pass_wait():
                dve.sem_inc(S["waits_passed"], 1)

            def moments(n, k, src, stats, mv, sm, bn, mean, var):
                for c in range(2):
                    last = dve.bn_stats(stats[:, c, :], src[:, c, :])
                last.then_inc(bn.sem, 1)
                aggregate(n, k, stats, mv, sm, bn, mean, var)

            def aggregate(n, k, stats, mv, sm, bn, mean, var):
                dve.wait_ge(bn.sem, bn.at(n, k))
                pass_wait()
                for c in range(2):
                    last = dve.bn_aggr(mv[:, c, :], stats[:, c, :])
                last.then_inc(mean.sem, 1)
                dve.wait_ge(mean.sem, mean.at(n, k))
                dve.tensor_scalar(of(sm, VE), mv[:, :, 1], EPS, None, ALU.add).then_inc(var.sem, 1)

            def moments_e(n, k, src):
                moments(n, k, src, stats_e, mv_e, sm_e, bn_e, mean_e, var_e)

            def moments_f(n, k, src):
                moments(n, k, src, stats_f, mv_f, sm_f, bn_f, mean_f, var_f)

            def moments_b(n, k, src):
                moments(n, k, src, stats_b, mv_b, sm_b, bn_b, mean_b, var_b)

            def normalise(n, k, dst, src, mv, sm, rstd):
                dve.wait_ge(rstd.sem, rstd.at(n, k))
                for c in range(2):
                    last = dve.tensor_scalar(dst[:, c, :], src[:, c, :], mv[:, c, 0:1], of(sm, RSTD, c), ALU.subtract, ALU.mult)
                return last

            def row_max(n, src):
                for c in range(2):
                    if src is hid:
                        dve.wait_ge(gelu_ready.sem, gelu_ready.at(n, c + 1))
                    last = dve.tensor_reduce(of(sm_b, AMAX, c), src[:, c, :], AX.X, ALU.max, apply_absolute_value=True)
                last.then_inc(quant_step.sem, 1)

            def quantise(n, k, src, dst, root_ready, root_k, w):
                def one(ins):
                    nonlocal k
                    k += 1
                    ins.then_inc(quant_step.sem, 1)
                    dve.wait_ge(quant_step.sem, quant_step.at(n, k))

                k += 1
                dve.wait_ge(quant_step.sem, quant_step.at(n, k))
                dve.wait_ge(root_ready.sem, root_ready.at(n, root_k))
                if w == 0:
                    one(dve.tensor_tensor(of(sm_b, RR), of(sm_b, RSTD), of(sm_b, R2), ALU.mult))
                one(dve.tensor_tensor(of(sm_b, AMAX), of(sm_b, AMAX), of(sm_b, RR), ALU.mult))
                one(dve.tensor_scalar(of(sm_b, AMAX), of(sm_b, AMAX), QUANT_EPS, None, ALU.max))
                one(dve.reciprocal(of(sm_b, QS), of(sm_b, AMAX)))
                dve.tensor_scalar(of(sm_b, DQ), of(sm_b, AMAX), 1.0 / 127, wscale[0:C, w:w + 1], ALU.mult, ALU.mult)
                one(dve.scalar_tensor_tensor(of(sm_b, QS), of(sm_b, QS), 127.0, of(sm_b, RR), ALU.mult, ALU.mult))
                for c in range(2):
                    last = dve.tensor_scalar(src[:, c, :], src[:, c, :], of(sm_b, QS, c), ROUND, ALU.mult, ALU.add)
                one(last)
                return dve.tensor_scalar(dst, src, -ROUND, 127.0, ALU.add, ALU.min), k

            def take_phases(n, u):
                r, w = extent(u)
                nr, ph = near(u)[0:r, 0:w], fb[1 + u % 2][0:r, 0:w]
                if rounds_on_act(u):
                    dve.wait_ge(turns_ready.sem, turns_ready.at(n, u // 2 + 1))
                    if u >= 2:
                        dve.wait_ge(feat_ready.sem, feat_ready.at(n, u - 1))
                    dve.scalar_tensor_tensor(nr, nr, -ROUND, ph, ALU.add, ALU.subtract).then_inc(near_ready.sem, 1)
                else:
                    dve.wait_ge(phase_done.sem, phase_done.at(n, u + 1))
                    if u >= 2:
                        dve.wait_ge(feat_ready.sem, feat_ready.at(n, u - 1))
                    dve.tensor_scalar(nr, ph, ROUND, -ROUND, ALU.add, ALU.add).then_inc(whole_ready.sem, 1)
                    dve.wait_ge(whole_ready.sem, whole_ready.at(n, u // 2 + 1))
                    dve.tensor_tensor(nr, ph, nr, ALU.subtract).then_inc(near_ready.sem, 1)
                dve.wait_ge(near_ready.sem, near_ready.at(n, u + 1))
                dve.tensor_scalar(dist(u)[0:r, 0:w].bitcast(U32), nr.bitcast(U32), 0x7FFFFFFF, None, ALU.bitwise_and).then_inc(dist_ready.sem, 1)

            def route(n, p):
                k = 0

                def one(ins):
                    nonlocal k
                    k += 1
                    ins.then_inc(route_step.sem, 1)
                    dve.wait_ge(route_step.sem, route_step.at(n, k))

                dve.wait_ge(logit_done.sem, logit_done.at(n))
                one(dve.tensor_tensor(rt[:, LOGIT], bb[2][0:C, 0:2 * E].rearrange("p (c e) -> p c e", c=2), rb_s[:, :, :], ALU.add))
                pass_wait()
                for c in range(2):
                    last = dve.max(rt[:, TOP, c, :], rt[:, LOGIT, c, :])
                one(last)
                dve.tensor_tensor(of(sm_b, D12), rt[:, TOP, :, 1], rt[:, TOP, :, 0], ALU.subtract).then_inc(gap_ready.sem, 1)
                for c in range(2):
                    last = dve.max_index(rt_i[:, c, :], rt[:, TOP, c, :], rt[:, LOGIT, c, :])
                one(last)
                one(dve.tensor_copy(rt[:, IDX], rt_i[:, :, :]))
                for c in range(2):
                    for j, oh in enumerate((OH1, OH2)):
                        last = dve.tensor_scalar(rt[:, oh, c, :], expert_no[:, :], rt[:, IDX, c, j:j + 1], None, ALU.is_equal)
                one(last)
                dve.tensor_tensor(rt[:, CNT], rt[:, OH1], rt[:, OH2], ALU.add).then_inc(count_ready.sem, 1)
                dve.wait_ge(gap_exp.sem, gap_exp.at(n))
                one(dve.tensor_scalar(of(sm_b, W2), of(sm_b, E12), 1.0, None, ALU.add))
                one(dve.reciprocal(of(sm_b, W1), of(sm_b, W2)))
                one(dve.tensor_tensor(of(sm_b, W2), of(sm_b, E12), of(sm_b, W1), ALU.mult))
                one(dve.tensor_copy(weigh[:, bass.ds(n, 1), :].rearrange("p o (j c) -> p (o j) c", j=2), sm_b[:, W1:W2 + 1, :]))
                return k

            def place_tokens(n, p, k):
                def one(ins):
                    nonlocal k
                    k += 1
                    ins.then_inc(route_step.sem, 1)
                    dve.wait_ge(route_step.sem, route_step.at(n, k))

                dve.wait_ge(prefix_done.sem, prefix_done.at(n))
                dve.wait_ge(base_ready.sem, base_ready.at(n, 0))
                one(dve.tensor_tensor(rt[:, POS], bb[3][0:C, 0:2 * E].rearrange("p (c e) -> p c e", c=2),
                                      base[0:C, :].unsqueeze(1).broadcast_to([C, 2, E]), ALU.add))
                dve.tensor_tensor(base[:, :], bb[2][:, 0:E], base[:, :], ALU.add).then_inc(base_ready.sem, 1)
                for oh, pick in ((OH1, PICK1), (OH2, PICK2)):
                    last = dve.tensor_tensor(rt[:, pick], rt[:, oh], rt[:, POS], ALU.mult)
                one(last)
                for j, pick in enumerate((PICK1, PICK2)):
                    last = dve.tensor_reduce(pos_f[:, 2 * j:2 * j + 2], rt[:, pick], AX.X, ALU.add)
                last.then_inc(picked.sem, 1)
                dve.wait_ge(picked.sem, picked.at(n))
                dve.wait_ge(rows_gone.sem, n * rows_gone.per + 1)
                dve.tensor_copy(pos[p][:, :], pos_f[:, :]).then_inc(pos_ready.sem, 1)
                dve.tensor_copy(place[:, bass.ds(n, 1), :].rearrange("p o k -> p (o k)"), pos_f[:, :]).then_inc(placed.sem, 1)
                assert k == route_step.per

            def back(n, p, s):
                hp = h
                if s == SUM1:
                    dve.wait_ge(hx_ready.sem, hx_ready.at(n))
                    for c in range(2):
                        dve.wait_ge(mlp_done.sem, mlp_done.at(n, c + 1))
                        dve.tensor_tensor(h[:, c, :], tm(bb[1 + c])[:, c, :], h[:, c, :], ALU.add).then_inc(h1_ready.sem, 1)
                        dve.wait_ge(h1_ready.sem, h1_ready.at(n, c + 1))
                        last = dve.bn_stats(stats_b[:, c, :], h[:, c, :])
                    last.then_inc(bn_b.sem, 1)
                    aggregate(n, 1, stats_b, mv_b, sm_b, bn_b, mean_b, var_b)
                    for c in range(2):
                        last = dve.tensor_scalar(zn_b[:, c, :], h[:, c, :], mv_b[:, c, 0:1], None, ALU.subtract)
                    last.then_inc(z3_ready.sem, 1)
                    dve.wait_ge(z3_ready.sem, z3_ready.at(n))
                    row_max(n, zn_b)
                elif s == QIN:
                    last, _ = quantise(n, 0, zn_b[:, :, :], qin[p], rstd_b, 1, 0)
                    last.then_inc(qin_ready.sem, 1)
                elif s == F1:
                    dve.wait_ge(qinT_done.sem, qinT_done.at(n))
                    dve.tensor_copy(qinT, fm16(bb[2], KT)).then_inc(qinT_ready.sem, 1)
                    for k, b in enumerate((3, 0, 1, 2)):
                        c, half = divmod(k, 2)
                        dve.wait_ge(f1_done.sem, f1_done.at(n, k + 1))
                        dve.scalar_tensor_tensor(hid[:, c, half * 512:(half + 1) * 512], bb[b][0:C, :], of(sm_b, DQ, c),
                                                 fb1_s[:, half * 512:(half + 1) * 512], ALU.mult, ALU.add).then_inc(pre_ready.sem, 1)
                elif s == AMAX_HID:
                    row_max(n, hid)
                elif s == QHID:
                    last, k = quantise(n, 7, hid, qhid, rms_ready, 1, 1)
                    last.then_inc(qhid_ready.sem, 1)
                    assert k == quant_step.per
                elif s == QHID_TURN:
                    for k, b in enumerate((3, 0)):
                        dve.wait_ge(qhidT_done.sem, qhidT_done.at(n, k + 1))
                        dve.tensor_copy(qhidT[:, 4 * k:4 * k + 4, :], fm16(bb[b], 4)).then_inc(qhidT_ready.sem, 1)
                elif s == F2:
                    dve.wait_ge(f2_done.sem, f2_done.at(n))
                    dve.wait_ge(hb_ready.sem, hb_ready.at(n))
                    for c in range(2):
                        last = dve.scalar_tensor_tensor(hp[:, c, :], tm(bb[1])[:, c, :], of(sm_b, DQ, c), hp[:, c, :], ALU.mult, ALU.add)
                    last.then_inc(h2_ready.sem, 1)
                    dve.wait_ge(h2_ready.sem, h2_ready.at(n))
                    moments_b(n, 2, hp)
                elif s == LN4:
                    normalise(n, 2, zn_b, hp, mv_b, sm_b, rstd_b).then_inc(z4_ready.sem, 1)
                elif s == PROJ:
                    dve.wait_ge(vb_done.sem, vb_done.at(n))
                    dve.tensor_tensor(v_b[:, :, :], tm(bb[1]), both(cbv_s), ALU.add).then_inc(vb_ready.sem, 1)
                elif s == SCORE:
                    dve.wait_ge(score_done.sem, score_done.at(n))
                    dve.scalar_tensor_tensor(score, bb[2][0:C, 0:3 * C], SCORE_SCALE, mask[:, :], ALU.mult, ALU.add).then_inc(score_ready.sem, 1)
                    dve.wait_ge(score_ready.sem, score_ready.at(n))
                    for c in range(2):
                        last = dve.tensor_reduce(of(sm_b, NMAX, c), score[:, keys[c]], AX.X, ALU.max, negate=True)
                    last.then_inc(nmax_ready.sem, 1)
                elif s == PROB_TURN:
                    dve.wait_ge(prob_ready.sem, prob_ready.at(n))
                    dve.reciprocal(of(sm_b, RSUM), of(sm_b, SUM)).then_inc(rsum_ready.sem, 1)
                    dve.wait_ge(probT_done.sem, probT_done.at(n))
                    dve.tensor_copy(probT, bb[3][0:C, 0:3 * C].rearrange("p (b t) -> p b t", b=3)).then_inc(probT_ready.sem, 1)
                elif s == PV:
                    dve.wait_ge(pv_done.sem, pv_done.at(n))
                    dve.wait_ge(rsum_ready.sem, rsum_ready.at(n))
                    for c in range(2):
                        last = dve.scalar_tensor_tensor(hp[:, c, :], tm(bb[0])[:, c, :], of(sm_b, RSUM, c), hp[:, c, :], ALU.mult, ALU.add)
                    last.then_inc(h3_ready.sem, 1)
                    dve.wait_ge(h3_ready.sem, h3_ready.at(n))
                    moments_b(n, 3, hp)
                elif s == LN5:
                    dve.wait_ge(rows_gone.sem, n * rows_gone.per + 1)
                    normalise(n, 3, xs[p], hp, mv_b, sm_b, rstd_b).then_inc(z5_ready.sem, 1)
                elif s == LOGITS:
                    k = route(n, p)
                elif s == PREFIX:
                    place_tokens(n, p, 9)

            def entry(n, p, s):
                if s == EMB:
                    dve.wait_ge(tok_done.sem, tok_done.at(n))
                    dve.tensor_tensor(emb[p][:, :, :], tm(bb[2]), both(tok_b_s), ALU.add).then_inc(emb_ready.sem, 1)
                    dve.wait_ge(emb_ready.sem, emb_ready.at(n))
                    moments_e(n, 1, emb[p])
                elif s == LN0:
                    normalise(n, 1, a[p], emb[p], mv_e, sm_e, rstd_e).then_inc(a_ready.sem, 1)
                    dve.wait_ge(a_ready.sem, a_ready.at(n))
                    for c in range(2):
                        last = dve.tensor_scalar(zn_f[:, c, :], a[p][:, c, :], of(sm_e, R2, c), None, ALU.mult)
                    last.then_inc(znf_ready.sem, 1)
                elif s == VALUES:
                    dve.wait_ge(vf_done.sem, vf_done.at(n))
                    for s in range(2):
                        last = dve.tensor_tensor(
                            v_f[:, :, s::2, s * DH:(s + 1) * DH],
                            tm(fb[0]).rearrange("p c (j s d) -> p c j s d", s=2, d=DH)[:, :, :, s, :],
                            bv_s[:, :].rearrange("p (o j s d) -> p o j s d", o=1, s=2, d=DH)[:, :, :, s, :].broadcast_to([C, 2, PAIRS, DH]), ALU.add)
                    last.then_inc(vf_ready.sem, 1)

            def step(e, f, b):
                for s in range(SLOTS):
                    if f:
                        if s < UNITS:
                            take_phases(f[0], s)
                        if s in KV_TURN:
                            half = KV_TURN[s]
                            dve.wait_ge(kv_done.sem, kv_done.at(f[0], half + 1))
                            dve.tensor_copy(kv[:, 4 * half:4 * half + 4, :], (fb[3], fb[0])[half][:, :].rearrange("p (j m) -> p j m", j=4)).then_inc(kv_ready.sem, 1)
                        if s == LN2:
                            n, p = f
                            dve.wait_ge(wo_done.sem, wo_done.at(n))
                            dve.wait_ge(ab_ready.sem, ab_ready.at(n))
                            dve.tensor_tensor(a[p][:, :, :], tm(fb[3]), a[p][:, :, :], ALU.add).then_inc(x1_ready.sem, 1)
                            dve.wait_ge(x1_ready.sem, x1_ready.at(n))
                            moments_f(n, 1, a[p])
                        if s == LN2 + 1:
                            normalise(f[0], 1, zn_b, a[f[1]], mv_f, sm_f, rstd_f).then_inc(zn2_ready.sem, 1)
                    if b:
                        back(*b, s)
                    if e:
                        entry(*e, s)

            steps(dve, step)

            dve.wait_ge(base_ready.sem, base_ready.at(IMAGES - 1))
            dve.tensor_scalar(pad_row[:, :], base[:, :], part_no[:, 0:1], None, ALU.add).then_inc(S["table_step"], 1)
            dve.wait_ge(S["table_step"], 1)
            dve.tensor_copy(pad_idx[:, :], pad_row[:, :]).then_inc(S["pad_ready"], 1)
            k = 1

            def one(ins):
                nonlocal_k[0] += 1
                ins.then_inc(S["table_step"], 1)
                dve.wait_ge(S["table_step"], nonlocal_k[0])

            nonlocal_k = [1]
            one(dve.tensor_tensor(few[:, FULL, :], base[:, :], region0[:, :], ALU.subtract))
            one(dve.tensor_scalar(few[:, FULL, :], few[:, FULL, :], 1.0 / P, 127.0 / P - 0.5 + 0.5 / P, ALU.mult, ALU.add))
            one(dve.tensor_scalar(few[:, WHOLE, :], few[:, FULL, :], ROUND, -ROUND, ALU.add, ALU.add))
            one(dve.tensor_copy(few[:, END, :], few[:, WHOLE, :]))
            for e in range(1, E):
                one(dve.tensor_tensor(few[:, END, e:e + 1], few[:, END, e:e + 1], few[:, END, e - 1:e], ALU.add))
            one(dve.tensor_scalar(few[:, JUMP, :], few[:, WHOLE, :], -float(P), float(REGION), ALU.mult, ALU.add))
            one(dve.memset(TAB[:, 1, :], 0.0))
            one(dve.tensor_scalar(TAB[:, 2, :], TAB[:, 0, :], float(P), None, ALU.mult))
            for e in range(E):
                one(dve.tensor_scalar(TAB[:, 3, :], TAB[:, 0, :], few[0:1, END, e:e + 1], None, ALU.is_ge))
                one(dve.tensor_tensor(TAB[:, 1, :], TAB[:, 1, :], TAB[:, 3, :], ALU.add))
                one(dve.scalar_tensor_tensor(TAB[:, 2, :], TAB[:, 3, :], few[0:1, JUMP, e:e + 1], TAB[:, 2, :], ALU.mult, ALU.add))
            dve.tensor_scalar(tab_i[:, 0, :], TAB[:, 1, :], float(E - 1), None, ALU.min)
            dve.tensor_copy(tab_i[:, 1, :], TAB[:, 2, :]).then_inc(S["table_ready"], 1)

            def bank(q, k):
                return (fb, bb)[q][k]

            def turned_rows(t, q):
                dve.wait_ge(tx_done.sem, tx_done.at(t))
                dve.tensor_copy(tile_xT[q], bank(q, 0)[:, 0:D]).then_inc(tx_ready.sem, 1)

            def gated(t, q):
                dve.wait_ge(silu_ready.sem, silu_ready.at(t))
                dve.tensor_tensor(tile_act[q], tile_silu[q], bank(q, 1)[:, D:2 * D], ALU.mult).then_inc(act_ready.sem, 1)

            def result(t, q):
                dve.wait_ge(dn_done.sem, dn_done.at(t))
                dve.wait_ge(tile_stored[q], t * 8 + 16 - 8 * q)
                dve.tensor_copy(tile_y[q], bank(q, 3)[:, 0:D]).then_inc(y_ready.sem, 1)

            turned_rows(0, 0)
            for t in range(2):
                gated(t, t)
                turned_rows(t + 1, (t + 1) % 2)
            with dve.Fori(0, TILES - 5, 2) as t:
                for k in range(2):
                    gated(t + k + 2, k)
                    turned_rows(t + k + 3, (k + 1) % 2)
                    result(t + k, k)
            for t in range(TILES - 4, TILES):
                if t + 2 < TILES:
                    gated(t + 2, t % 2)
                if t + 3 < TILES:
                    turned_rows(t + 3, (t + 1) % 2)
                result(t, t % 2)

            for q in range(2):
                dve.wait_ge(tile_stored[q], 16 * (TILES // 2) + 16)
            dve.wait_ge(S["found_ready"], 1)

            def set_rows(j, n):
                dve.tensor_copy(idx_o[n][:, :], found_i[:, bass.ds(j, 1), :].rearrange("p o k -> p (o k)")).then_inc(idx_set.sem, 1)

            def add_up(j, n, r):
                dve.wait_ge(rows_here[n], r * 64 + 64)
                dve.wait_ge(resid_here[n], r * 16 + 16)
                w = weigh[:, bass.ds(j, 1), :].rearrange("p o k -> p (o k)")
                for c in range(2):
                    s = slice(c * D, (c + 1) * D)
                    last = dve.scalar_tensor_tensor(out_h[n][:, s], out_y1[n][:, s], w[:, c:c + 1], out_h[n][:, s], ALU.mult, ALU.add)
                last.then_inc(sum_step.sem, 1)
                dve.wait_ge(sum_step.sem, sum_step.at(j))
                for c in range(2):
                    s = slice(c * D, (c + 1) * D)
                    last = dve.scalar_tensor_tensor(out_h[n][:, s], out_y2[n][:, s], w[:, 2 + c:3 + c], out_h[n][:, s], ALU.mult, ALU.add)
                last.then_inc(sum_ready.sem, 1)

            for n in range(OUT_SLOTS):
                set_rows(n, n)
            with dve.Fori(0, IMAGES // OUT_SLOTS - 1) as r:
                for n in range(OUT_SLOTS):
                    add_up(r * OUT_SLOTS + n, n, r)
                    dve.wait_ge(sum_ready.sem, sum_ready.at(r * OUT_SLOTS + n))
                    set_rows((r + 1) * OUT_SLOTS + n, n)
            for n in range(OUT_SLOTS):
                add_up(IMAGES - OUT_SLOTS + n, n, IMAGES // OUT_SLOTS - 1)


_INS = ['x', 'L0_tok_W', 'L0_tok_b', 'L0_attn_proj_mat', 'L0_attn_wq', 'L0_attn_bq', 'L0_attn_wk', 'L0_attn_bk',
        'L0_attn_wv', 'L0_attn_bv', 'L0_attn_wo', 'L0_attn_bo', 'L0_attn_ln1_g', 'L0_attn_ln1_b', 'L0_attn_w1',
        'L0_attn_b1', 'L0_attn_w2', 'L0_attn_b2', 'L0_attn_ln2_g', 'L0_attn_ln2_b', 'L0_ffn_w1', 'L0_ffn_b1',
        'L0_ffn_w2', 'L0_ffn_b2', 'L1_attn_Wq', 'L1_attn_bq', 'L1_attn_Wk', 'L1_attn_bk', 'L1_attn_Wv', 'L1_attn_bv',
        'L1_ffn_router_w', 'L1_ffn_router_b', 'L1_ffn_we_gate', 'L1_ffn_we_up', 'L1_ffn_we_down']
_OUTS = [((64, 196, 256), 'float32')]


def kernel(**inputs):
    import numpy as _np
    import concourse.bacc as _bacc
    from concourse import mybir as _mybir
    from concourse.bass_utils import run_bass_kernel_spmd as _run

    nc = _bacc.Bacc("TRN2", target_bir_lowering=False, num_devices=1)
    arrays, args = {}, []
    for name in _INS:
        a = _np.ascontiguousarray(inputs[name])
        arrays[f"in_{name}_dram"] = a
        args.append(nc.dram_tensor(f"in_{name}_dram", a.shape, _mybir.dt.from_np(a.dtype), kind="ExternalInput").ap())
    for i, (shape, dtype) in enumerate(_OUTS):
        dt = _mybir.dt.from_np(_np.dtype(dtype))
        args.append(nc.dram_tensor(f"out_{i}_dram", shape, dt, kind="ExternalOutput").ap())
    vit_tower(nc, *args)
    r = _run(nc, [arrays], core_ids=[0])
    return r.results[0]["out_0_dram"]
```
